# Optimizing a Trainium2 kernel written in Bass

```python
import numpy as np
import jax
import jax.numpy as jnp

def _softmax(x, axis=-1):
    return jax.nn.softmax(x, axis=axis)

def _gelu(x):
    return jax.nn.gelu(x, approximate=True)

def _silu(x):
    return jax.nn.silu(x)

def _sigmoid(x):
    return jax.nn.sigmoid(x)

def _layernorm(x, axis=-1, eps=1e-05):
    m = jnp.mean(x, axis=axis, keepdims=True)
    v = jnp.var(x, axis=axis, keepdims=True)
    return (x - m) / jnp.sqrt(v + eps)

def _scatter_add(tgt, idx, src, axis=0):
    return tgt.at[idx].add(src)

def _segment_sum(src, seg, n):
    return jax.ops.segment_sum(src, seg, n)
kernel_name = 'mk_adaln_ffn_d1_seqx_r4_66b874'

def setup_inputs(seed: int=0):
    np.random.seed(seed)
    _w = jnp.asarray

    def _rec_inputs():
        import jax
        import jax.numpy as jnp
        _rk = jax.random.key(seed)
        x = -0.0003929 + 0.9999 * jax.random.normal(jax.random.fold_in(_rk, 1), (4, 512, 512), jnp.float32)
        _lenS = 512 - jax.random.randint(jax.random.fold_in(_rk, 7), (4,), 0, max(1, 512 // 4) + 1, jnp.int32)
        _lenS2 = 512 - jax.random.randint(jax.random.fold_in(_rk, 8), (4,), 0, max(1, 512 // 4) + 1, jnp.int32)
        cond_2048 = 0.00782532 + 1.00527 * jax.random.normal(jax.random.fold_in(_rk, 11), (4, 512), jnp.float32)
        return (x, cond_2048)
    x, cond_2048 = _rec_inputs()

    def _L0_cond_setup():
        import jax, jax.numpy as jnp
        import numpy as np
        HEADS = 16
        EPS = 1e-06

        def _rms_norm(x, g):
            xf = x.astype(jnp.float32)
            y = xf * jax.lax.rsqrt(jnp.mean(xf * xf, axis=-1, keepdims=True) + EPS)
            return y.astype(x.dtype) * g
        key = jax.random.key(seed)
        ks = jax.random.split(key, 6)
        b, n, dim, emb_dim = (4, 512, 512, 512)
        d_head = dim // HEADS
        return {'x': jax.random.normal(ks[0], (b, n, dim), jnp.float32), 'emb': jax.random.normal(ks[1], (b, 1, emb_dim), jnp.float32), 'W_emb': jax.random.normal(ks[2], (emb_dim, 2 * dim), jnp.float32) * emb_dim ** (-0.5), 'b_emb': jnp.zeros((2 * dim,), jnp.float32), 'g_norm': jnp.ones((dim,), jnp.float32), 'W_qkv': jax.random.normal(ks[3], (dim, 3 * dim), jnp.float32) * dim ** (-0.5), 'g_q': jnp.ones((d_head,), jnp.float32), 'g_k': jnp.ones((d_head,), jnp.float32), 'W_out': jax.random.normal(ks[4], (dim, dim), jnp.float32) * dim ** (-0.5)}
    _L0_cond_all = _L0_cond_setup()
    _L0_cond_in = {k: v for k, v in _L0_cond_all.items() if k in ('W_emb', 'b_emb', 'g_norm', 'W_qkv', 'g_q', 'g_k', 'W_out')}
    del _L0_cond_all

    def _L0_ffn_setup():
        import jax, jax.numpy as jnp
        import numpy as np
        B, S, H = (4, 256, 512)
        NH = 16
        HD = H // NH
        RD = HD // 2
        LAT = H // 4
        I = 256
        NE = 8
        NSH = 1
        NR = NE - NSH
        TOPK = 2
        EPS = 1e-05
        SCALING = 8.0

        def _w(key, shape, fan_in):
            return jax.random.normal(key, shape, dtype=jnp.float32) / np.sqrt(fan_in)

        def rmsnorm(x, w):
            rms = jax.lax.rsqrt(jnp.mean(x * x, axis=-1, keepdims=True) + EPS)
            return w * rms * x

        def rope_cos_sin(seq_len):
            inv_freq = 1.0 / 10000.0 ** (jnp.arange(0, RD, 2, dtype=jnp.float32) / RD)
            t = jnp.arange(seq_len, dtype=jnp.float32)
            ang = jnp.outer(t, inv_freq)
            emb = jnp.concatenate([ang, ang], axis=-1)
            return (jnp.cos(emb), jnp.sin(emb))

        def apply_rope(x, cos, sin):
            c = cos[None, :, None, :]
            s = sin[None, :, None, :]
            x1, x2 = jnp.split(x, 2, axis=-1)
            rot = jnp.concatenate([-x2, x1], axis=-1)
            return x * c + rot * s

        def expert_ffn(x, wg, wu, wd):
            h = jax.nn.silu(x @ wg) * (x @ wu) / SCALING
            return h @ wd

        def attention(x, kv_d_w, q_d_w, k_u_w, v_u_w, q_u_w, rope_k_w, rope_q_w, o_w):
            b, s, _ = x.shape
            kv_d = x @ kv_d_w
            q_d = x @ q_d_w
            k_p = (kv_d @ k_u_w).reshape(b, s, NH, RD)
            q_p = (q_d @ q_u_w).reshape(b, s, NH, RD)
            v = (kv_d @ v_u_w).reshape(b, s, NH, HD)
            k_r = (x @ rope_k_w).reshape(b, s, NH, RD)
            q_r = (q_d @ rope_q_w).reshape(b, s, NH, RD)
            cos, sin = rope_cos_sin(s)
            k_r = apply_rope(k_r, cos, sin)
            q_r = apply_rope(q_r, cos, sin)
            k = jnp.concatenate([k_p, k_r], axis=-1)
            q = jnp.concatenate([q_p, q_r], axis=-1)
            scale = 1.0 / np.sqrt(HD)
            scores = jnp.einsum('bqhd,bkhd->bhqk', q, k) * scale
            causal = jnp.tril(jnp.ones((s, s), dtype=bool))
            scores = jnp.where(causal[None, None], scores, jnp.finfo(scores.dtype).min)
            probs = jax.nn.softmax(scores, axis=-1)
            out = jnp.einsum('bhqk,bkhd->bqhd', probs, v).reshape(b, s, H)
            return out @ o_w

        def moe(x, sh_gate, sh_up, sh_down, r_gate, r_up, r_down, router_w, router_b):
            shared = expert_ffn(x, sh_gate, sh_up, sh_down)
            logits = x @ router_w + router_b
            probs = jax.nn.sigmoid(logits)
            scores, idx = jax.lax.top_k(probs, TOPK)
            scores = scores / jnp.sum(scores, axis=-1, keepdims=True)
            w = jnp.sum(jax.nn.one_hot(idx, NR, dtype=x.dtype) * scores[..., None], axis=-2)
            combined = jnp.zeros_like(x)
            for e in range(NR):
                combined = combined + w[..., e:e + 1] * expert_ffn(x, r_gate[e], r_up[e], r_down[e])
            return shared + combined
        key = jax.random.key(seed)
        ks = jax.random.split(key, 24)
        return {'x': jax.random.normal(ks[0], (B, S, H), dtype=jnp.float32), 'ln1_w': jnp.ones((H,), jnp.float32), 'ln2_w': jnp.ones((H,), jnp.float32), 'kv_d_w': _w(ks[1], (H, LAT), H), 'q_d_w': _w(ks[2], (H, LAT), H), 'k_u_w': _w(ks[3], (LAT, H // 2), LAT), 'v_u_w': _w(ks[4], (LAT, H), LAT), 'q_u_w': _w(ks[5], (LAT, H // 2), LAT), 'rope_k_w': _w(ks[6], (H, H // 2), H), 'rope_q_w': _w(ks[7], (LAT, H // 2), LAT), 'o_w': _w(ks[8], (H, H), H), 'sh_gate': _w(ks[9], (H, I), H), 'sh_up': _w(ks[10], (H, I), H), 'sh_down': _w(ks[11], (I, H), I), 'r_gate': _w(ks[12], (NR, H, I), H), 'r_up': _w(ks[13], (NR, H, I), H), 'r_down': _w(ks[14], (NR, I, H), I), 'router_w': _w(ks[15], (H, NR), H), 'router_b': jnp.zeros((NR,), jnp.float32)}
    _L0_ffn_all = _L0_ffn_setup()
    _L0_ffn_in = {k: v for k, v in _L0_ffn_all.items() if k in ('ln1_w', 'ln2_w', 'kv_d_w', 'q_d_w', 'k_u_w', 'v_u_w', 'q_u_w', 'rope_k_w', 'rope_q_w', 'o_w', 'sh_gate', 'sh_up', 'sh_down', 'r_gate', 'r_up', 'r_down', 'router_w', 'router_b')}
    del _L0_ffn_all
    return {'x': x, 'cond_2048': cond_2048, 'L0_cond_W_emb': _L0_cond_in['W_emb'], 'L0_cond_b_emb': _L0_cond_in['b_emb'], 'L0_cond_g_norm': _L0_cond_in['g_norm'], 'L0_cond_W_qkv': _L0_cond_in['W_qkv'], 'L0_cond_g_q': _L0_cond_in['g_q'], 'L0_cond_g_k': _L0_cond_in['g_k'], 'L0_cond_W_out': _L0_cond_in['W_out'], 'L0_ffn_ln1_w': _L0_ffn_in['ln1_w'], 'L0_ffn_ln2_w': _L0_ffn_in['ln2_w'], 'L0_ffn_kv_d_w': _L0_ffn_in['kv_d_w'], 'L0_ffn_q_d_w': _L0_ffn_in['q_d_w'], 'L0_ffn_k_u_w': _L0_ffn_in['k_u_w'], 'L0_ffn_v_u_w': _L0_ffn_in['v_u_w'], 'L0_ffn_q_u_w': _L0_ffn_in['q_u_w'], 'L0_ffn_rope_k_w': _L0_ffn_in['rope_k_w'], 'L0_ffn_rope_q_w': _L0_ffn_in['rope_q_w'], 'L0_ffn_o_w': _L0_ffn_in['o_w'], 'L0_ffn_sh_gate': _L0_ffn_in['sh_gate'], 'L0_ffn_sh_up': _L0_ffn_in['sh_up'], 'L0_ffn_sh_down': _L0_ffn_in['sh_down'], 'L0_ffn_r_gate': _L0_ffn_in['r_gate'], 'L0_ffn_r_up': _L0_ffn_in['r_up'], 'L0_ffn_r_down': _L0_ffn_in['r_down'], 'L0_ffn_router_w': _L0_ffn_in['router_w'], 'L0_ffn_router_b': _L0_ffn_in['router_b']}

def reference(x, cond_2048, L0_cond_W_emb, L0_cond_b_emb, L0_cond_g_norm, L0_cond_W_qkv, L0_cond_g_q, L0_cond_g_k, L0_cond_W_out, L0_ffn_ln1_w, L0_ffn_ln2_w, L0_ffn_kv_d_w, L0_ffn_q_d_w, L0_ffn_k_u_w, L0_ffn_v_u_w, L0_ffn_q_u_w, L0_ffn_rope_k_w, L0_ffn_rope_q_w, L0_ffn_o_w, L0_ffn_sh_gate, L0_ffn_sh_up, L0_ffn_sh_down, L0_ffn_r_gate, L0_ffn_r_up, L0_ffn_r_down, L0_ffn_router_w, L0_ffn_router_b):
    import jax
    import jax.numpy as jnp

    def _L0_cond_ref(x, emb, W_emb, b_emb, g_norm, W_qkv, g_q, g_k, W_out):
        import jax, jax.numpy as jnp
        import numpy as np
        HEADS = 16
        EPS = 1e-06

        def _rms_norm(x, g):
            xf = x.astype(jnp.float32)
            y = xf * jax.lax.rsqrt(jnp.mean(xf * xf, axis=-1, keepdims=True) + EPS)
            return y.astype(x.dtype) * g
        b, n, dim = x.shape
        h = HEADS
        d = dim // h
        scale_shift = emb @ W_emb + b_emb
        scale, shift = jnp.split(scale_shift, 2, axis=-1)
        xn = _rms_norm(x, g_norm) * (1.0 + scale) + shift
        qkv = xn @ W_qkv
        qkv = qkv.reshape(b, n, 3, h, d)
        q, k, v = jnp.moveaxis(qkv, 2, 0)
        q = jnp.swapaxes(q, 1, 2)
        k = jnp.swapaxes(k, 1, 2)
        v = jnp.swapaxes(v, 1, 2)
        q = _rms_norm(q, g_q)
        k = _rms_norm(k, g_k)
        logits = jnp.einsum('bhqd,bhkd->bhqk', q, k) * d ** (-0.5)
        attn = jax.nn.softmax(logits, axis=-1)
        o = jnp.einsum('bhqk,bhkd->bhqd', attn, v)
        o = jnp.swapaxes(o, 1, 2).reshape(b, n, dim)
        return o + o @ W_out

    def _L0_ffn_ref(x, ln1_w, ln2_w, kv_d_w, q_d_w, k_u_w, v_u_w, q_u_w, rope_k_w, rope_q_w, o_w, sh_gate, sh_up, sh_down, r_gate, r_up, r_down, router_w, router_b):
        import jax, jax.numpy as jnp
        import numpy as np
        B, S, H = (4, 256, 512)
        NH = 16
        HD = H // NH
        RD = HD // 2
        LAT = H // 4
        I = 256
        NE = 8
        NSH = 1
        NR = NE - NSH
        TOPK = 2
        EPS = 1e-05
        SCALING = 8.0

        def _w(key, shape, fan_in):
            return jax.random.normal(key, shape, dtype=jnp.float32) / np.sqrt(fan_in)

        def rmsnorm(x, w):
            rms = jax.lax.rsqrt(jnp.mean(x * x, axis=-1, keepdims=True) + EPS)
            return w * rms * x

        def rope_cos_sin(seq_len):
            inv_freq = 1.0 / 10000.0 ** (jnp.arange(0, RD, 2, dtype=jnp.float32) / RD)
            t = jnp.arange(seq_len, dtype=jnp.float32)
            ang = jnp.outer(t, inv_freq)
            emb = jnp.concatenate([ang, ang], axis=-1)
            return (jnp.cos(emb), jnp.sin(emb))

        def apply_rope(x, cos, sin):
            c = cos[None, :, None, :]
            s = sin[None, :, None, :]
            x1, x2 = jnp.split(x, 2, axis=-1)
            rot = jnp.concatenate([-x2, x1], axis=-1)
            return x * c + rot * s

        def expert_ffn(x, wg, wu, wd):
            h = jax.nn.silu(x @ wg) * (x @ wu) / SCALING
            return h @ wd

        def attention(x, kv_d_w, q_d_w, k_u_w, v_u_w, q_u_w, rope_k_w, rope_q_w, o_w):
            b, s, _ = x.shape
            kv_d = x @ kv_d_w
            q_d = x @ q_d_w
            k_p = (kv_d @ k_u_w).reshape(b, s, NH, RD)
            q_p = (q_d @ q_u_w).reshape(b, s, NH, RD)
            v = (kv_d @ v_u_w).reshape(b, s, NH, HD)
            k_r = (x @ rope_k_w).reshape(b, s, NH, RD)
            q_r = (q_d @ rope_q_w).reshape(b, s, NH, RD)
            cos, sin = rope_cos_sin(s)
            k_r = apply_rope(k_r, cos, sin)
            q_r = apply_rope(q_r, cos, sin)
            k = jnp.concatenate([k_p, k_r], axis=-1)
            q = jnp.concatenate([q_p, q_r], axis=-1)
            scale = 1.0 / np.sqrt(HD)
            scores = jnp.einsum('bqhd,bkhd->bhqk', q, k) * scale
            causal = jnp.tril(jnp.ones((s, s), dtype=bool))
            scores = jnp.where(causal[None, None], scores, jnp.finfo(scores.dtype).min)
            probs = jax.nn.softmax(scores, axis=-1)
            out = jnp.einsum('bhqk,bkhd->bqhd', probs, v).reshape(b, s, H)
            return out @ o_w

        def moe(x, sh_gate, sh_up, sh_down, r_gate, r_up, r_down, router_w, router_b):
            shared = expert_ffn(x, sh_gate, sh_up, sh_down)
            logits = x @ router_w + router_b
            probs = jax.nn.sigmoid(logits)
            scores, idx = jax.lax.top_k(probs, TOPK)
            scores = scores / jnp.sum(scores, axis=-1, keepdims=True)
            w = jnp.sum(jax.nn.one_hot(idx, NR, dtype=x.dtype) * scores[..., None], axis=-2)
            combined = jnp.zeros_like(x)
            for e in range(NR):
                combined = combined + w[..., e:e + 1] * expert_ffn(x, r_gate[e], r_up[e], r_down[e])
            return shared + combined
        h = x + attention(rmsnorm(x, ln1_w), kv_d_w, q_d_w, k_u_w, v_u_w, q_u_w, rope_k_w, rope_q_w, o_w)
        out = h + moe(rmsnorm(h, ln2_w), sh_gate, sh_up, sh_down, r_gate, r_up, r_down, router_w, router_b)
        return out
    x = x + _L0_ffn_ref(_L0_cond_ref(x, cond_2048[:, None, :], L0_cond_W_emb, L0_cond_b_emb, L0_cond_g_norm, L0_cond_W_qkv, L0_cond_g_q, L0_cond_g_k, L0_cond_W_out), L0_ffn_ln1_w, L0_ffn_ln2_w, L0_ffn_kv_d_w, L0_ffn_q_d_w, L0_ffn_k_u_w, L0_ffn_v_u_w, L0_ffn_q_u_w, L0_ffn_rope_k_w, L0_ffn_rope_q_w, L0_ffn_o_w, L0_ffn_sh_gate, L0_ffn_sh_up, L0_ffn_sh_down, L0_ffn_r_gate, L0_ffn_r_up, L0_ffn_r_down, L0_ffn_router_w, L0_ffn_router_b)
    return x

_drawn_inputs = setup_inputs


def setup_inputs(seed=0):
    import zlib

    import numpy as np

    out = dict(_drawn_inputs(seed))
    spreads = {'L0_cond_b_emb': (0.0, 0.1),
     'L0_cond_g_norm': (1.0, 0.2),
     'L0_cond_g_q': (1.0, 0.6),
     'L0_cond_g_k': (1.0, 0.6),
     'L0_ffn_ln1_w': (1.0, 0.2),
     'L0_ffn_ln2_w': (1.0, 0.6),
     'L0_ffn_router_b': (0.0, 2.0)}
    factors = {'L0_ffn_q_d_w': 8.0,
     'L0_ffn_k_u_w': 8.0,
     'L0_ffn_q_u_w': 8.0,
     'L0_ffn_rope_k_w': 8.0,
     'L0_ffn_rope_q_w': 8.0}
    for name, (base, spread) in spreads.items():
        noise = np.random.default_rng([zlib.crc32(name.encode()), seed]).standard_normal(out[name].shape)
        drawn = base * np.exp(spread * noise) if base else spread * noise
        out[name] = jnp.asarray(drawn.astype(out[name].dtype))
    for name, factor in factors.items():
        out[name] = (out[name] * factor).astype(out[name].dtype)
    return out
```

```python
from contextlib import ExitStack

import numpy as np

import concourse.bass as bass
from concourse import mybir

F32 = mybir.dt.float32
F32R = mybir.dt.float32r
I32 = mybir.dt.int32
ALU = mybir.AluOpType
ACT = mybir.ActivationFunctionType
AX = mybir.AxisListType

P = 128
B, S, D = 4, 512, 512
NT, NC = S // P, D // P
H, DH = 16, 32
RD = DH // 2
LAT = 128
INNER = 256
NE, NR = 8, 7
NI = INNER // P
HPG, NG = P // DH, H * DH // P
SCALE = float(DH) ** -0.5
SCALING = 8.0
EPS_COND, EPS_FFN = 1e-6, 1e-5
NEG = -1e30
MAGIC = 0x5F3759DF
RSQRT_STEPS = 12
XSTACK = 3 * DH
NSTK = 8

_HEADS = [k for h in range(H) for k in
          ([("max", h + 1)] if h + 1 < H else []) +
          ([("turn", h // 4 + 2, "k"), ("turn", h // 4 + 2, "q")] if h % 4 == 2 and h // 4 + 2 < NG else [])]
_FIRST = [("turn", g, c) for g in range(2) for c in "kq"] + [("max", 0)]
_TURN_O = [("turn_o", c) for c in range(NC)]
ITEMS = {
    1: [("x", c) for c in range(NC)] + [("qk", t, c) for t in range(NT) for c in "qk"]
    + [("v", t) for t in range(NT)] + _FIRST + _HEADS + _TURN_O + [("out", t) for t in range(NT)],
    2: [("x", c) for c in range(NC)] + ["kv_d", "q_d"] + [("qk", t, c) for t in range(NT) for c in "qk"]
    + [("v", t) for t in range(NT)] + _FIRST + _HEADS + _TURN_O + [("out", t) for t in range(NT)]
    + [("x2", c) for c in range(NC)] + [("router", n) for n in range(2)],
}
assert all(len(x) % 2 == 0 for x in ITEMS.values())


class Ring:

    def __init__(self, name, sem, banks, per_loop):
        self.banks, self.n = banks, len(banks)
        self.per = per_loop // self.n
        self.full = [sem(f"{name}_full{i}") for i in range(self.n)]
        self.free = [sem(f"{name}_free{i}") for i in range(self.n)]

    def bank(self, m):
        return self.banks[m % self.n]

    def wait_free(self, eng, i, m):
        eng.wait_ge(self.free[m % self.n], i * self.per + (m // self.n + 1))

    def wait_full(self, eng, i, m):
        eng.wait_ge(self.full[m % self.n], i * self.per + (m // self.n + 1))

    def wait_read(self, eng, i, m):
        eng.wait_ge(self.free[m % self.n], i * self.per + (m // self.n + 2))

    def filled(self, ins, m):
        ins.then_inc(self.full[m % self.n], 1)

    def cleared(self, ins, m):
        ins.then_inc(self.free[m % self.n], 1)


def build(nc, x_d, cond_d, wemb_d, bemb_d, gnorm_d, wqkv_d, gq_d, gk_d, wout_d, ln1_d, ln2_d, kvd_d,
          qd_d, ku_d, vu_d, qu_d, rk_d, rq_d, ow_d, gate_d, up_d, down_d, rw_d, rb_d, cos_d, sin_d,
          out_d):
    dram = lambda name, shape: nc.dram_tensor(name, shape, F32, kind="Internal").ap()
    x1_s = dram("x1_s", (B, P, NT, D))
    acc_s = dram("acc_s", (B, P, NT, D))
    xt_s = dram("xt_s", (2, P, NC, B, S))
    split_s = dram("split_s", (2, P, 4, S))

    with ExitStack() as ctx:
        sem = lambda name: ctx.enter_context(nc.semaphore(name))
        keep = lambda name, shape, dt=F32: ctx.enter_context(nc.sbuf_tensor(name, shape, dt))
        psum = ctx.enter_context(nc.psum_tensor("psum", [P, 8, 512], F32))

        ident = keep("ident", [P, P])
        identr = keep("identr", [P, P], F32R)
        vrow = keep("vrow", [P, P])
        vcol = keep("vcol", [P, 38])
        logits = keep("logits", [P, B * NT, NE])

        room = ExitStack()
        sb = lambda name, shape, dt=F32: room.enter_context(nc.sbuf_tensor(name, shape, dt))
        wh = sb("wh", [P, 8192], F32R)
        wl = sb("wl", [P, 8192], F32R)
        xh = sb("xh", [P, NC, S], F32R)
        xl = sb("xl", [P, NC, S], F32R)
        split = sb("split", [P, 2, 4, S], F32R)
        stack = sb("stack", [P, NSTK, 2, S], F32R)
        vs = sb("vs", [P, 2, S])
        qk = sb("qk", [P, NT, 2 * D])
        sq = sb("sq", [P, 2, S])
        vaug = sb("vaug", [P, NT, H, DH + 1])
        probs = sb("probs", [P, 2, NT, S])
        xt = sb("xt", [P, NT, D])
        ot = sb("ot", [P, NT, D])
        yt = sb("yt", [P, NT, D])
        maskq = sb("maskq", [P, P], F32R)
        maskk = sb("maskk", [P, P], F32R)
        rope = sb("rope", [P, 2, NT, RD])
        modall = sb("modall", [P, B, 2 * NC])
        mod = sb("mod", [P, 2 * NC])
        gqk = sb("gqk", [P, 1])
        sst = sb("sst", [P, NT])
        rst = sb("rst", [P, 2, NT])
        ssh = sb("ssh", [P, NT, 2 * H])
        rsh = sb("rsh", [P, 2, NT * 2 * H])
        nmax = sb("nmax", [P, 4, NT])
        rden = sb("rden", [P, 2, NT])
        rwt = sb("rwt", [P, NC, NE])
        rwh = sb("rwh", [P, NC, NE], F32R)
        rwl = sb("rwl", [P, NC, NE], F32R)
        rb = sb("rb", [P, NE])
        lg = sb("lg", [P, NT, NE])
        room.close()

        room3 = ctx.enter_context(ExitStack())
        sb = lambda name, shape, dt=F32: room3.enter_context(nc.sbuf_tensor(name, shape, dt))
        acc = sb("acc", [P, B * NT, D])
        x3 = sb("x3", [P, 2, NC, B * S], F32R)
        wstage = sb("wstage", [P, NC + NI, 512])
        ew = sb("ew", [P, 2, 2, NC + NI, 512], F32R)
        sg = sb("sg", [P, NI, S])
        hv = sb("hv", [P, NI, S])
        hs = sb("hs", [P, 2, 2, NI, S], F32R)
        w8 = sb("w8", [P, NE, B * NT])
        wcur = sb("wcur", [P, 2, B * NT])
        gtmp = sb("gtmp", [P, 6, B * NT, NE])
        gden = sb("gden", [P, 2, B * NT])

        v_ld = sem("vectors_loaded")
        c_ok = sem("constants_ready")
        prep = sem("vector_prep_steps")
        vT = sem("vectors_turned")
        wemb_ld = sem("w_emb_loaded")
        mod_mm = sem("modulation_product")
        spn = sem("sp_waits_passed")
        phase_done = sem("phase_done")
        r_ok = sem("rounded_constants_ready")
        rw_ok = sem("router_weights_scaled")
        m_ld = sem("phase3_inputs_loaded")
        mm_free0 = sem("phase3_psum_free")
        ew_ld, ew_ln, ew_hi, ew_lo = (sem(f"expert_{x}") for x in ("loaded", "scaled", "hi", "lo"))
        h_v, h_hi, h_lo = (sem(f"hidden_{x}") for x in ("ready", "hi", "lo"))
        w_cur = sem("expert_token_weights")
        g_exp, g_step = sem("router_exp"), sem("router_steps")
        out_st = sem("out_stored")
        guring = Ring("gate_up", sem, (0, 1, 2, 3), 2 * B * 4)
        dring = Ring("down", sem, (4, 5, 6, 7), 2 * B * 4)

        class Phase:
            pass

        ph = {}
        for n in (1, 2):
            p = ph[n] = Phase()
            s = lambda name, n=n: sem(f"{name}_{n}")
            p.n = n
            p.items = {k: i for i, k in enumerate(ITEMS[n])}
            p.ring = Ring(f"ring{n}", sem, (0, 1), len(ITEMS[n]))
            p.sq = Ring(f"scores{n}", sem, (2, 3), H * NT)
            p.sk = Ring(f"scoresT{n}", sem, (4, 5), H * NT)
            p.o = Ring(f"pv{n}", sem, (6, 7), H)
            p.w_ld = [s("weights_loaded_even"), s("weights_loaded_odd")]
            p.w_hi, p.w_lo, p.w_ln = s("weights_hi"), s("weights_lo"), s("weights_scaled")
            p.x_ld, p.xn, p.ss = s("x_loaded"), s("x_normalized"), s("token_squares")
            p.step = s("dve_steps")
            p.hi = s("hi_of_psum")
            p.v, p.vhi, p.vlo = s("value_ready"), s("value_hi"), s("value_lo")
            p.head_sq, p.head_ss = s("head_squares"), s("head_square_sums")
            p.qn, p.kn = s("q_normalized"), s("k_normalized")
            p.rt, p.ra = s("rotary_terms"), s("rotary_added")
            p.split_st, p.split_free = s("split_stored"), s("split_free")
            p.stack_ld = [s("stack_loaded_even"), s("stack_loaded_odd")]
            p.y_st, p.y_free = s("y_stored"), s("y_free")
            p.acc_ok = s("acc_ready")
            p.lg_ok = s("logits_ready")
            p.norms = sum(1 for _ in ITEMS[n])
        V1 = NC + NG
        HI = {1: NG + NC, 2: 2 * NG + 3 * NC - 2}

        def item(p, key):
            return p.items[key]

        HI_ORDER = {
            1: [("turn", g, "k") for g in range(NG)] + [("turn_o", c) for c in range(NC)],
            2: [("x", c) for c in range(NC)] + ["kv_d", "q_d"]
            + [("turn", g, c) for g in range(NG) for c in "kq"] + [("turn_o", c) for c in range(NC)]
            + [("x2", c) for c in range(NC)],
        }
        HI = {n: len(x) for n, x in HI_ORDER.items()}
        hi_no = {n: {k: i for i, k in enumerate(x)} for n, x in HI_ORDER.items()}
        STEPS = {1: 1 + 2 * RSQRT_STEPS + H, 2: 2 * RSQRT_STEPS + H}

        W2_D, W2_KU, W2_Q, W2_VU, W2_O = 0, 2048, 2304, 2816, 3328
        fc = lambda w: w.rearrange("(c p) n -> p c n", p=P)
        PIECES = {
            1: [(c * 1536, 1536, [(slice(0, 1536), wqkv_d[c * P:(c + 1) * P, :])]) for c in range(NC)]
            + [(6144, 2048, [("c", 0, 512, fc(wout_d))])],
            2: [(W2_D, 2048, [("c", 0, 128, fc(kvd_d)), ("c", 128, 128, fc(qd_d)), ("c", 256, 256, fc(rk_d))]),
                (W2_KU, 1280, [(slice(0, 256), ku_d), (slice(256, 512), qu_d), (slice(512, 768), rq_d),
                               (slice(768, 1280), vu_d)]),
                (W2_O, 2048, [("c", 0, 512, fc(ow_d))])],
        }
        NLOAD = {n: [sum(len(q[2]) for q in pc[i % 2:i + 1:2]) for i in range(len(pc))] for n, pc in PIECES.items()}

        def stage(i):
            return qk[:, :, :].rearrange("p t n -> p (t n)")[:, 2048 * (i % 2):2048 * (i % 2) + 2048]

        block = ctx.enter_context(nc.Block())

        @block.sync
        def _(sp):
            def passed():
                sp.sem_inc(spn, 1)

            def load_weights(n):
                p = ph[n]
                for i, (_, cols, parts) in enumerate(PIECES[n]):
                    if i >= 2:
                        sp.wait_ge(p.w_lo, i - 1)
                    for part in parts:
                        if part[0] == "c":
                            _, at, width, src = part
                            dst = stage(i).rearrange("p (c n) -> p c n", c=NC)[:, :, at:at + width]
                        else:
                            dst, src = stage(i)[:, part[0]], part[1]
                        sp.dma_start(dst, src).then_inc(p.w_ld[i % 2], 16)

            def stacks(p, b, g):
                if p.n == 1:
                    sp.wait_ge(p.vlo, b * V1 + (2 + NC + g + 1))
                    passed()
                else:
                    p.ring.wait_read(sp, b, item(p, ("turn", g, "q")))
                    passed()
                p.ring.wait_read(sp, b, item(p, ("turn", g, "k")))
                passed()
                sp.dma_start(split_s[g % 2], split[:, g % 2].bitcast(F32)).then_inc(p.split_st, 16)
                sp.wait_ge(p.split_st, b * 16 * NG + 16 * (g + 1))
                passed()
                sp.sem_inc(p.split_free, 1)
                last = 4 * (HPG * (g - 2) + HPG - 1) + 3
                sp.wait_ge(p.sk.full[1], b * p.sk.per + (H + last // 2 + 1))
                passed()
                src = split_s[g % 2].rearrange("(h p) c t -> p h c t", p=DH)
                at = HPG * (g % 2)
                for role, (cq, ck) in enumerate(((0, 2), (1, 2), (0, 3))):
                    for n, c in enumerate((cq, ck)):
                        sp.dma_start(stack[DH * role:DH * role + DH, at:at + HPG, n].bitcast(F32),
                                     src[:, :, c]).then_inc(p.stack_ld[g % 2], 16)

            sp.dma_start(vrow[0:16, :], cond_d.rearrange("b (c p) -> (b c) p", p=P)).then_inc(v_ld, 16)
            for at, rows, src in ((16, 8, bemb_d), (24, 4, gnorm_d), (28, 4, ln1_d), (32, 4, ln2_d)):
                sp.dma_start(vrow[at:at + rows, :], src.rearrange("(c p) -> c p", p=P)).then_inc(v_ld, 16)
            for row, src in ((36, gq_d), (37, gk_d)):
                for h in range(HPG):
                    sp.dma_start(vrow[row:row + 1, h * DH:(h + 1) * DH],
                                 src.rearrange("(a d) -> a d", a=1)).then_inc(v_ld, 16)
            sp.dma_start(probs[:, :, :, :].rearrange("p a t n -> p (a t n)").rearrange("p (k n) -> p k n", k=NC),
                         wemb_d.rearrange("(k p) n -> p k n", p=P)).then_inc(wemb_ld, 16)
            sp.dma_start(rope[:, 0], cos_d.rearrange("(t p) r -> p t r", p=P)).then_inc(v_ld, 16)
            sp.dma_start(rope[:, 1], sin_d.rearrange("(t p) r -> p t r", p=P)).then_inc(v_ld, 16)
            sp.dma_start(rwt[:, :, 0:NR], rw_d.rearrange("(c p) e -> p c e", p=P)).then_inc(v_ld, 16)
            sp.dma_start(rb[:, 0:NR], rb_d.rearrange("(a e) -> a e", a=1).broadcast_to([P, NR])).then_inc(v_ld, 16)
            load_weights(1)
            p = ph[1]
            sp.sem_inc(p.split_free, 2)
            sp.sem_inc(p.y_free, 1)
            with sp.Fori(0, B) as b:
                sp.wait_ge(p.xn, b * NT + NT)
                passed()
                sp.dma_start(xt[:, :, :], x_d[bass.ds(b, 1)].rearrange("a (t p) n -> p (a t) n", p=P)).then_inc(p.x_ld, 16)
                for g in range(NG):
                    stacks(p, b, g)
                for t in (NT - 2, NT - 1):
                    p.ring.wait_read(sp, b, item(p, ("out", t)))
                    passed()
                sp.dma_start(x1_s[bass.ds(b, 1)].rearrange("a p t n -> p (a t) n"), yt[:, :, :]).then_inc(p.y_st, 16)
                sp.wait_ge(p.y_st, b * 16 + 16)
                passed()
                sp.sem_inc(p.y_free, 1)
            sp.wait_ge(p.y_st, 16 * B)
            sp.sem_inc(phase_done, 1)

            load_weights(2)
            p = ph[2]
            sp.sem_inc(p.split_free, 2)
            sp.sem_inc(p.y_free, 1)
            with sp.Fori(0, B) as b:
                sp.wait_ge(p.y_free, b + 1)
                passed()
                sp.dma_start(xt[:, :, :], x1_s[bass.ds(b, 1)].rearrange("a p t n -> p (a t) n")).then_inc(p.x_ld, 16)
                sp.dma_start(yt[:, :, :], x_d[bass.ds(b, 1)].rearrange("a (t p) n -> p (a t) n", p=P)).then_inc(p.x_ld, 16)
                for g in range(NG):
                    stacks(p, b, g)
                sp.wait_ge(p.acc_ok, b * NT + NT)
                passed()
                sp.dma_start(acc_s[bass.ds(b, 1)].rearrange("a p t n -> p (a t) n"), yt[:, :, :]).then_inc(p.y_st, 16)
                for c in (NC - 2, NC - 1):
                    p.ring.wait_read(sp, b, item(p, ("x2", c)))
                    passed()
                for n, t_ in enumerate((xh, xl)):
                    sp.dma_start(xt_s[n, :, :, bass.ds(b, 1), :].rearrange("p c a t -> p c (a t)"),
                                 t_[:, :, :].bitcast(F32)).then_inc(p.y_st, 16)
                sp.wait_ge(p.lg_ok, b * 2 + 2)
                passed()
                sp.dma_start(logits[:, bass.ds(b * NT, NT), :], lg[:, :, :]).then_inc(p.y_st, 16)
                sp.wait_ge(p.y_st, b * 64 + 64)
                passed()
                sp.sem_inc(p.y_free, 1)
            sp.wait_ge(p.y_st, 64 * B)
            sp.sem_inc(phase_done, 1)

            sp.dma_start(acc[:, :, :], acc_s.rearrange("b p t n -> p b (t n)")).then_inc(m_ld, 16)
            for n in range(2):
                sp.dma_start(x3[:, n].rearrange("p c t -> p (c t)").bitcast(F32),
                             xt_s[n].rearrange("p c b t -> p (c b t)")).then_inc(m_ld, 16)

            def load_expert(e):
                for at, src in ((0, gate_d), (INNER, up_d)):
                    sp.dma_start(wstage[:, 0:NC, at:at + INNER],
                                 src[bass.ds(e, 1)].rearrange("a (c p) i -> p (a c) i", p=P)).then_inc(ew_ld, 16)
                sp.dma_start(wstage[:, NC:, :],
                             down_d[bass.ds(e, 1)].rearrange("a (c p) i -> p (a c) i", p=P)).then_inc(ew_ld, 16)

            load_expert(0)
            with sp.Fori(0, NE // 2) as i:
                for j in range(2):
                    sp.wait_ge(ew_lo, i * 6 + 3 * (j + 1))
                    passed()
                    load_expert((i * 2 + (j + 1)) % NE)
            for t in range(NT):
                sp.wait_ge(dring.free[t], 1 + B * NE)
            sp.wait_ge(ew_ld, 48 * (NE + 1))
            sp.dma_start(out_d.rearrange("b (t p) n -> p (b t) n", p=P), acc[:, :, :]).then_inc(out_st, 16)
            sp.wait_ge(out_st, 16)

        @block.tensor
        def _(pe):
            def three(out, lhs, rhs, last_of=None):
                n = len(lhs)
                for i, ((ah, al), (bh, bl)) in enumerate(zip(lhs, rhs)):
                    nc.tensor.matmul(out, ah, bh, start=(i == 0), stop=False)
                    nc.tensor.matmul(out, al, bh, start=False, stop=False)
                    last = nc.tensor.matmul(out, ah, bl, start=False, stop=(i == n - 1))
                return last

            def turn(p, b, key, src):
                m = item(p, key)
                p.ring.wait_free(pe, b, m)
                for t in range(NT):
                    last = nc.tensor.transpose(psum[:, p.ring.bank(m), t * P:(t + 1) * P], src(t), ident[:, :])
                p.ring.filled(last, m)

            def heads(p, b, causal):
                def scores(h, t):
                    m = 4 * h + t
                    g = h // HPG
                    if t == 0:
                        pe.wait_ge(p.stack_ld[g % 2], b * 192 + 96 * (g // 2 + 1))
                    p.sq.wait_free(pe, b, m)
                    n = (t + 1) * P if causal else S
                    bank = p.sq.bank(m)
                    st = stack[0:XSTACK, h % NSTK]
                    last = nc.tensor.matmul(psum[:, bank, 0:n], st[:, 0, t * P:(t + 1) * P], st[:, 1, 0:n],
                                            start=True, stop=not causal)
                    if causal:
                        last = nc.tensor.matmul(psum[:, bank, t * P:n], identr[:, :], maskq[:, :],
                                                start=False, stop=True)
                    p.sq.filled(last, m)

                def turn_max(h):
                    m = item(p, ("max", h))
                    p.ring.wait_free(pe, b, m)
                    for t in (2, 3):
                        p.sq.wait_read(pe, b, 4 * h + t)
                    for t in range(NT):
                        last = nc.tensor.transpose(psum[0:1, p.ring.bank(m), t * P:(t + 1) * P],
                                                   nmax[:, h % 4, t:t + 1], ident[:, :])
                    p.ring.filled(last, m)

                def scores_t(h, t):
                    m = 4 * h + t
                    if t == 0:
                        p.ring.wait_read(pe, b, item(p, ("max", h)))
                    p.sk.wait_free(pe, b, m)
                    lo = t * P if causal else 0
                    bank = p.sk.bank(m)
                    st = stack[0:XSTACK + 1, h % NSTK]
                    last = nc.tensor.matmul(psum[:, bank, lo:S], st[:, 1, t * P:(t + 1) * P], st[:, 0, lo:S],
                                            start=True, stop=not causal)
                    if causal:
                        last = nc.tensor.matmul(psum[:, bank, lo:lo + P], identr[:, :], maskk[:, :],
                                                start=False, stop=True)
                    last.then_inc(p.sk.full[m % 2], 1)

                def pv(h, t):
                    if t == 0:
                        p.o.wait_free(pe, b, h)
                        for kt in (2, 3):
                            p.sk.wait_read(pe, b, 4 * h + kt)
                    keys = t + 1 if causal else NT
                    for kt in range(keys):
                        last = nc.tensor.matmul(psum[:, p.o.bank(h), t * 64:t * 64 + DH + 1],
                                                probs[:, h % 2, kt, t * P:(t + 1) * P], vaug[:, kt, h, :],
                                                start=(kt == 0), stop=(kt == keys - 1))
                    if t == NT - 1:
                        p.o.filled(last, h)

                def turn_qk(g, c):
                    at = (D if c == "k" else 0) + g * P
                    turn(p, b, ("turn", g, c), lambda t: qk[:, t, at:at + P])

                if p.n == 1:
                    pe.wait_ge(p.kn, b * NT + NT)
                    pe.wait_ge(p.qn, b * NT + NT)
                else:
                    pe.wait_ge(p.ra, b * 8 + 10)
                for g in range(2):
                    for c in "kq":
                        turn_qk(g, c)
                for h in range(2):
                    for t in range(NT):
                        scores(h, t)
                turn_max(0)
                for h in range(H + 1):
                    for t in range(NT):
                        if h + 2 < H:
                            scores(h + 2, t)
                        if t == 1 and h + 1 < H:
                            turn_max(h + 1)
                        if h < H:
                            scores_t(h, t)
                        if h >= 1:
                            pv(h - 1, t)
                    if h % 4 == 2 and h // 4 + 2 < NG:
                        for c in "kq":
                            turn_qk(h // 4 + 2, c)
                for h in (H - 2, H - 1):
                    p.o.wait_read(pe, b, h)
                for c in range(NC):
                    turn(p, b, ("turn_o", c), lambda t: ot[:, t, c * P:(c + 1) * P])

            def x_by(wat, width, stride):
                return [(wh[:, wat + c * stride:wat + c * stride + width], wl[:, wat + c * stride:wat + c * stride + width])
                        for c in range(NC)]

            def tokens(t):
                return [(xh[:, c, t * P:(t + 1) * P], xl[:, c, t * P:(t + 1) * P]) for c in range(NC)]

            def chans():
                return [(xh[:, c, :], xl[:, c, :]) for c in range(NC)]

            def project(p, b, key, lhs, rhs):
                m = item(p, key)
                p.ring.wait_free(pe, b, m)
                n = rhs[0][0].shape[-1]
                p.ring.filled(three(psum[:, p.ring.bank(m), 0:n], lhs, rhs), m)

            pe.wait_ge(c_ok, 7)
            pe.wait_ge(r_ok, 3)
            pe.wait_ge(v_ld, 17 * 16)
            nc.tensor.transpose(psum[:, 0, 0:38], vrow[0:38, :], ident[0:38, 0:38]).then_inc(vT, 1)
            pe.wait_ge(prep, 1)
            pe.wait_ge(wemb_ld, 16)
            wemb = probs[:, :, :, :].rearrange("p a t n -> p (a t n)").rearrange("p (k n) -> p k n", k=NC)
            for m in range(2 * NC):
                for k in range(NC):
                    last = nc.tensor.matmul(psum[:, 1, m * B:(m + 1) * B], wemb[:, k, m * P:(m + 1) * P],
                                            vcol[:, k:16:4], start=(k == 0), stop=(k == NC - 1))
            last.then_inc(mod_mm, 1)

            p = ph[1]
            pe.sem_inc(p.sk.full[1], H)
            pe.sem_inc(p.o.full[0], 1)
            pe.sem_inc(p.o.full[1], 1)
            pe.wait_ge(p.w_lo, len(PIECES[1]))
            with pe.Fori(0, B) as b:
                pe.wait_ge(p.xn, b * NT + 2 * NT)
                for c in range(NC):
                    turn(p, b, ("x", c), lambda t: ot[:, t, c * P:(c + 1) * P])
                pe.wait_ge(p.vlo, b * V1 + (2 + NC))
                for t in range(NT):
                    for n, c in enumerate("qk"):
                        project(p, b, ("qk", t, c), tokens(t), x_by(n * D, D, 3 * D))
                for t in range(NT):
                    project(p, b, ("v", t), tokens(t), x_by(2 * D, D, 3 * D))
                heads(p, b, causal=False)
                for c in (NC - 2, NC - 1):
                    p.ring.wait_read(pe, b, item(p, ("turn_o", c)))
                for t in range(NT):
                    project(p, b, ("out", t), tokens(t), x_by(3 * D * NC, D, D))

            p = ph[2]
            pe.wait_ge(phase_done, 1)
            pe.sem_inc(p.sk.full[1], H)
            pe.sem_inc(p.o.full[0], 1)
            pe.sem_inc(p.o.full[1], 1)
            pe.wait_ge(p.w_lo, len(PIECES[2]) + 1)
            kvh, qdh = (wh[:, 6144:6656], wl[:, 6144:6656]), (wh[:, 6656:7168], wl[:, 6656:7168])
            pair = lambda at, n: (wh[:, at:at + n], wl[:, at:at + n])
            cut = lambda xx, t: (xx[0][:, t * P:(t + 1) * P], xx[1][:, t * P:(t + 1) * P])
            with pe.Fori(0, B) as b:
                pe.wait_ge(p.xn, b * 2 * NT + NT)
                for c in range(NC):
                    turn(p, b, ("x", c), lambda t: ot[:, t, c * P:(c + 1) * P])
                for c in (NC - 2, NC - 1):
                    p.ring.wait_read(pe, b, item(p, ("x", c)))
                project(p, b, "kv_d", x_by(W2_D, P, 512), chans())
                project(p, b, "q_d", x_by(W2_D + P, P, 512), chans())
                for key in ("kv_d", "q_d"):
                    p.ring.wait_read(pe, b, item(p, key))
                for t in range(NT):
                    project(p, b, ("qk", t, "q"), [cut(qdh, t)], [pair(W2_Q, 512)])
                    m = item(p, ("qk", t, "k"))
                    p.ring.wait_free(pe, b, m)
                    three(psum[:, p.ring.bank(m), 0:256], [cut(kvh, t)], [pair(W2_KU, 256)])
                    p.ring.filled(three(psum[:, p.ring.bank(m), 256:512], tokens(t), x_by(W2_D + 256, 256, 512)), m)
                for t in range(NT):
                    project(p, b, ("v", t), [cut(kvh, t)], [pair(W2_VU, 512)])
                heads(p, b, causal=True)
                for c in (NC - 2, NC - 1):
                    p.ring.wait_read(pe, b, item(p, ("turn_o", c)))
                for t in range(NT):
                    project(p, b, ("out", t), tokens(t), x_by(W2_O, D, D))
                pe.wait_ge(p.xn, b * 2 * NT + 2 * NT)
                for c in range(NC):
                    turn(p, b, ("x2", c), lambda t: ot[:, t, c * P:(c + 1) * P])
                for c in (NC - 2, NC - 1):
                    p.ring.wait_read(pe, b, item(p, ("x2", c)))
                for n in range(2):
                    m = item(p, ("router", n))
                    p.ring.wait_free(pe, b, m)
                    for t in (2 * n, 2 * n + 1):
                        last = three(psum[:, p.ring.bank(m), t * NE:(t + 1) * NE], tokens(t),
                                     [(rwh[:, c, :], rwl[:, c, :]) for c in range(NC)])
                    p.ring.filled(last, m)

            pe.wait_ge(m_ld, 48)
            pe.wait_ge(mm_free0, 1)
            with pe.Fori(0, NE // 2) as i:
                def gate_up(k):
                    j, blk = divmod(k, B)
                    if blk == 0:
                        pe.wait_ge(ew_lo, i * 6 + 3 * (j + 1))
                    for n in range(NI):
                        for u in range(2):
                            m = 4 * k + 2 * n + u
                            guring.wait_free(pe, i, m)
                            at = u * INNER + n * P
                            last = three(psum[:, guring.bank(m), :],
                                         [(ew[:, j, 0, c, at:at + P], ew[:, j, 1, c, at:at + P]) for c in range(NC)],
                                         [(x3[:, 0, c, blk * S:(blk + 1) * S], x3[:, 1, c, blk * S:(blk + 1) * S])
                                          for c in range(NC)])
                            guring.filled(last, m)

                def down(k):
                    j = k // B
                    pe.wait_ge(h_lo, i * 16 + (2 + 2 * k + 2))
                    for t in range(NT):
                        m = 4 * k + t
                        dring.wait_free(pe, i, m)
                        last = three(psum[:, dring.bank(m), :],
                                     [(hs[:, k % 2, 0, n, t * P:(t + 1) * P], hs[:, k % 2, 1, n, t * P:(t + 1) * P])
                                      for n in range(NI)],
                                     [(ew[:, j, 0, NC + n, :], ew[:, j, 1, NC + n, :]) for n in range(NI)])
                        dring.filled(last, m)

                for k in range(2 * B):
                    gate_up(k)
                    if k:
                        down(k - 1)
                down(2 * B - 1)

        @block.scalar
        def _(act):
            def weights(n):
                p = ph[n]
                for i, (at, cols, _) in enumerate(PIECES[n]):
                    if n == 2 and i == 0:
                        act.wait_ge(p.w_ln, NC)
                    act.wait_ge(p.w_ld[i % 2], 16 * NLOAD[n][i])
                    nc.scalar.activation(wh[:, at:at + cols], stage(i)[:, 0:cols], ACT.Copy).then_inc(p.w_hi, 1)

            def squares(p, b, src, first, per):
                for t in range(NT):
                    nc.scalar.activation(probs[:, 0, t, :], src[:, t, :], ACT.Square,
                                         accum_out=sst[:, t:t + 1]).then_inc(p.ss, 1)

            def hi_of(p, b, key, out):
                m = item(p, key)
                p.ring.wait_full(act, b, m)
                nc.scalar.activation(out, psum[:, p.ring.bank(m), :], ACT.Copy).then_inc(p.hi, 1)

            def hi_of_value(p, b, k, out):
                act.wait_ge(p.v, b * V1 + (k + 1))
                nc.scalar.activation(out, vs[:, k % 2, :], ACT.Copy).then_inc(p.vhi, 1)

            def turn_qk(p, b, g, c):
                at = {"q": 0, "k": 2}[c]
                act.wait_ge(p.split_free, b * NG + (g + 1))
                if p.n == 1 and c == "q":
                    hi_of_value(p, b, NC + g, split[:, g % 2, at, :])
                else:
                    hi_of(p, b, ("turn", g, c), split[:, g % 2, at, :])

            def values(p, b):
                for t in range(NT):
                    m = item(p, ("v", t))
                    p.ring.wait_full(act, b, m)
                    p.ring.cleared(nc.scalar.activation(
                        vaug[:, t, :, 0:DH], psum[:, p.ring.bank(m), :].rearrange("p (h d) -> p h d", d=DH), ACT.Copy), m)

            def max_row(p, b, h):
                m = item(p, ("max", h))
                p.ring.wait_full(act, b, m)
                p.ring.cleared(nc.scalar.activation(stack[XSTACK:XSTACK + 1, h % NSTK, 0, :],
                                                    psum[0:1, p.ring.bank(m), :], ACT.Copy), m)

            def heads(p, b, causal):
                for g in range(2):
                    for c in "kq":
                        turn_qk(p, b, g, c)
                max_row(p, b, 0)
                for h in range(H):
                    for t in range(NT):
                        m = 4 * h + t
                        if m % 2 == 0:
                            act.wait_ge(p.sk.full[0], b * p.sk.per + (m // 2 + 1))
                        else:
                            act.wait_ge(p.sk.full[1], b * p.sk.per + (H + m // 2 + 1))
                        if t == 0:
                            act.wait_ge(p.o.full[h % 2], b * p.o.per + (h // 2 + 1))
                        lo = t * P if causal else 0
                        p.sk.cleared(nc.scalar.activation(probs[:, h % 2, t, lo:S], psum[:, p.sk.bank(m), lo:S],
                                                          ACT.Exp, scale=SCALE), m)
                        if t == 2 and h + 1 < H:
                            max_row(p, b, h + 1)
                    if h % 4 == 2 and h // 4 + 2 < NG:
                        for c in "kq":
                            turn_qk(p, b, h // 4 + 2, c)
                for c in range(NC):
                    hi_of(p, b, ("turn_o", c), xh[:, c, :])

            act.wait_ge(c_ok, 4)
            nc.scalar.activation(identr[:, :], ident[:, :], ACT.Copy).then_inc(r_ok, 1)
            act.wait_ge(c_ok, 6)
            nc.scalar.activation(maskq[:, :], vs[:, 0, 0:P], ACT.Copy).then_inc(r_ok, 1)
            nc.scalar.activation(maskk[:, :], vs[:, 1, 0:P], ACT.Copy).then_inc(r_ok, 1)
            weights(1)
            p = ph[1]
            act.sem_inc(p.sk.free[0], 1)
            act.sem_inc(p.sk.free[1], 1)
            act.wait_ge(mod_mm, 1)
            with act.Fori(0, B) as b:
                act.wait_ge(p.x_ld, b * 16 + 16)
                squares(p, b, xt, 0, NT)
                for k in range(NC):
                    hi_of_value(p, b, k, xh[:, k, :])
                for t in range(NT):
                    for n, c in enumerate("qk"):
                        m = item(p, ("qk", t, c))
                        p.ring.wait_full(act, b, m)
                        p.ring.cleared(nc.scalar.activation(qk[:, t, n * D:(n + 1) * D],
                                                            psum[:, p.ring.bank(m), :], ACT.Copy), m)
                values(p, b)
                heads(p, b, causal=False)

            p = ph[2]
            act.wait_ge(phase_done, 1)
            act.sem_inc(p.sk.free[0], 1)
            act.sem_inc(p.sk.free[1], 1)
            weights(2)
            act.wait_ge(rw_ok, 1)
            nc.scalar.activation(rwh[:, :, :], rwt[:, :, :], ACT.Copy).then_inc(p.w_hi, 1)
            with act.Fori(0, B) as b:
                act.wait_ge(p.x_ld, b * 32 + 32)
                squares(p, b, xt, 0, 2 * NT)
                act.wait_ge(p.y_free, b + 1)
                for c in range(NC):
                    hi_of(p, b, ("x", c), xh[:, c, :])
                hi_of(p, b, "kv_d", wh[:, 6144:6656])
                hi_of(p, b, "q_d", wh[:, 6656:7168])
                for t in range(NT):
                    for n, c in enumerate("qk"):
                        m = item(p, ("qk", t, c))
                        p.ring.wait_full(act, b, m)
                        nc.scalar.activation(
                            qk[:, t, n * D:(n + 1) * D].rearrange("p (h d) -> p h d", d=DH)[:, :, 0:RD],
                            psum[:, p.ring.bank(m), 0:H * RD].rearrange("p (h d) -> p h d", d=RD),
                            ACT.Copy).then_inc(p.head_sq, 1)
                values(p, b)
                heads(p, b, causal=True)
                act.wait_ge(p.acc_ok, b * NT + NT)
                squares(p, b, xt, NT, 2 * NT)
                for c in range(NC):
                    hi_of(p, b, ("x2", c), xh[:, c, :])

            act.wait_ge(phase_done, 2)
            for n in (0, 2):
                act.sem_inc(guring.free[n], 1)
            nc.scalar.activation(gtmp[:, 0], logits[:, :, :], ACT.Exp, scale=-1.0).then_inc(g_exp, 1)

            def split_expert(e, j, c):
                nc.scalar.activation(ew[:, j, 0, 2 * c:2 * c + 2, :], wstage[:, 2 * c:2 * c + 2, :],
                                     ACT.Copy).then_inc(ew_hi, 1)

            act.wait_ge(ew_ln, NC)
            for c in range(3):
                split_expert(0, 0, c)
            with act.Fori(0, NE // 2) as i:
                for k in range(2 * B):
                    j, blk = divmod(k, B)
                    for n in range(NI):
                        m = 4 * k + 2 * n
                        guring.wait_full(act, i, m)
                        act.wait_ge(h_v, i * 16 + (2 + 2 * k + n - 1))
                        guring.cleared(nc.scalar.activation(sg[:, n, :], psum[:, guring.bank(m), :], ACT.Silu), m)
                    for n in range(NI):
                        act.wait_ge(h_v, i * 16 + (2 + 2 * k + n + 1))
                        nc.scalar.activation(hs[:, k % 2, 0, n, :], hv[:, n, :], ACT.Copy).then_inc(h_hi, 1)
                    if blk:
                        act.wait_ge(ew_ln, i * 2 * NC + NC * (j + 2))
                        split_expert(0, 1 - j, blk - 1)

        @block.gpsimd
        def _(pool):
            nc.gpsimd.memset(ident[:, :], 0.0).then_inc(c_ok, 1)
            pool.wait_ge(c_ok, 1)
            nc.gpsimd.affine_select(out=ident[:, :], in_=ident[:, :], compare_op=ALU.not_equal, fill=1.0, base=0,
                                    pattern=[[-1, P]], channel_multiplier=1).then_inc(c_ok, 1)
            nc.gpsimd.memset(vaug[:, :, :, DH:DH + 1], 1.0).then_inc(c_ok, 1)
            nc.gpsimd.memset(vs[:, :, 0:P], 0.0).then_inc(c_ok, 1)
            pool.wait_ge(c_ok, 4)
            nc.gpsimd.affine_select(out=vs[:, 0, 0:P], in_=vs[:, 0, 0:P], compare_op=ALU.is_ge, fill=NEG, base=0,
                                    pattern=[[-1, P]], channel_multiplier=1).then_inc(c_ok, 1)
            nc.gpsimd.affine_select(out=vs[:, 1, 0:P], in_=vs[:, 1, 0:P], compare_op=ALU.is_ge, fill=NEG, base=0,
                                    pattern=[[1, P]], channel_multiplier=-1).then_inc(c_ok, 1)
            pool.wait_ge(c_ok, 6)
            nc.gpsimd.memset(stack[XSTACK:XSTACK + 1, :, 1, :].bitcast(F32), 1.0).then_inc(c_ok, 1)

            def lo_of_value(p, b, k, hi, out):
                pool.wait_ge(p.vhi, b * V1 + (k + 1))
                nc.gpsimd.tensor_tensor(out, vs[:, k % 2, :], hi.bitcast(F32), ALU.subtract).then_inc(p.vlo, 1)

            def turn_q(p, b, g):
                lo_of_value(p, b, NC + g, split[:, g % 2, 0, :], split[:, g % 2, 1, :])

            pool.wait_ge(c_ok, 7)
            p = ph[1]
            pool.sem_inc(p.vlo, 2)
            with pool.Fori(0, B) as b:
                for c in range(NC):
                    lo_of_value(p, b, c, xh[:, c, :], xl[:, c, :])
                for n in range(2 * NT):
                    t, c = divmod(n, 2)
                    p.ring.wait_read(pool, b, item(p, ("qk", t, "qk"[c])))
                    pool.wait_ge(p.head_ss, b * 2 * NT + (n + 1))
                    src = qk[:, t, c * D:(c + 1) * D]
                    nc.gpsimd.tensor_tensor(sq[:, n % 2, :], src, src, ALU.mult).then_inc(p.head_sq, 1)
                pool.wait_ge(p.step, b * STEPS[1] + (1 + 2 * RSQRT_STEPS))
                for t in range(NT):
                    kk = qk[:, t, D:2 * D].rearrange("p (h d) -> p h d", d=DH)
                    r = rsh[:, 0, t * 2 * H + H:(t + 1) * 2 * H].unsqueeze(2).broadcast_to([P, H, DH])
                    nc.gpsimd.tensor_tensor(kk, kk, r, ALU.mult).then_inc(p.kn, 1)
                for g in range(NG):
                    turn_q(p, b, g)

            p = ph[2]
            pool.wait_ge(phase_done, 1)
            with pool.Fori(0, B) as b:
                for n in range(2 * NT):
                    t, c = divmod(n, 2)
                    pool.wait_ge(p.rt, b * 2 * NT + (n + 1))
                    r = lambda a: sq[:, n % 2, a * 256:(a + 1) * 256].rearrange("p (h d) -> p h d", d=RD)
                    nc.gpsimd.tensor_tensor(
                        qk[:, t, c * D:(c + 1) * D].rearrange("p (h d) -> p h d", d=DH)[:, :, RD:DH],
                        r(0), r(1), ALU.add).then_inc(p.ra, 1)
                for t in range(NT):
                    p.ring.wait_read(pool, b, item(p, ("out", t)))
                    nc.gpsimd.tensor_tensor(yt[:, t, :], yt[:, t, :], xt[:, t, :], ALU.add).then_inc(p.acc_ok, 1)

            pool.wait_ge(phase_done, 2)
            pool.sem_inc(h_lo, 2)

            def split_expert(e, j, c):
                nc.gpsimd.tensor_tensor(ew[:, j, 1, 2 * c:2 * c + 2, :], wstage[:, 2 * c:2 * c + 2, :],
                                        ew[:, j, 0, 2 * c:2 * c + 2, :].bitcast(F32), ALU.subtract).then_inc(ew_lo, 1)

            for c in range(3):
                pool.wait_ge(ew_hi, c + 1)
                split_expert(0, 0, c)
            with pool.Fori(0, NE // 2) as i:
                for k in range(2 * B):
                    j, blk = divmod(k, B)
                    for n in range(NI):
                        pool.wait_ge(h_hi, i * 16 + (2 * k + n + 1))
                        nc.gpsimd.tensor_tensor(hs[:, k % 2, 1, n, :], hv[:, n, :], hs[:, k % 2, 0, n, :].bitcast(F32),
                                                ALU.subtract).then_inc(h_lo, 1)
                    if blk:
                        pool.wait_ge(ew_hi, i * 6 + (3 * (j + 1) + blk))
                        split_expert(0, 1 - j, blk - 1)

        @block.vector
        def _(dve):
            class Chain:

                def __init__(self, s, base=None, per=0):
                    self.s, self.base, self.per, self.n = s, base, per, 0

                def __call__(self, ins):
                    self.n += 1
                    ins.then_inc(self.s, 1)
                    v = self.n if self.base is None else self.base * self.per + self.n
                    dve.wait_ge(self.s, v)

            V = nc.vector

            def rsqrt(link, x, y, t, mean, eps):
                link(V.tensor_scalar(x, x, mean, eps, ALU.mult, ALU.add))
                link(V.tensor_scalar(y.bitcast(I32), x.bitcast(I32), 1, None, ALU.logical_shift_right))
                link(V.tensor_scalar(y.bitcast(I32), y.bitcast(I32), -1, MAGIC, ALU.mult, ALU.add))
                for _ in range(3):
                    link(V.scalar_tensor_tensor(out=t, in0=y, scalar=-0.5, in1=y, op0=ALU.mult, op1=ALU.mult))
                    link(V.tensor_tensor(t, t, x, ALU.mult))
                    link(V.scalar_tensor_tensor(out=y, in0=t, scalar=1.5, in1=y, op0=ALU.add, op1=ALU.mult))

            def normalize(p, b, link, eps, src, nth, per, order):
                dve.wait_ge(p.ss, b * per + NT * (nth + 1))
                rsqrt(link, sst[:, :], rst[:, 0, :], rst[:, 1, :], 1.0 / D, eps)
                for t in range(NT):
                    V.tensor_scalar(ot[:, t, :], src[:, t, :], rst[:, 0, t:t + 1], None, ALU.mult).then_inc(p.xn, 1)

            def lo_of(p, b, key, hi, out):
                m = item(p, key)
                dve.wait_ge(p.hi, b * HI[p.n] + (hi_no[p.n][key] + 1))
                p.ring.cleared(V.tensor_tensor(out, psum[:, p.ring.bank(m), :], hi.bitcast(F32), ALU.subtract), m)

            def value(p, b, k, key, s1, s2):
                m = item(p, key)
                p.ring.wait_full(dve, b, m)
                dve.wait_ge(p.vlo, b * V1 + (k + 1))
                if s2 is None:
                    V.tensor_scalar(vs[:, k % 2, :], psum[:, p.ring.bank(m), :], s1, None, ALU.mult).then_inc(p.v, 1)
                else:
                    V.tensor_scalar(vs[:, k % 2, :], psum[:, p.ring.bank(m), :], s1, s2, ALU.mult, ALU.add)\
                        .then_inc(p.v, 1)
                dve.wait_ge(p.v, b * V1 + (k + 1))
                dve.sem_inc(p.ring.free[m % 2], 1)

            def turn_qk(p, b, g, c):
                if p.n == 1 and c == "q":
                    value(p, b, NC + g, ("turn", g, c), gqk[:, 0:1], None)
                else:
                    at = {"q": 0, "k": 2}[c]
                    lo_of(p, b, ("turn", g, c), split[:, g % 2, at, :], split[:, g % 2, at + 1, :])

            def heads(p, b, link, causal):
                def maxima(h):
                    for t in range(NT):
                        m = 4 * h + t
                        p.sq.wait_full(dve, b, m)
                        n = (t + 1) * P if causal else S
                        p.sq.cleared(V.tensor_reduce(nmax[:, h % 4, t:t + 1], psum[:, p.sq.bank(m), 0:n], AX.X,
                                                     ALU.max, negate=True), m)

                def output(h):
                    dve.wait_ge(p.o.full[h % 2], b * p.o.per + (h // 2 + 2))
                    o = psum[:, p.o.bank(h), 0:256].rearrange("p (t d) -> p t d", d=64)
                    r = rden[:, h % 2, :]
                    link(V.reciprocal(r, o[:, :, DH]))
                    p.o.cleared(V.tensor_tensor(ot[:, :, h * DH:(h + 1) * DH], o[:, :, 0:DH],
                                                r.unsqueeze(2).broadcast_to([P, NT, DH]), ALU.mult), h)

                for g in range(2):
                    for c in "kq":
                        turn_qk(p, b, g, c)
                for h in range(2):
                    maxima(h)
                for h in range(H):
                    if h + 2 < H:
                        maxima(h + 2)
                    if h >= 2:
                        output(h - 2)
                    if h % 4 == 2 and h // 4 + 2 < NG:
                        for c in "kq":
                            turn_qk(p, b, h // 4 + 2, c)
                output(H - 2)
                output(H - 1)
                for c in range(NC):
                    lo_of(p, b, ("turn_o", c), xh[:, c, :], xl[:, c, :])

            link = Chain(prep)
            dve.wait_ge(vT, 1)
            link(V.tensor_copy(vcol[:, :], psum[:, 0, 0:38]))
            dve.wait_ge(v_ld, 17 * 16)
            link(V.tensor_tensor(gqk[:, :], vcol[:, 36:37], vcol[:, 37:38], ALU.mult))
            link(V.memset(rwt[:, :, NR:NE], 0.0))
            link(V.memset(rb[:, NR:NE], 0.0))
            dve.wait_ge(mod_mm, 1)
            for m in range(2 * NC):
                link(V.tensor_scalar(modall[:, :, m], psum[:, 1, m * B:(m + 1) * B], vcol[:, 16 + m:17 + m], None, ALU.add))
            for m in range(NC):
                link(V.tensor_scalar(modall[:, :, m], modall[:, :, m], 1.0, vcol[:, 24 + m:25 + m], ALU.add, ALU.mult))

            def weights(n):
                p = ph[n]
                for i, (at, cols, _) in enumerate(PIECES[n]):
                    if n == 2 and i == 0:
                        dve.wait_ge(p.w_ld[0], 16 * NLOAD[n][0])
                        for c in range(NC):
                            w = stage(0)[:, c * 512:(c + 1) * 512]
                            V.tensor_scalar(w, w, vcol[:, 28 + c:29 + c], None, ALU.mult).then_inc(p.w_ln, 1)
                    dve.wait_ge(p.w_hi, i + 1)
                    V.tensor_tensor(wl[:, at:at + cols], stage(i)[:, 0:cols], wh[:, at:at + cols].bitcast(F32),
                                    ALU.subtract).then_inc(p.w_lo, 1)

            weights(1)
            p = ph[1]
            for r in (p.ring, p.sq, p.o):
                for n in range(2):
                    dve.sem_inc(r.free[n], 1)
            dve.sem_inc(p.xn, NT)
            dve.sem_inc(p.head_ss, 2)
            dve.wait_ge(r_ok, 3)
            with dve.Fori(0, B) as b:
                link = Chain(p.step, b, STEPS[1])
                link(V.tensor_copy(mod[:, :], modall[:, bass.ds(b, 1), :].rearrange("p a m -> p (a m)")))
                normalize(p, b, link, EPS_COND, xt, 0, NT, None)
                for c in range(NC):
                    value(p, b, c, ("x", c), mod[:, c:c + 1], mod[:, NC + c:NC + c + 1])
                for n in range(2 * NT):
                    t, c = divmod(n, 2)
                    dve.wait_ge(p.head_sq, b * 2 * NT + (n + 1))
                    V.tensor_reduce(ssh[:, t, c * H:(c + 1) * H], sq[:, n % 2, :].rearrange("p (h d) -> p h d", d=DH),
                                    AX.X, ALU.add).then_inc(p.head_ss, 1)
                dve.wait_ge(p.head_ss, b * 2 * NT + (2 * NT + 2))
                rsqrt(link, ssh[:, :, :].rearrange("p t h -> p (t h)"), rsh[:, 0, :], rsh[:, 1, :], 1.0 / DH, EPS_COND)
                for t in range(NT):
                    qq = qk[:, t, 0:D].rearrange("p (h d) -> p h d", d=DH)
                    r = rsh[:, 0, t * 2 * H:t * 2 * H + H].unsqueeze(2).broadcast_to([P, H, DH])
                    V.tensor_tensor(qq, qq, r, ALU.mult).then_inc(p.qn, 1)
                heads(p, b, link, causal=False)
                dve.wait_ge(p.y_free, b + 1)
                for t in range(NT):
                    m = item(p, ("out", t))
                    p.ring.wait_full(dve, b, m)
                    p.ring.cleared(V.tensor_tensor(yt[:, t, :], psum[:, p.ring.bank(m), :], ot[:, t, :], ALU.add), m)
                assert link.n == STEPS[1]

            p = ph[2]
            dve.wait_ge(phase_done, 1)
            for r in (p.ring, p.sq, p.o):
                for n in range(2):
                    dve.sem_inc(r.free[n], 1)
            dve.sem_inc(p.ra, 2)
            for c in range(NC):
                ins = V.tensor_scalar(rwt[:, c, :], rwt[:, c, :], vcol[:, 32 + c:33 + c], None, ALU.mult)
            ins.then_inc(rw_ok, 1)
            weights(2)
            dve.wait_ge(p.w_hi, len(PIECES[2]) + 1)
            V.tensor_tensor(rwl[:, :, :], rwt[:, :, :], rwh[:, :, :].bitcast(F32), ALU.subtract).then_inc(p.w_lo, 1)
            with dve.Fori(0, B) as b:
                link = Chain(p.step, b, STEPS[2])
                normalize(p, b, link, EPS_FFN, xt, 0, 2 * NT, None)
                for c in range(NC):
                    lo_of(p, b, ("x", c), xh[:, c, :], xl[:, c, :])
                lo_of(p, b, "kv_d", wh[:, 6144:6656], wl[:, 6144:6656])
                lo_of(p, b, "q_d", wh[:, 6656:7168], wl[:, 6656:7168])
                for n in range(2 * NT):
                    t, c = divmod(n, 2)
                    m = item(p, ("qk", t, "qk"[c]))
                    dve.wait_ge(p.head_sq, b * 2 * NT + (n + 1))
                    dve.wait_ge(p.ra, b * 2 * NT + (n + 1))
                    x = psum[:, p.ring.bank(m), 256:512].rearrange("p (h d) -> p h d", d=RD)
                    t1 = sq[:, n % 2, 0:256].rearrange("p (h d) -> p h d", d=RD)
                    t2 = sq[:, n % 2, 256:512].rearrange("p (h d) -> p h d", d=RD)
                    wide = lambda a, w: a.unsqueeze(1).broadcast_to([P, H, w])
                    V.tensor_tensor(t1, x, wide(rope[:, 0, t, :], RD), ALU.mult)
                    V.tensor_tensor(t2[:, :, 0:RD // 2], x[:, :, RD // 2:RD], wide(rope[:, 1, t, 0:RD // 2], RD // 2), ALU.mult)
                    V.tensor_tensor(t2[:, :, RD // 2:RD], x[:, :, 0:RD // 2], wide(rope[:, 1, t, RD // 2:RD], RD // 2),
                                    ALU.mult).then_inc(p.rt, 1)
                    dve.wait_ge(p.rt, b * 2 * NT + (n + 1))
                    dve.sem_inc(p.ring.free[m % 2], 1)
                heads(p, b, link, causal=True)
                for t in range(NT):
                    m = item(p, ("out", t))
                    p.ring.wait_full(dve, b, m)
                    p.ring.cleared(V.tensor_tensor(xt[:, t, :], psum[:, p.ring.bank(m), :], xt[:, t, :], ALU.add), m)
                normalize(p, b, link, EPS_FFN, xt, 1, 2 * NT, None)
                for c in range(NC):
                    lo_of(p, b, ("x2", c), xh[:, c, :], xl[:, c, :])
                for n in range(2):
                    m = item(p, ("router", n))
                    p.ring.wait_full(dve, b, m)
                    V.tensor_tensor(lg[:, 2 * n:2 * n + 2, :],
                                    psum[:, p.ring.bank(m), 2 * n * NE:(2 * n + 2) * NE].rearrange("p (t e) -> p t e", e=NE),
                                    rb[:, :].unsqueeze(1).broadcast_to([P, 2, NE]), ALU.add).then_inc(p.lg_ok, 1)
                    dve.wait_ge(p.lg_ok, b * 2 + (n + 1))
                    dve.sem_inc(p.ring.free[m % 2], 1)
                assert link.n == STEPS[2]

            dve.wait_ge(phase_done, 2)
            dve.sem_inc(h_v, 2)
            for n in (1, 3):
                dve.sem_inc(guring.free[n], 1)
            for n in range(4):
                dve.sem_inc(dring.free[n], 1)
            dve.sem_inc(mm_free0, 1)

            def scale_expert():
                for c in range(NC):
                    V.tensor_scalar(wstage[:, c, :], wstage[:, c, :], vcol[:, 32 + c:33 + c], None,
                                    ALU.mult).then_inc(ew_ln, 1)

            dve.wait_ge(ew_ld, 48)
            scale_expert()
            link = Chain(g_step)
            prob, rank, cmp, gg = gtmp[:, 1], gtmp[:, 2], gtmp[:, 3], gtmp[:, 4]
            dve.wait_ge(g_exp, 1)
            link(V.tensor_scalar(gtmp[:, 0], gtmp[:, 0], 1.0, None, ALU.add))
            link(V.reciprocal(prob, gtmp[:, 0]))
            link(V.memset(rank, 0.0))
            for j in range(NR):
                for lo, hi, op in ((0, j, ALU.is_gt), (j + 1, NR, ALU.is_ge)):
                    if lo < hi:
                        pj = prob[:, :, j:j + 1].broadcast_to([P, B * NT, hi - lo])
                        link(V.tensor_tensor(cmp[:, :, lo:hi], pj, prob[:, :, lo:hi], op))
                        link(V.tensor_tensor(rank[:, :, lo:hi], rank[:, :, lo:hi], cmp[:, :, lo:hi], ALU.add))
            link(V.tensor_scalar(cmp[:, :, 0:NR], rank[:, :, 0:NR], 2.0, None, ALU.is_lt))
            link(V.tensor_tensor(gg[:, :, 0:NR], prob[:, :, 0:NR], cmp[:, :, 0:NR], ALU.mult))
            link(V.tensor_reduce(gden[:, 0, :], gg[:, :, 0:NR], AX.X, ALU.add))
            link(V.reciprocal(gden[:, 1, :], gden[:, 0, :]))
            link(V.memset(w8[:, 0, :], 1.0 / SCALING))
            for e in range(NR):
                link(V.scalar_tensor_tensor(out=w8[:, 1 + e, :], in0=gg[:, :, e], scalar=1.0 / SCALING,
                                            in1=gden[:, 1, :], op0=ALU.mult, op1=ALU.mult))
            dve.wait_ge(m_ld, 48)
            with dve.Fori(0, NE // 2) as i:
                def combine(k):
                    j, blk = divmod(k, B)
                    for t in range(NT):
                        m = 4 * k + t
                        a = acc[:, blk * NT + t, :]
                        dring.wait_full(dve, i, m)
                        dring.cleared(V.scalar_tensor_tensor(out=a, in0=psum[:, dring.bank(m), :],
                                                             scalar=wcur[:, j, blk * NT + t:blk * NT + t + 1], in1=a,
                                                             op0=ALU.mult, op1=ALU.add), m)

                for k in range(2 * B):
                    j, blk = divmod(k, B)
                    if blk == 0:
                        V.tensor_copy(wcur[:, j, :], w8[:, bass.ds(i * 2 + j, 1), :].rearrange("p a t -> p (a t)"))\
                            .then_inc(w_cur, 1)
                        dve.wait_ge(w_cur, i * 2 + (j + 1))
                        dve.wait_ge(ew_ld, i * 96 + 48 * (j + 2))
                        scale_expert()
                    for n in range(NI):
                        m = 4 * k + 2 * n + 1
                        guring.wait_full(dve, i, m)
                        guring.wait_read(dve, i, m - 1)
                        dve.wait_ge(h_lo, i * 16 + (2 * k + n + 1))
                        V.tensor_tensor(hv[:, n, :], psum[:, guring.bank(m), :], sg[:, n, :], ALU.mult).then_inc(h_v, 1)
                        dve.wait_ge(h_v, i * 16 + (2 + 2 * k + n + 1))
                        dve.sem_inc(guring.free[m % 4], 1)
                    if k:
                        combine(k - 1)
                combine(2 * B - 1)


_INS = ['x', 'cond_2048', 'L0_cond_W_emb', 'L0_cond_b_emb', 'L0_cond_g_norm', 'L0_cond_W_qkv', 'L0_cond_g_q',
        'L0_cond_g_k', 'L0_cond_W_out', 'L0_ffn_ln1_w', 'L0_ffn_ln2_w', 'L0_ffn_kv_d_w', 'L0_ffn_q_d_w',
        'L0_ffn_k_u_w', 'L0_ffn_v_u_w', 'L0_ffn_q_u_w', 'L0_ffn_rope_k_w', 'L0_ffn_rope_q_w', 'L0_ffn_o_w',
        'gate', 'up', 'down', 'L0_ffn_router_w', 'L0_ffn_router_b', 'rope_cos', 'rope_sin']


def rope_tables():
    half = RD // 2
    freq = (1.0 / np.float32(10000.0) ** (np.arange(0, RD, 2, dtype=np.float32) / np.float32(RD))).astype(np.float32)
    ang = np.outer(np.arange(S, dtype=np.float32), freq).astype(np.float32)
    cos, sin = np.cos(ang), np.sin(ang)
    return (np.concatenate([cos, cos], 1).astype(np.float32), np.concatenate([-sin, sin], 1).astype(np.float32))


def kernel(**inputs):
    import concourse.bacc as bacc
    from concourse.bass_utils import run_bass_kernel_spmd as run

    data = dict(inputs)
    for name in ("gate", "up", "down"):
        shared = np.asarray(inputs[f"L0_ffn_sh_{name}"])[None]
        data[name] = np.concatenate([shared, np.asarray(inputs[f"L0_ffn_r_{name}"])], axis=0)
    data["rope_cos"], data["rope_sin"] = rope_tables()

    nc = bacc.Bacc("TRN2", target_bir_lowering=False, num_devices=1)
    arrays, args = {}, []
    for name in _INS:
        a = np.ascontiguousarray(data[name])
        arrays[f"in_{name}_dram"] = a
        args.append(nc.dram_tensor(f"in_{name}_dram", a.shape, mybir.dt.from_np(a.dtype), kind="ExternalInput").ap())
    args.append(nc.dram_tensor("out_dram", (B, S, D), F32, kind="ExternalOutput").ap())
    build(nc, *args)
    r = run(nc, [arrays], core_ids=[0])
    return r.results[0]["out_dram"]
```

```python
from contextlib import ExitStack

import numpy as np

import concourse.bass as bass
from concourse import mybir

F32 = mybir.dt.float32
F32R = mybir.dt.float32r
I32 = mybir.dt.int32
ALU = mybir.AluOpType
ACT = mybir.ActivationFunctionType
AX = mybir.AxisListType

P = 128
B, S, D = 4, 512, 512
NT, NC = S // P, D // P
H, DH = 16, 32
RD = DH // 2
LAT = 128
INNER = 256
NE, NR = 8, 7
NI = INNER // P
HPG, NG = P // DH, H * DH // P
SCALE = float(DH) ** -0.5
SCALING = 8.0
EPS_COND, EPS_FFN = 1e-6, 1e-5
EPS = {1: EPS_COND, 2: EPS_FFN}
NEG = -1e30
MAGIC = 0x5F3759DF
RSQRT_STEPS = 12
XSTACK = 3 * DH
NSTK = 8

STEPS_H = H * NT
LEAD = 2 * NT
LAG = 3
VW = H * (DH + 1) + P - DH


def head_max(m):
    return m // NT + 1 if m % NT == 1 and m // NT + 1 < H else None


def head_out(m):
    h = (m - NT + 1 - LAG - 3) // NT
    return h if (m - NT + 1 - LAG - 3) % NT == 0 and 0 <= h < H else None


def group_turn(m):
    g = m // (4 * NT) + 2
    return g if m % (4 * NT) == 3 * NT - 1 and g < NG else None


LAST = NT - 1 + LAG + 3 + NT * (H - 1)

SQUARE_STEP, NORM_STEP = 30, 33
BESIDE = {
    1: {38 + 4 * c: ("x", c) for c in range(NC)},
    2: {38 + 4 * c: ("x", c) for c in range(NC)} | {3 + c: ("x2", c) for c in range(NC)}
    | {7 + n: ("router", n) for n in range(2)},
}

_FIRST = [x for g in range(2) for x in (("turn", g, "k"), ("turn", g, "q"), ("v", 2 * g), ("v", 2 * g + 1))]
_HEADS = {n: [("max", 0)] + [
    x for m in range(LAST + 1) for x in
    ([("max", head_max(m))] if head_max(m) is not None else [])
    + ([("o", head_out(m))] if head_out(m) is not None else [])
    + ([("turn", group_turn(m), "k"), ("turn", group_turn(m), "q")] if group_turn(m) else [])
    + ([BESIDE[n][m]] if m in BESIDE[n] else [])] for n in (1, 2)}
_TURN_O = [("turn_o", c) for c in range(NC)]
_X0 = [("x0", c) for c in range(NC)]
_OUT = [("out", t) for t in range(NT)]
_QK = [("qk", t, c) for t in range(NT) for c in "qk"]
BEFORE = {1: _X0, 2: _X0}
BODY = {
    1: _QK + _OUT + _FIRST + _HEADS[1] + _TURN_O,
    2: ["kv_d", "q_d"] + _QK + _OUT + _FIRST + _HEADS[2] + _TURN_O,
}
AFTER = {
    1: [("last", t) for t in range(NT)],
    2: [("last", t) for t in range(NT)] + [("last_x2", c) for c in range(NC)] + [("last_router", n) for n in range(2)],
}
ITEMS = {n: BEFORE[n] + BODY[n] + AFTER[n] for n in (1, 2)}
assert all(len(x[n]) % 2 == 0 for x in (BEFORE, BODY, AFTER) for n in (1, 2))


class Ring:

    def __init__(self, name, sem, banks, per_loop, outside=0):
        self.banks, self.n = banks, len(banks)
        self.per = per_loop // self.n
        self.extra = outside // self.n
        self.full = [sem(f"{name}_full{i}") for i in range(self.n)]
        self.free = [sem(f"{name}_free{i}") for i in range(self.n)]

    def bank(self, m):
        return self.banks[m % self.n]

    def wait_free(self, eng, i, m):
        eng.wait_ge(self.free[m % self.n], i * self.per + (m // self.n + 1))

    def wait_full(self, eng, i, m):
        eng.wait_ge(self.full[m % self.n], i * self.per + (m // self.n + 1))

    def wait_read(self, eng, i, m):
        eng.wait_ge(self.free[m % self.n], i * self.per + (m // self.n + 2))

    def filled(self, ins, m):
        ins.then_inc(self.full[m % self.n], 1)

    def cleared(self, ins, m):
        ins.then_inc(self.free[m % self.n], 1)


def build(nc, x_d, cond_d, wemb_d, bemb_d, gnorm_d, wqkv_d, gq_d, gk_d, wout_d, ln1_d, ln2_d, kvd_d,
          qd_d, ku_d, vu_d, qu_d, rk_d, rq_d, ow_d, gate_d, up_d, down_d, rw_d, rb_d, cos_d, sin_d,
          out_d):
    dram = lambda name, shape: nc.dram_tensor(name, shape, F32, kind="Internal").ap()
    x1_s = dram("x1_s", (B, P, NT, D))
    acc_s = dram("acc_s", (B, P, NT, D))
    xt_s = dram("xt_s", (B, P, 2, NC, S))
    split_s = dram("split_s", (2, P, 4, S))

    with ExitStack() as ctx:
        sem = lambda name: ctx.enter_context(nc.semaphore(name))
        keep = lambda name, shape, dt=F32: ctx.enter_context(nc.sbuf_tensor(name, shape, dt))
        psum = ctx.enter_context(nc.psum_tensor("psum", [P, 8, 512], F32))

        ident = keep("ident", [P, P])
        identr = keep("identr", [P, P], F32R)
        vrow = keep("vrow", [P, P])
        vcol = keep("vcol", [P, 38])
        logits = keep("logits", [P, B * NT, NE])
        xh = keep("xh", [P, NC, S], F32R)
        xl = keep("xl", [P, NC, S], F32R)
        yt = keep("yt", [P, NT, D])

        room = ExitStack()
        sb = lambda name, shape, dt=F32: room.enter_context(nc.sbuf_tensor(name, shape, dt))
        wh = sb("wh", [P, 8192], F32R)
        wl = sb("wl", [P, 8192], F32R)
        split = sb("split", [P, 4, S], F32R)
        stack = sb("stack", [P, NSTK, 2, S], F32R)
        vs = sb("vs", [P, 2, S])
        qk = sb("qk", [P, NT, 2 * D])
        vh = sb("vh", [P, NT, VW], F32R)
        vl = sb("vl", [P, NT, VW], F32R)
        probs = sb("probs", [P, NT, S])
        ph_ = sb("probs_hi", [P, NT, S], F32R)
        pl_ = sb("probs_lo", [P, NT, S], F32R)
        ov = sb("ov", [P, 2, S])
        xt = sb("xt", [P, NT, D])
        ot = sb("ot", [P, NT, D])
        maskq = sb("maskq", [P, P], F32R)
        maskk = sb("maskk", [P, P], F32R)
        rope = sb("rope", [P, 2, NT, RD])
        modall = sb("modall", [P, B + 1, 2 * NC])
        mod = sb("mod", [P, 2 * NC])
        gqk = sb("gqk", [P, 1])
        junk = sb("junk", [P, S])
        sst = sb("sst", [P, NT])
        rst = sb("rst", [P, 2, NT])
        ssh = sb("ssh", [P, NT, 2 * H])
        rsh = sb("rsh", [P, 2, NT * 2 * H])
        nmax = sb("nmax", [P, 4, NT])
        rden = sb("rden", [P, 2, NT])
        rwt = sb("rwt", [P, NC, NE])
        rwh = sb("rwh", [P, NC, NE], F32R)
        rwl = sb("rwl", [P, NC, NE], F32R)
        rb = sb("rb", [P, NE])
        lg = sb("lg", [P, NT, NE])
        room.close()

        room3 = ctx.enter_context(ExitStack())
        sb = lambda name, shape, dt=F32: room3.enter_context(nc.sbuf_tensor(name, shape, dt))
        x3 = sb("x3", [P, B - 1, 2, NC, S], F32R)
        acc = sb("acc", [P, B - 1, NT, D])
        hs = sb("hs", [P, 2, 2, NI, S], F32R)
        wstage = sb("wstage", [P, NC + NI, 512])
        ew = sb("ew", [P, 2, 2, NC + NI, 512], F32R)
        sg = sb("sg", [P, NI, S])
        hv = sb("hv", [P, NI, S])
        w8 = sb("w8", [P, NE, B * NT])
        wcur = sb("wcur", [P, 2, B * NT])
        gtmp = sb("gtmp", [P, 6, B * NT, NE])
        gden = sb("gden", [P, 2, B * NT])

        v_ld = sem("vectors_loaded")
        c_ok = sem("constants_ready")
        prep, prep2 = sem("vector_prep_steps"), sem("dve_steps_between_loops")
        vT = sem("vectors_turned")
        wemb_ld = sem("w_emb_loaded")
        mod_mm = sem("modulation_product")
        spn, pln = sem("sp_waits_passed"), sem("pool_waits_passed")
        r_ok = sem("rounded_constants_ready")
        rw_ok = sem("router_weights_scaled")
        x3_ld = [sem(f"x3_loaded{blk}") for blk in range(B - 1)]
        acc_ld = [sem(f"acc_loaded{blk}") for blk in range(B - 1)]
        ew_ld, ew_ln, ew_hi, ew_lo = (sem(f"expert_{x}") for x in ("loaded", "scaled", "hi", "lo"))
        h_v, h_hi, h_lo = (sem(f"hidden_{x}") for x in ("ready", "hi", "lo"))
        w_cur = sem("expert_token_weights")
        g_exp, g_step = sem("router_exp"), sem("router_steps")
        out_st = sem("out_stored")
        guring = Ring("gate_up", sem, (0, 1, 2, 3), 2 * B * 4)
        dring = Ring("down", sem, (4, 5, 6, 7), 2 * B * 4)

        class Phase:
            pass

        ph = {}
        for n in (1, 2):
            p = ph[n] = Phase()
            s = lambda name, n=n: sem(f"{name}_{n}")
            p.n = n
            p.items = {k: i for i, k in enumerate(ITEMS[n])}
            p.ring = Ring(f"ring{n}", sem, (0, 1), len(BODY[n]), len(BEFORE[n]) + len(AFTER[n]))
            p.sq = Ring(f"scores{n}", sem, (2, 3), H * NT)
            p.sk = Ring(f"scoresT{n}", sem, (4, 5), H * NT)
            p.o = Ring(f"pv{n}", sem, (6, 7), H)
            p.w_ld = [s("weights_loaded_even"), s("weights_loaded_odd")]
            p.w_hi, p.w_lo, p.w_ln = s("weights_hi"), s("weights_lo"), s("weights_scaled")
            p.x_ld, p.xn, p.ss = s("x_loaded"), s("x_normalized"), s("token_squares")
            p.step = s("dve_steps")
            p.hi = s("hi_of_psum")
            p.v, p.vhi, p.vlo = s("value_ready"), s("value_hi"), s("value_lo")
            p.head_sq, p.head_ss = s("head_squares"), s("head_square_sums")
            p.qn, p.kn = s("q_normalized"), s("k_normalized")
            p.p_x = [s(f"probs_ready{t}") for t in range(NT - 1)]
            p.p_hi = s("probs_hi_by_dve")
            p.p_lo = [s(f"probs_lo{t}") for t in range(NT)]
            p.rt, p.ra = s("rotary_terms"), s("rotary_added")
            p.split_st, p.split_free = s("split_stored"), s("split_free")
            p.stack_ld = [s("stack_loaded_even"), s("stack_loaded_odd")]
            p.y_st, p.y_free = s("y_stored"), s("y_free")
            p.ones = s("ones_rows_set")
            p.acc_ok = s("acc_ready")
            p.r_ld = s("residual_inputs_loaded")
            p.lg_ok = s("logits_ready")
        V1 = NC + NG

        def item(p, key):
            return p.items[key]

        HI_ORDER = {
            1: [k for k in ITEMS[1] if k[0] in ("turn", "v", "turn_o") and k[-1] != "q"],
            2: [k for k in ITEMS[2] if k in ("kv_d", "q_d") or k[0] in ("x0", "x", "turn", "v", "turn_o", "x2", "last_x2")],
        }
        HI = {n: sum(k in BODY[n] for k in x) for n, x in HI_ORDER.items()}
        hi_no = {n: {k: i for i, k in enumerate(x)} for n, x in HI_ORDER.items()}
        STEPS = {1: 1 + 2 * RSQRT_STEPS + H, 2: 2 * RSQRT_STEPS + H}
        PER = {1: NT, 2: 2 * NT}

        W2_D, W2_KU, W2_Q, W2_VU, W2_O = 0, 2048, 2304, 2816, 3328
        fc = lambda w: w.rearrange("(c p) n -> p c n", p=P)
        PIECES = {
            1: [(c * 1536, 1536, [(slice(0, 1536), wqkv_d[c * P:(c + 1) * P, :])]) for c in range(NC)]
            + [(6144, 2048, [("c", 0, 512, fc(wout_d))])],
            2: [(W2_D, 2048, [("c", 0, 128, fc(kvd_d)), ("c", 128, 128, fc(qd_d)), ("c", 256, 256, fc(rk_d))]),
                (W2_KU, 1280, [(slice(0, 256), ku_d), (slice(256, 512), qu_d), (slice(512, 768), rq_d),
                               (slice(768, 1280), vu_d)]),
                (W2_O, 2048, [("c", 0, 512, fc(ow_d))])],
        }
        NLOAD = {n: [sum(len(q[2]) for q in pc[i % 2:i + 1:2]) for i in range(len(pc))] for n, pc in PIECES.items()}

        def stage(i):
            return qk[:, :, :].rearrange("p t n -> p (t n)")[:, 2048 * (i % 2):2048 * (i % 2) + 2048]

        def take_over(eng, old, new):
            for m in range(2):
                eng.wait_ge(old.free[m], B * old.per + old.extra + 1)
                eng.sem_inc(new.free[m], 1)

        def acc_of(blk):
            return acc[:, blk] if blk < B - 1 else yt

        def x3_of(blk, c):
            return (x3[:, blk, 0, c, :], x3[:, blk, 1, c, :]) if blk < B - 1 else (xh[:, c, :], xl[:, c, :])

        def resid(t):
            return (wh, wl)[t // 2][:, 7168 + t % 2 * D:7168 + (t % 2 + 1) * D].bitcast(F32)

        def o_t(c):
            return stack[:, c, 0, :], stack[:, c, 1, :]

        block = ctx.enter_context(nc.Block())

        @block.sync
        def _(sp):
            def passed():
                sp.sem_inc(spn, 1)

            def load_weights(n, pieces):
                p = ph[n]
                for i in pieces:
                    parts = PIECES[n][i][2]
                    if i >= 2:
                        sp.wait_ge(p.w_lo, i - 1)
                    for part in parts:
                        if part[0] == "c":
                            _, at, width, src = part
                            dst = stage(i).rearrange("p (c n) -> p c n", c=NC)[:, :, at:at + width]
                        else:
                            dst, src = stage(i)[:, part[0]], part[1]
                        sp.dma_start(dst, src).then_inc(p.w_ld[i % 2], 16)

            def stacks(p, b, g):
                if p.n == 1:
                    sp.wait_ge(p.vlo, b * V1 + (2 + NC + g + 1))
                    passed()
                else:
                    p.ring.wait_read(sp, b, item(p, ("turn", g, "q")))
                    passed()
                p.ring.wait_read(sp, b, item(p, ("turn", g, "k")))
                passed()
                sp.dma_start(split_s[g % 2], split[:, :, :].bitcast(F32)).then_inc(p.split_st, 16)
                sp.wait_ge(p.split_st, b * 16 * NG + 16 * (g + 1))
                passed()
                sp.sem_inc(p.split_free, 1)
                last = 4 * (HPG * (g - 2) + HPG - 1) + 3
                sp.wait_ge(p.sk.full[1], b * p.sk.per + (H + last // 2 + 1))
                passed()
                src = split_s[g % 2].rearrange("(h p) c t -> p h c t", p=DH)
                at = HPG * (g % 2)
                for role, (cq, ck) in enumerate(((0, 2), (1, 2), (0, 3))):
                    for n, c in enumerate((cq, ck)):
                        sp.dma_start(stack[DH * role:DH * role + DH, at:at + HPG, n].bitcast(F32),
                                     src[:, :, c]).then_inc(p.stack_ld[g % 2], 16)

            def load_x(b):
                sp.dma_start(xt[:, :, :], x_d[bass.ds(b, 1)].rearrange("a (t p) n -> p (a t) n", p=P))\
                    .then_inc(ph[1].x_ld, 16)

            def load_x1(b):
                sp.dma_start(xt[:, :, :], x1_s[bass.ds(b, 1)].rearrange("a p t n -> p (a t) n")).then_inc(ph[2].x_ld, 16)

            sp.dma_start(vrow[0:16, :], cond_d.rearrange("b (c p) -> (b c) p", p=P)).then_inc(v_ld, 16)
            for at, rows, src in ((16, 8, bemb_d), (24, 4, gnorm_d), (28, 4, ln1_d), (32, 4, ln2_d)):
                sp.dma_start(vrow[at:at + rows, :], src.rearrange("(c p) -> c p", p=P)).then_inc(v_ld, 16)
            for row, src in ((36, gq_d), (37, gk_d)):
                for h in range(HPG):
                    sp.dma_start(vrow[row:row + 1, h * DH:(h + 1) * DH],
                                 src.rearrange("(a d) -> a d", a=1)).then_inc(v_ld, 16)
            for n, t_ in enumerate((ot, yt)):
                sp.dma_start(t_[:, :, :].rearrange("p a n -> p (a n)").rearrange("p (k n) -> p k n", k=2),
                             wemb_d.rearrange("(k p) n -> p k n", p=P)[:, 2 * n:2 * n + 2]).then_inc(wemb_ld, 16)
            sp.dma_start(rope[:, 0], cos_d.rearrange("(t p) r -> p t r", p=P)).then_inc(v_ld, 16)
            sp.dma_start(rope[:, 1], sin_d.rearrange("(t p) r -> p t r", p=P)).then_inc(v_ld, 16)
            sp.dma_start(rwt[:, :, 0:NR], rw_d.rearrange("(c p) e -> p c e", p=P)).then_inc(v_ld, 16)
            sp.dma_start(rb[:, 0:NR], rb_d.rearrange("(a e) -> a e", a=1).broadcast_to([P, NR])).then_inc(v_ld, 16)
            load_x(0)
            load_weights(1, range(len(PIECES[1])))
            p = ph[1]
            sp.sem_inc(p.split_free, 1)
            sp.sem_inc(p.y_free, 1)
            with sp.Fori(0, B) as b:
                sp.wait_ge(p.v, b * V1 + NC)
                passed()
                load_x((b + 1) % B)
                for t in (NT - 2, NT - 1):
                    p.ring.wait_read(sp, b, item(p, ("out", t)))
                    passed()
                sp.dma_start(x1_s[bass.ds((b + (B - 1)) % B, 1)].rearrange("a p t n -> p (a t) n"), yt[:, :, :])\
                    .then_inc(p.y_st, 16)
                for g in range(NG):
                    stacks(p, b, g)
                sp.wait_ge(p.y_st, b * 16 + 16)
                passed()
                sp.sem_inc(p.y_free, 1)
            load_weights(2, range(2))
            sp.wait_ge(p.v, B * V1 + NC)
            load_x1(0)
            load_weights(2, range(2, 3))
            for t in (NT - 2, NT - 1):
                p.ring.wait_read(sp, B - 1, item(p, ("last", t)))
            sp.dma_start(x1_s[B - 1], yt[:, :, :]).then_inc(p.y_st, 16)
            sp.wait_ge(p.y_st, 16 * (B + 1))

            p = ph[2]
            sp.sem_inc(p.split_free, 1)
            sp.sem_inc(p.r_ld, 1)
            with sp.Fori(0, B) as b:
                sp.wait_ge(p.hi, b * HI[2] + NC)
                passed()
                load_x1((b + 1) % B)
                for g in range(2):
                    stacks(p, b, g)
                sp.wait_ge(p.acc_ok, b * NT + NT)
                passed()
                before = bass.ds((b + (B - 1)) % B, 1)
                sp.dma_start(acc_s[before].rearrange("a p t n -> p (a t) n"), yt[:, :, :]).then_inc(p.y_st, 16)
                for c in (NC - 2, NC - 1):
                    p.ring.wait_read(sp, b, item(p, ("x2", c)))
                    passed()
                for n, t_ in enumerate((xh, xl)):
                    sp.dma_start(xt_s[bass.ds((b + (B - 1)) % B, 1), :, n].rearrange("a p c t -> p (a c) t"),
                                 t_[:, :, :].bitcast(F32)).then_inc(p.y_st, 16)
                sp.wait_ge(p.lg_ok, b * 2 + 2)
                passed()
                sp.dma_start(logits[:, bass.ds((b + (B - 1)) % B * NT, NT), :], lg[:, :, :]).then_inc(p.y_st, 16)
                stacks(p, b, 2)
                sp.wait_ge(p.y_st, b * 64 + 64)
                passed()
                sp.sem_inc(p.y_free, 1)
                sp.dma_start(yt[:, :, :], x_d[bass.ds(b, 1)].rearrange("a (t p) n -> p (a t) n", p=P)).then_inc(p.r_ld, 16)
                for n, w in enumerate((wh, wl)):
                    sp.dma_start(w[:, 7168:8192].bitcast(F32).rearrange("p (t n) -> p t n", n=D),
                                 x1_s[bass.ds(b, 1), :, 2 * n:2 * n + 2].rearrange("a p t n -> p (a t) n"))\
                        .then_inc(p.r_ld, 16)
                stacks(p, b, 3)

            def load_expert(e):
                for at, src in ((0, gate_d), (INNER, up_d)):
                    sp.dma_start(wstage[:, 0:NC, at:at + INNER],
                                 src[bass.ds(e, 1)].rearrange("a (c p) i -> p (a c) i", p=P)).then_inc(ew_ld, 16)
                sp.dma_start(wstage[:, NC:, :],
                             down_d[bass.ds(e, 1)].rearrange("a (c p) i -> p (a c) i", p=P)).then_inc(ew_ld, 16)

            sp.wait_ge(p.sk.full[1], B * p.sk.per + H)
            load_expert(0)
            p.ring.wait_full(sp, B - 1, item(p, ("last", NT - 1)))
            for blk in range(B - 1):
                sp.dma_start(x3[:, blk].rearrange("p n c t -> p (n c t)").bitcast(F32),
                             xt_s[blk].rearrange("p n c t -> p (n c t)")).then_inc(x3_ld[blk], 16)
                if blk == 0:
                    for t in (NT - 2, NT - 1):
                        p.ring.wait_read(sp, B - 1, item(p, ("last", t)))
                sp.dma_start(acc[:, blk], acc_s[blk]).then_inc(acc_ld[blk], 16)
            with sp.Fori(0, NE // 2) as i:
                for j in range(2):
                    sp.wait_ge(ew_lo, i * 6 + 3 * (j + 1))
                    passed()
                    load_expert((i * 2 + (j + 1)) % NE)
            sp.wait_ge(ew_ld, 48 * (NE + 1))
            sp.wait_ge(ph[2].y_st, 64 * B)
            sp.wait_ge(ph[2].x_ld, 16 * (B + 1))
            for blk in range(B):
                for t in range(NT):
                    sp.wait_ge(dring.free[t], 1 + B * (NE - 1) + blk + 1)
                sp.dma_start(out_d[blk].rearrange("(t p) n -> p t n", p=P), acc_of(blk)[:, :, :]).then_inc(out_st, 16)
            sp.wait_ge(out_st, 16 * B)

        @block.tensor
        def _(pe):
            def three(out, lhs, rhs, last_of=None):
                n = len(lhs)
                for i, ((ah, al), (bh, bl)) in enumerate(zip(lhs, rhs)):
                    nc.tensor.matmul(out, ah, bh, start=(i == 0), stop=False)
                    nc.tensor.matmul(out, al, bh, start=False, stop=False)
                    last = nc.tensor.matmul(out, ah, bl, start=False, stop=(i == n - 1))
                return last

            def turn(p, b, key, src):
                m = item(p, key)
                p.ring.wait_free(pe, b, m)
                for t in range(NT):
                    last = nc.tensor.transpose(psum[:, p.ring.bank(m), t * P:(t + 1) * P], src(t), ident[:, :])
                p.ring.filled(last, m)

            def beside(p, b, key, c):
                if key == "x":
                    if c == 0:
                        pe.wait_ge(p.xn, b * PER[p.n] + (PER[p.n] + NT))
                    turn(p, b, (key, c), lambda t: xt[:, t, c * P:(c + 1) * P])
                elif key in ("x2", "last_x2"):
                    if c == 0:
                        pe.wait_ge(p.xn, b * 2 * NT + (4 * NT if key == "last_x2" else 2 * NT))
                    turn(p, b, (key, c), lambda t: ot[:, t, c * P:(c + 1) * P])
                else:
                    if c == 0:
                        for k in (NC - 2, NC - 1):
                            p.ring.wait_read(pe, b, item(p, (key.replace("router", "x2"), k)))
                    m = item(p, (key, c))
                    p.ring.wait_free(pe, b, m)
                    for t in (2 * c, 2 * c + 1):
                        last = three(psum[:, p.ring.bank(m), t * NE:(t + 1) * NE], tokens(t),
                                     [(rwh[:, k, :], rwl[:, k, :]) for k in range(NC)])
                    p.ring.filled(last, m)

            def heads(p, b, causal, values):
                def scores(h, t):
                    m = 4 * h + t
                    g = h // HPG
                    if t == 0:
                        pe.wait_ge(p.stack_ld[g % 2], b * 192 + 96 * (g // 2 + 1))
                    p.sq.wait_free(pe, b, m)
                    n = (t + 1) * P if causal else S
                    bank = p.sq.bank(m)
                    st = stack[0:XSTACK, h % NSTK]
                    last = nc.tensor.matmul(psum[:, bank, 0:n], st[:, 0, t * P:(t + 1) * P], st[:, 1, 0:n],
                                            start=True, stop=not causal)
                    if causal:
                        last = nc.tensor.matmul(psum[:, bank, t * P:n], identr[:, :], maskq[:, :],
                                                start=False, stop=True)
                    p.sq.filled(last, m)

                def turn_max(h):
                    m = item(p, ("max", h))
                    p.ring.wait_free(pe, b, m)
                    for t in (2, 3):
                        p.sq.wait_read(pe, b, 4 * h + t)
                    for t in range(NT):
                        last = nc.tensor.transpose(psum[0:1, p.ring.bank(m), t * P:(t + 1) * P],
                                                   nmax[:, h % 4, t:t + 1], ident[:, :])
                    p.ring.filled(last, m)

                def scores_t(h, t):
                    m = 4 * h + t
                    if t == 0:
                        p.ring.wait_read(pe, b, item(p, ("max", h)))
                    if m == 0:
                        pe.wait_ge(p.ones, b + 1)
                    p.sk.wait_free(pe, b, m)
                    lo = t * P if causal else 0
                    bank = p.sk.bank(m)
                    st = stack[0:XSTACK + 1, h % NSTK]
                    last = nc.tensor.matmul(psum[:, bank, lo:S], st[:, 1, t * P:(t + 1) * P], st[:, 0, lo:S],
                                            start=True, stop=not causal)
                    if causal:
                        last = nc.tensor.matmul(psum[:, bank, lo:lo + P], identr[:, :], maskk[:, :],
                                                start=False, stop=True)
                    last.then_inc(p.sk.full[m % 2], 1)

                def pv(h, t):
                    if t == 0:
                        p.o.wait_free(pe, b, h)
                    pe.wait_ge(p.p_lo[t], b * H + (h + 1))
                    lo = t * P if causal else 0
                    out = psum[:, p.o.bank(h), lo:S]
                    at = h * (DH + 1)
                    for n, (v, pr) in enumerate(((vh, ph_), (vl, ph_), (vh, pl_))):
                        last = nc.tensor.matmul(out, v[:, t, at:at + P], pr[:, t, lo:S],
                                                start=(t == 0 and n == 0), stop=(t == NT - 1 and n == 2))
                    if t == NT - 1:
                        p.o.filled(last, h)

                def turn_out(h):
                    m = item(p, ("o", h))
                    p.ring.wait_free(pe, b, m)
                    p.o.wait_read(pe, b, h)
                    for t in range(NT):
                        last = nc.tensor.transpose(psum[:, p.ring.bank(m), t * P:(t + 1) * P],
                                                   ov[:, h % 2, t * P:(t + 1) * P], ident[:, :])
                    p.ring.filled(last, m)

                def turn_qk(g, c):
                    at = (D if c == "k" else 0) + g * P
                    turn(p, b, ("turn", g, c), lambda t: qk[:, t, at:at + P])

                if p.n == 1:
                    pe.wait_ge(p.kn, b * 3 + 3)
                    pe.wait_ge(p.qn, b * (NT + 1) + NT + 1)
                else:
                    pe.wait_ge(p.ra, b * 8 + 10)
                for g in range(2):
                    for c in "kq":
                        turn_qk(g, c)
                    for t in (2 * g, 2 * g + 1):
                        values(t)
                for m in range(LEAD):
                    scores(*divmod(m, NT))
                turn_max(0)
                for t in (2, 3):
                    p.ring.wait_read(pe, b, item(p, ("v", t)))
                for m in range(LAST + 1):
                    if m + LEAD < STEPS_H:
                        scores(*divmod(m + LEAD, NT))
                    if head_max(m) is not None:
                        turn_max(head_max(m))
                    if m < STEPS_H:
                        scores_t(*divmod(m, NT))
                    if 0 <= m - LAG < STEPS_H:
                        pv(*divmod(m - LAG, NT))
                    if head_out(m) is not None:
                        turn_out(head_out(m))
                    if group_turn(m):
                        for c in "kq":
                            turn_qk(group_turn(m), c)
                    if m in BESIDE[p.n]:
                        beside(p, b, *BESIDE[p.n][m])
                for h in (H - 2, H - 1):
                    p.ring.wait_read(pe, b, item(p, ("o", h)))
                for c in range(NC):
                    turn(p, b, ("turn_o", c), lambda t: ot[:, t, c * P:(c + 1) * P])

            def x_by(wat, width, stride):
                return [(wh[:, wat + c * stride:wat + c * stride + width], wl[:, wat + c * stride:wat + c * stride + width])
                        for c in range(NC)]

            def tokens(t):
                return [(xh[:, c, t * P:(t + 1) * P], xl[:, c, t * P:(t + 1) * P]) for c in range(NC)]

            def o_tokens(t):
                return [tuple(o_t(c)[n][:, t * P:(t + 1) * P] for n in range(2)) for c in range(NC)]

            def chans():
                return [(xh[:, c, :], xl[:, c, :]) for c in range(NC)]

            def project(p, b, key, lhs, rhs):
                m = item(p, key)
                p.ring.wait_free(pe, b, m)
                n = rhs[0][0].shape[-1]
                p.ring.filled(three(psum[:, p.ring.bank(m), 0:n], lhs, rhs), m)

            pe.wait_ge(c_ok, 9)
            pe.wait_ge(r_ok, 3)
            pe.wait_ge(v_ld, 17 * 16)
            nc.tensor.transpose(psum[:, 0, 0:38], vrow[0:38, :], ident[0:38, 0:38]).then_inc(vT, 1)
            pe.wait_ge(prep, 1)
            pe.wait_ge(wemb_ld, 32)
            wemb = [t_[:, :, :].rearrange("p a n -> p (a n)")[:, k * 2 * D:(k + 1) * 2 * D]
                    for t_ in (ot, yt) for k in range(2)]
            for m in range(2 * NC):
                for k in range(NC):
                    last = nc.tensor.matmul(psum[:, 1, m * B:(m + 1) * B], wemb[k][:, m * P:(m + 1) * P],
                                            vcol[:, k:16:4], start=(k == 0), stop=(k == NC - 1))
            last.then_inc(mod_mm, 1)

            p = ph[1]
            pe.sem_inc(p.sk.full[1], H)
            pe.wait_ge(p.xn, NT)
            for c in range(NC):
                turn(p, 0, ("x0", c), lambda t: xt[:, t, c * P:(c + 1) * P])
            pe.wait_ge(p.w_lo, len(PIECES[1]))
            with pe.Fori(0, B) as b:
                pe.wait_ge(p.vlo, b * V1 + (2 + NC))
                for t in range(NT):
                    for n, c in enumerate("qk"):
                        project(p, b, ("qk", t, c), tokens(t), x_by(n * D, D, 3 * D))
                for t in range(NT):
                    project(p, b, ("out", t), o_tokens(t), x_by(3 * D * NC, D, D))
                heads(p, b, False, lambda t: project(p, b, ("v", t), tokens(t), x_by(2 * D, D, 3 * D)))
            for c in (NC - 2, NC - 1):
                p.ring.wait_read(pe, B - 1, item(p, ("turn_o", c)))
            for t in range(NT):
                project(p, B - 1, ("last", t), o_tokens(t), x_by(3 * D * NC, D, D))

            p = ph[2]
            pe.sem_inc(p.sk.full[1], H)
            pe.wait_ge(p.xn, NT)
            for c in range(NC):
                turn(p, 0, ("x0", c), lambda t: xt[:, t, c * P:(c + 1) * P])
            pe.wait_ge(p.w_lo, 2)
            kvh, qdh = (wh[:, 6144:6656], wl[:, 6144:6656]), (wh[:, 6656:7168], wl[:, 6656:7168])
            pair = lambda at, n: (wh[:, at:at + n], wl[:, at:at + n])
            cut = lambda xx, t: (xx[0][:, t * P:(t + 1) * P], xx[1][:, t * P:(t + 1) * P])
            for c in (NC - 2, NC - 1):
                p.ring.wait_read(pe, 0, item(p, ("x0", c)))
            with pe.Fori(0, B) as b:
                project(p, b, "kv_d", x_by(W2_D, P, 512), chans())
                project(p, b, "q_d", x_by(W2_D + P, P, 512), chans())
                for key in ("kv_d", "q_d"):
                    p.ring.wait_read(pe, b, item(p, key))
                for t in range(NT):
                    project(p, b, ("qk", t, "q"), [cut(qdh, t)], [pair(W2_Q, 512)])
                    m = item(p, ("qk", t, "k"))
                    p.ring.wait_free(pe, b, m)
                    three(psum[:, p.ring.bank(m), 0:256], [cut(kvh, t)], [pair(W2_KU, 256)])
                    p.ring.filled(three(psum[:, p.ring.bank(m), 256:512], tokens(t), x_by(W2_D + 256, 256, 512)), m)
                pe.wait_ge(p.w_lo, len(PIECES[2]) + 1)
                for t in range(NT):
                    project(p, b, ("out", t), o_tokens(t), x_by(W2_O, D, D))
                heads(p, b, True, lambda t: project(p, b, ("v", t), [cut(kvh, t)], [pair(W2_VU, 512)]))
            for c in (NC - 2, NC - 1):
                p.ring.wait_read(pe, B - 1, item(p, ("turn_o", c)))
            for t in range(NT):
                project(p, B - 1, ("last", t), o_tokens(t), x_by(W2_O, D, D))
            for c in range(NC):
                beside(p, B - 1, "last_x2", c)
            for c in range(2):
                beside(p, B - 1, "last_router", c)

            with pe.Fori(0, NE // 2) as i:
                def gate_up(k):
                    j, blk = divmod(k, B)
                    if blk == 0:
                        pe.wait_ge(ew_lo, i * 6 + 3 * (j + 1))
                    if blk < B - 1 and j == 0:
                        pe.wait_ge(x3_ld[blk], 16)
                    for n in range(NI):
                        for u in range(2):
                            m = 4 * k + 2 * n + u
                            guring.wait_free(pe, i, m)
                            at = u * INNER + n * P
                            last = three(psum[:, guring.bank(m), :],
                                         [(ew[:, j, 0, c, at:at + P], ew[:, j, 1, c, at:at + P]) for c in range(NC)],
                                         [x3_of(blk, c) for c in range(NC)])
                            guring.filled(last, m)

                def down(k):
                    j = k // B
                    pe.wait_ge(h_lo, i * 16 + (2 + 2 * k + 2))
                    for t in range(NT):
                        m = 4 * k + t
                        dring.wait_free(pe, i, m)
                        last = three(psum[:, dring.bank(m), :],
                                     [(hs[:, k % 2, 0, n, t * P:(t + 1) * P], hs[:, k % 2, 1, n, t * P:(t + 1) * P])
                                      for n in range(NI)],
                                     [(ew[:, j, 0, NC + n, :], ew[:, j, 1, NC + n, :]) for n in range(NI)])
                        dring.filled(last, m)

                for k in range(2 * B):
                    gate_up(k)
                    if k:
                        down(k - 1)
                down(2 * B - 1)

        @block.scalar
        def _(act):
            def weights(n):
                p = ph[n]
                for i, (at, cols, _) in enumerate(PIECES[n]):
                    if n == 2 and i == 0:
                        act.wait_ge(p.w_ln, NC)
                    act.wait_ge(p.w_ld[i % 2], 16 * NLOAD[n][i])
                    nc.scalar.activation(wh[:, at:at + cols], stage(i)[:, 0:cols], ACT.Copy).then_inc(p.w_hi, 1)

            def square(p, b, src, first, per, t):
                if first + t:
                    act.wait_ge(p.ss, b * per + (first + t))
                nc.scalar.activation(junk[:, :], src[:, t, :], ACT.Square,
                                     accum_out=sst[:, t:t + 1]).then_inc(p.ss, 1)

            def squares(p, b, src, first, per):
                for t in range(NT):
                    square(p, b, src, first, per, t)

            def hi_of(p, b, key, out):
                m = item(p, key)
                p.ring.wait_full(act, b, m)
                nc.scalar.activation(out, psum[:, p.ring.bank(m), :], ACT.Copy).then_inc(p.hi, 1)

            def hi_of_value(p, b, k, out):
                act.wait_ge(p.v, b * V1 + (k + 1))
                nc.scalar.activation(out, vs[:, k % 2, :], ACT.Copy).then_inc(p.vhi, 1)

            def turn_qk(p, b, g, c):
                at = {"q": 0, "k": 2}[c]
                act.wait_ge(p.split_free, b * NG + (g + 1))
                if p.n == 1 and c == "q":
                    hi_of_value(p, b, NC + g, split[:, at, :])
                else:
                    hi_of(p, b, ("turn", g, c), split[:, at, :])

            def values(p, b, t):
                m = item(p, ("v", t))
                p.ring.wait_full(act, b, m)
                nc.scalar.activation(vh[:, t, 0:H * (DH + 1)].rearrange("p (h d) -> p h d", d=DH + 1)[:, :, 0:DH],
                                     psum[:, p.ring.bank(m), :].rearrange("p (h d) -> p h d", d=DH),
                                     ACT.Copy).then_inc(p.hi, 1)

            def max_row(p, b, h):
                m = item(p, ("max", h))
                p.ring.wait_full(act, b, m)
                p.ring.cleared(nc.scalar.activation(stack[XSTACK:XSTACK + 1, h % NSTK, 0, :],
                                                    psum[0:1, p.ring.bank(m), :], ACT.Copy), m)

            def heads(p, b, causal):
                for g in range(2):
                    for c in "kq":
                        turn_qk(p, b, g, c)
                    for t in (2 * g, 2 * g + 1):
                        values(p, b, t)
                    if p.n == 2 and g == 0:
                        for t in (NT - 2, NT - 1):
                            p.ring.wait_read(act, b, item(p, ("out", t)))
                        squares(p, b, ot, NT, 2 * NT)
                max_row(p, b, 0)
                for m in range(LAST + 1):
                    h, t = divmod(m, NT)
                    if m < STEPS_H:
                        act.wait_ge(p.sk.full[m % 2], b * p.sk.per + (H * (m % 2) + m // 2 + 1))
                        lo = t * P if causal else 0
                        scoresT = psum[:, p.sk.bank(m), lo:S]
                        ins = nc.scalar.activation(probs[:, t, lo:S], scoresT, ACT.Exp, scale=SCALE)
                        if t < NT - 1:
                            ins.then_inc(p.p_x[t], 1)
                            p.sk.cleared(nc.scalar.activation(ph_[:, t, lo:S], scoresT, ACT.Exp, scale=SCALE), m)
                        else:
                            p.sk.cleared(ins, m)
                    if t == 2 and h + 1 < H:
                        max_row(p, b, h + 1)
                    ho = h - (LAG + NT) // NT
                    if t == (NT - 1 + LAG + 1) % NT and 0 <= ho < H:
                        p.o.wait_full(act, b, ho)
                        p.o.cleared(nc.scalar.activation(ov[:, ho % 2, :], psum[:, p.o.bank(ho), :],
                                                         ACT.Copy), ho)
                    if group_turn(m):
                        for c in "kq":
                            turn_qk(p, b, group_turn(m), c)
                    if m == SQUARE_STEP:
                        act.wait_ge(p.x_ld, b * 16 + 32)
                        squares(p, b, xt, PER[p.n], PER[p.n])
                    if m in BESIDE[p.n]:
                        key, c = BESIDE[p.n][m]
                        if p.n == 1:
                            hi_of_value(p, b, NC + NG + c, xh[:, c, :])
                        elif key != "router":
                            if key == "x" and c == 0:
                                act.wait_ge(p.y_free, b + 1)
                            hi_of(p, b, (key, c), xh[:, c, :])
                for c in range(NC):
                    hi_of(p, b, ("turn_o", c), o_t(c)[0])

            act.wait_ge(c_ok, 2)
            nc.scalar.activation(identr[:, :], ident[:, :], ACT.Copy).then_inc(r_ok, 1)
            act.wait_ge(c_ok, 7)
            nc.scalar.activation(maskq[:, :], vs[:, 0, 0:P], ACT.Copy).then_inc(r_ok, 1)
            nc.scalar.activation(maskk[:, :], vs[:, 1, 0:P], ACT.Copy).then_inc(r_ok, 1)
            act.wait_ge(ph[1].x_ld, 16)
            squares(ph[1], 0, xt, 0, NT)
            weights(1)
            p = ph[1]
            act.sem_inc(p.sk.free[0], 1)
            act.sem_inc(p.sk.free[1], 1)
            act.sem_inc(p.o.free[0], 1)
            act.sem_inc(p.o.free[1], 1)
            for k in range(NC):
                hi_of_value(p, 0, k, xh[:, k, :])
            with act.Fori(0, B) as b:
                for t in range(NT):
                    for n, c in enumerate("qk"):
                        m = item(p, ("qk", t, c))
                        p.ring.wait_full(act, b, m)
                        p.ring.cleared(nc.scalar.activation(qk[:, t, n * D:(n + 1) * D],
                                                            psum[:, p.ring.bank(m), :], ACT.Copy), m)
                heads(p, b, causal=False)

            p = ph[2]
            take_over(act, ph[1].sk, p.sk)
            take_over(act, ph[1].o, p.o)
            act.wait_ge(p.x_ld, 16)
            squares(p, 0, xt, 0, 2 * NT)
            weights(2)
            for c in range(NC):
                hi_of(p, 0, ("x0", c), xh[:, c, :])
            act.wait_ge(rw_ok, 1)
            nc.scalar.activation(rwh[:, :, :], rwt[:, :, :], ACT.Copy).then_inc(p.w_hi, 1)
            with act.Fori(0, B) as b:
                hi_of(p, b, "kv_d", wh[:, 6144:6656])
                hi_of(p, b, "q_d", wh[:, 6656:7168])
                for t in range(NT):
                    for n, c in enumerate("qk"):
                        m = item(p, ("qk", t, c))
                        p.ring.wait_full(act, b, m)
                        nc.scalar.activation(
                            qk[:, t, n * D:(n + 1) * D].rearrange("p (h d) -> p h d", d=DH)[:, :, 0:RD],
                            psum[:, p.ring.bank(m), 0:H * RD].rearrange("p (h d) -> p h d", d=RD),
                            ACT.Copy).then_inc(p.head_sq, 1)
                heads(p, b, causal=True)

            def split_expert(e, j, c):
                nc.scalar.activation(ew[:, j, 0, 2 * c:2 * c + 2, :], wstage[:, 2 * c:2 * c + 2, :],
                                     ACT.Copy).then_inc(ew_hi, 1)

            for t in range(NT):
                if t >= 2:
                    act.wait_ge(ew_ln, NC)
                    split_expert(0, 0, t - 2)
                p.ring.wait_read(act, B - 1, item(p, ("last", t)))
                square(p, B - 1, ot, 3 * NT, 2 * NT, t)
            split_expert(0, 0, 2)
            for c in range(NC):
                hi_of(p, B - 1, ("last_x2", c), xh[:, c, :])

            for old, n in ((p.sk, 0), (p.o, 2)):
                for m in range(2):
                    act.wait_ge(old.free[m], B * old.per + 1)
                    act.sem_inc(dring.free[n + m], 1)
            act.wait_ge(p.lg_ok, 2 * B + 2)
            nc.scalar.activation(gtmp[:, 0], logits[:, :, :], ACT.Exp, scale=-1.0).then_inc(g_exp, 1)
            with act.Fori(0, NE // 2) as i:
                for k in range(2 * B):
                    j, blk = divmod(k, B)
                    for n in range(NI):
                        m = 4 * k + 2 * n
                        guring.wait_full(act, i, m)
                        act.wait_ge(h_v, i * 16 + (2 + 2 * k + n - 1))
                        guring.cleared(nc.scalar.activation(sg[:, n, :], psum[:, guring.bank(m), :], ACT.Silu), m)
                    for n in range(NI):
                        act.wait_ge(h_v, i * 16 + (2 + 2 * k + n + 1))
                        nc.scalar.activation(hs[:, k % 2, 0, n, :], hv[:, n, :], ACT.Copy).then_inc(h_hi, 1)
                    if blk:
                        act.wait_ge(ew_ln, i * 2 * NC + NC * (j + 2))
                        split_expert(0, 1 - j, blk - 1)

        @block.gpsimd
        def _(pool):
            nc.gpsimd.memset(ident[:, :], 0.0).then_inc(c_ok, 1)
            pool.wait_ge(c_ok, 1)
            nc.gpsimd.affine_select(out=ident[:, :], in_=ident[:, :], compare_op=ALU.not_equal, fill=1.0, base=0,
                                    pattern=[[-1, P]], channel_multiplier=1).then_inc(c_ok, 1)
            nc.gpsimd.memset(vh[:, :, :].bitcast(F32), 1.0).then_inc(c_ok, 1)
            nc.gpsimd.memset(vl[:, :, :].bitcast(F32), 0.0).then_inc(c_ok, 1)
            nc.gpsimd.memset(vs[:, :, 0:P], 0.0).then_inc(c_ok, 1)
            pool.wait_ge(c_ok, 5)
            nc.gpsimd.affine_select(out=vs[:, 0, 0:P], in_=vs[:, 0, 0:P], compare_op=ALU.is_ge, fill=NEG, base=0,
                                    pattern=[[-1, P]], channel_multiplier=1).then_inc(c_ok, 1)
            nc.gpsimd.affine_select(out=vs[:, 1, 0:P], in_=vs[:, 1, 0:P], compare_op=ALU.is_ge, fill=NEG, base=0,
                                    pattern=[[1, P]], channel_multiplier=-1).then_inc(c_ok, 1)
            pool.wait_ge(c_ok, 7)
            nc.gpsimd.memset(stack[:, 0:NC].bitcast(F32), 0.0).then_inc(c_ok, 1)
            pool.wait_ge(c_ok, 8)
            nc.gpsimd.memset(stack[XSTACK:XSTACK + 1, HPG:, 1, :].bitcast(F32), 1.0).then_inc(c_ok, 1)

            def lo_of_value(p, b, k, hi, out):
                pool.wait_ge(p.vhi, b * V1 + (k + 1))
                nc.gpsimd.tensor_tensor(out, vs[:, k % 2, :], hi.bitcast(F32), ALU.subtract).then_inc(p.vlo, 1)

            def turn_q(p, b, g):
                lo_of_value(p, b, NC + g, split[:, 0, :], split[:, 1, :])

            pool.wait_ge(c_ok, 9)

            def heads(p, b, causal):
                for t in (NT - 2, NT - 1):
                    p.ring.wait_full(pool, b, item(p, ("out", t)))
                    pool.sem_inc(pln, 1)
                pool.wait_ge(*((p.kn, b * 3 + 3) if p.n == 1 else (p.acc_ok, b * NT + NT)))
                pool.sem_inc(pln, 1)
                nc.gpsimd.memset(stack[XSTACK:XSTACK + 1, 0:HPG, 1, :].bitcast(F32), 1.0).then_inc(p.ones, 1)
                pool.wait_ge(p.ones, b + 1)
                for g in range(2):
                    if p.n == 1:
                        turn_q(p, b, g)
                for m in range(STEPS_H):
                    h, t = divmod(m, NT)
                    if t < NT - 1:
                        lo = t * P if causal else 0
                        pool.wait_ge(p.p_x[t], b * H + (h + 1))
                        p.sk.wait_read(pool, b, m)
                        nc.gpsimd.tensor_tensor(pl_[:, t, lo:S], probs[:, t, lo:S], ph_[:, t, lo:S].bitcast(F32),
                                                ALU.subtract).then_inc(p.p_lo[t], 1)
                    if p.n == 1 and group_turn(m):
                        turn_q(p, b, group_turn(m))
                    if p.n == 1 and m in BESIDE[1]:
                        c = BESIDE[1][m][1]
                        lo_of_value(p, b, NC + NG + c, xh[:, c, :], xl[:, c, :])

            p = ph[1]
            pool.sem_inc(p.vlo, 2)
            for c in range(NC):
                lo_of_value(p, 0, c, xh[:, c, :], xl[:, c, :])
            with pool.Fori(0, B) as b:
                for n in range(2 * NT):
                    t, c = divmod(n, 2)
                    p.ring.wait_read(pool, b, item(p, ("qk", t, "qk"[c])))
                    pool.wait_ge(p.head_ss, b * 2 * NT + (n + 1))
                    src = qk[:, t, c * D:(c + 1) * D]
                    nc.gpsimd.tensor_tensor(probs[:, n % 2, :], src, src, ALU.mult).then_inc(p.head_sq, 1)
                pool.wait_ge(p.step, b * STEPS[1] + RSQRT_STEPS)
                for t in range(3):
                    kk = qk[:, t, D:2 * D].rearrange("p (h d) -> p h d", d=DH)
                    r = rsh[:, 0, t * 2 * H + H:(t + 1) * 2 * H].unsqueeze(2).broadcast_to([P, H, DH])
                    nc.gpsimd.tensor_tensor(kk, kk, r, ALU.mult).then_inc(p.kn, 1)
                heads(p, b, False)

            p = ph[2]

            def add_acc(b, key):
                for t in range(NT):
                    p.ring.wait_read(pool, b, item(p, (key, t)))
                    nc.gpsimd.tensor_tensor(yt[:, t, :], yt[:, t, :], ot[:, t, :], ALU.add).then_inc(p.acc_ok, 1)

            pool.wait_ge(ph[1].y_st, 16 * (B + 1))
            with pool.Fori(0, B) as b:
                for n in range(2 * NT):
                    t, c = divmod(n, 2)
                    pool.wait_ge(p.rt, b * 2 * NT + (n + 1))
                    r = lambda a: probs[:, n % 2, a * 256:(a + 1) * 256].rearrange("p (h d) -> p h d", d=RD)
                    nc.gpsimd.tensor_tensor(
                        qk[:, t, c * D:(c + 1) * D].rearrange("p (h d) -> p h d", d=DH)[:, :, RD:DH],
                        r(0), r(1), ALU.add).then_inc(p.ra, 1)
                pool.wait_ge(p.r_ld, b * 48 + 1)
                add_acc(b, "out")
                heads(p, b, True)
            pool.wait_ge(p.r_ld, B * 48 + 1)
            add_acc(B - 1, "last")

            pool.sem_inc(h_lo, 2)

            def split_expert(e, j, c):
                nc.gpsimd.tensor_tensor(ew[:, j, 1, 2 * c:2 * c + 2, :], wstage[:, 2 * c:2 * c + 2, :],
                                        ew[:, j, 0, 2 * c:2 * c + 2, :].bitcast(F32), ALU.subtract).then_inc(ew_lo, 1)

            for c in (1, 2):
                pool.wait_ge(ew_hi, c + 1)
                split_expert(0, 0, c)
            with pool.Fori(0, NE // 2) as i:
                for k in range(2 * B):
                    j, blk = divmod(k, B)
                    for n in range(NI):
                        pool.wait_ge(h_hi, i * 16 + (2 * k + n + 1))
                        nc.gpsimd.tensor_tensor(hs[:, k % 2, 1, n, :], hv[:, n, :], hs[:, k % 2, 0, n, :].bitcast(F32),
                                                ALU.subtract).then_inc(h_lo, 1)
                    if blk:
                        pool.wait_ge(ew_hi, i * 6 + (3 * (j + 1) + blk))
                        split_expert(0, 1 - j, blk - 1)

        @block.vector
        def _(dve):
            class Chain:

                def __init__(self, s, base=None, per=0):
                    self.s, self.base, self.per, self.n = s, base, per, 0

                def __call__(self, ins):
                    self.n += 1
                    ins.then_inc(self.s, 1)
                    v = self.n if self.base is None else self.base * self.per + self.n
                    dve.wait_ge(self.s, v)

            V = nc.vector

            def rsqrt(link, x, y, t, mean, eps):
                link(V.tensor_scalar(x, x, mean, eps, ALU.mult, ALU.add))
                link(V.tensor_scalar(y.bitcast(I32), x.bitcast(I32), 1, None, ALU.logical_shift_right))
                link(V.tensor_scalar(y.bitcast(I32), y.bitcast(I32), -1, MAGIC, ALU.mult, ALU.add))
                for _ in range(3):
                    link(V.scalar_tensor_tensor(out=t, in0=y, scalar=-0.5, in1=y, op0=ALU.mult, op1=ALU.mult))
                    link(V.tensor_tensor(t, t, x, ALU.mult))
                    link(V.scalar_tensor_tensor(out=y, in0=t, scalar=1.5, in1=y, op0=ALU.add, op1=ALU.mult))

            def normalize(p, b, link, eps, dst, src, nth, per):
                dve.wait_ge(p.ss, b * per + NT * (nth + 1))
                rsqrt(link, sst[:, :], rst[:, 0, :], rst[:, 1, :], 1.0 / D, eps)
                for t in range(NT):
                    V.tensor_scalar(dst[:, t, :], src[:, t, :], rst[:, 0, t:t + 1], None, ALU.mult).then_inc(p.xn, 1)

            def lo_of(p, b, key, hi, out):
                m = item(p, key)
                dve.wait_ge(p.hi, b * HI[p.n] + (hi_no[p.n][key] + 1))
                p.ring.cleared(V.tensor_tensor(out, psum[:, p.ring.bank(m), :], hi.bitcast(F32), ALU.subtract), m)

            def value(p, b, k, key, s1, s2):
                m = item(p, key)
                p.ring.wait_full(dve, b, m)
                dve.wait_ge(p.vlo, b * V1 + (k + 1))
                if s2 is None:
                    V.tensor_scalar(vs[:, k % 2, :], psum[:, p.ring.bank(m), :], s1, None, ALU.mult).then_inc(p.v, 1)
                else:
                    V.tensor_scalar(vs[:, k % 2, :], psum[:, p.ring.bank(m), :], s1, s2, ALU.mult, ALU.add)\
                        .then_inc(p.v, 1)
                dve.wait_ge(p.v, b * V1 + (k + 1))
                dve.sem_inc(p.ring.free[m % 2], 1)

            def turn_qk(p, b, g, c):
                if p.n == 1 and c == "q":
                    value(p, b, NC + g, ("turn", g, c), gqk[:, 0:1], None)
                else:
                    at = {"q": 0, "k": 2}[c]
                    lo_of(p, b, ("turn", g, c), split[:, at, :], split[:, at + 1, :])

            def route(p, b, key, n, out):
                m = item(p, key)
                p.ring.wait_full(dve, b, m)
                V.tensor_tensor(out, psum[:, p.ring.bank(m), 2 * n * NE:(2 * n + 2) * NE].rearrange("p (t e) -> p t e", e=NE),
                                rb[:, :].unsqueeze(1).broadcast_to([P, 2, NE]), ALU.add).then_inc(p.lg_ok, 1)
                dve.wait_ge(p.lg_ok, b * 2 + ((2 if key[0] == "last_router" else 0) + n + 1))
                dve.sem_inc(p.ring.free[m % 2], 1)

            def heads(p, b, link, causal):
                def maximum(h, t):
                    m = 4 * h + t
                    p.sq.wait_full(dve, b, m)
                    n = (t + 1) * P if causal else S
                    p.sq.cleared(V.tensor_reduce(nmax[:, h % 4, t:t + 1], psum[:, p.sq.bank(m), 0:n], AX.X,
                                                 ALU.max, negate=True), m)

                def output(h):
                    m = item(p, ("o", h))
                    p.ring.wait_full(dve, b, m)
                    o = psum[:, p.ring.bank(m), :].rearrange("p (t d) -> p t d", d=P)
                    r = rden[:, h % 2, :]
                    link(V.reciprocal(r, o[:, :, DH]))
                    p.ring.cleared(V.tensor_tensor(ot[:, :, h * DH:(h + 1) * DH], o[:, :, 0:DH],
                                                   r.unsqueeze(2).broadcast_to([P, NT, DH]), ALU.mult), m)

                def split_last(h):
                    t = NT - 1
                    lo = t * P if causal else 0
                    p.sk.wait_read(dve, b, 4 * h + t)
                    V.tensor_copy(ph_[:, t, lo:S], probs[:, t, lo:S]).then_inc(p.p_hi, 1)
                    dve.wait_ge(p.p_hi, b * H + (h + 1))
                    V.tensor_tensor(pl_[:, t, lo:S], probs[:, t, lo:S], ph_[:, t, lo:S].bitcast(F32),
                                    ALU.subtract).then_inc(p.p_lo[t], 1)

                for g in range(2):
                    for c in "kq":
                        turn_qk(p, b, g, c)
                    for t in (2 * g, 2 * g + 1):
                        m = item(p, ("v", t))
                        heads_of = lambda v: v[:, t, 0:H * (DH + 1)].rearrange("p (h d) -> p h d", d=DH + 1)[:, :, 0:DH]
                        dve.wait_ge(p.hi, b * HI[p.n] + (hi_no[p.n][("v", t)] + 1))
                        p.ring.cleared(V.tensor_tensor(
                            heads_of(vl), psum[:, p.ring.bank(m), :].rearrange("p (h d) -> p h d", d=DH),
                            heads_of(vh).bitcast(F32), ALU.subtract), m)
                for m in range(LEAD):
                    maximum(*divmod(m, NT))
                for m in range(LAST + 2):
                    if m + LEAD < STEPS_H:
                        maximum(*divmod(m + LEAD, NT))
                    if m % NT == 0 and 0 < m <= STEPS_H:
                        split_last(m // NT - 1)
                    if m and head_out(m - 1) is not None:
                        output(head_out(m - 1))
                    if group_turn(m):
                        for c in "kq":
                            turn_qk(p, b, group_turn(m), c)
                    if p.n == 2 and m == 0:
                        dve.wait_ge(p.acc_ok, b * NT + NT)
                        normalize(p, b, link, EPS_FFN, ot, ot, 1, 2 * NT)
                    if p.n == 1 and m == NORM_STEP:
                        link(V.tensor_copy(mod[:, :], modall[:, bass.ds(b + 1, 1), :].rearrange("p a m -> p (a m)")))
                    if m == NORM_STEP:
                        normalize(p, b, link, EPS[p.n], xt, xt, p.n, PER[p.n])
                    if m in BESIDE[p.n]:
                        key, c = BESIDE[p.n][m]
                        if p.n == 1:
                            value(p, b, NC + NG + c, ("x", c), mod[:, c:c + 1], mod[:, NC + c:NC + c + 1])
                        elif key != "router":
                            lo_of(p, b, (key, c), xh[:, c, :], xl[:, c, :])
                        else:
                            route(p, b, (key, c), c, lg[:, 2 * c:2 * c + 2, :])
                for c in range(NC):
                    lo_of(p, b, ("turn_o", c), *o_t(c))

            link = Chain(prep)
            dve.wait_ge(vT, 1)
            link(V.tensor_copy(vcol[:, :], psum[:, 0, 0:38]))
            normalize(ph[1], 0, link, EPS_COND, xt, xt, 0, NT)
            dve.wait_ge(v_ld, 17 * 16)
            link(V.tensor_tensor(gqk[:, :], vcol[:, 36:37], vcol[:, 37:38], ALU.mult))
            link(V.memset(rwt[:, :, NR:NE], 0.0))
            link(V.memset(rb[:, NR:NE], 0.0))
            dve.wait_ge(mod_mm, 1)
            for m in range(2 * NC):
                link(V.tensor_scalar(modall[:, 0:B, m], psum[:, 1, m * B:(m + 1) * B], vcol[:, 16 + m:17 + m], None, ALU.add))
            for m in range(NC):
                link(V.tensor_scalar(modall[:, 0:B, m], modall[:, 0:B, m], 1.0, vcol[:, 24 + m:25 + m], ALU.add, ALU.mult))
            link(V.tensor_copy(modall[:, B, :], modall[:, 0, :]))

            def weights(n, pieces):
                p = ph[n]
                for i in pieces:
                    at, cols, _ = PIECES[n][i]
                    dve.wait_ge(p.w_hi, i + 1)
                    V.tensor_tensor(wl[:, at:at + cols], stage(i)[:, 0:cols], wh[:, at:at + cols].bitcast(F32),
                                    ALU.subtract).then_inc(p.w_lo, 1)

            weights(1, range(len(PIECES[1])))
            p = ph[1]
            for r in (p.ring, p.sq):
                for n in range(2):
                    dve.sem_inc(r.free[n], 1)
            dve.sem_inc(p.head_ss, 2)
            dve.wait_ge(r_ok, 3)
            for c in range(NC):
                value(p, 0, c, ("x0", c), modall[:, 0, c:c + 1], modall[:, 0, NC + c:NC + c + 1])
            with dve.Fori(0, B) as b:
                link = Chain(p.step, b, STEPS[1])
                for n in range(2 * NT):
                    t, c = divmod(n, 2)
                    dve.wait_ge(p.head_sq, b * 2 * NT + (n + 1))
                    V.tensor_reduce(ssh[:, t, c * H:(c + 1) * H], probs[:, n % 2, :].rearrange("p (h d) -> p h d", d=DH),
                                    AX.X, ALU.add).then_inc(p.head_ss, 1)
                dve.wait_ge(p.head_ss, b * 2 * NT + (2 * NT + 2))
                rsqrt(link, ssh[:, :, :].rearrange("p t h -> p (t h)"), rsh[:, 0, :], rsh[:, 1, :], 1.0 / DH, EPS_COND)

                def y(t, i, key):
                    m = item(p, (key, t))
                    p.ring.wait_full(dve, i, m)
                    p.ring.cleared(V.tensor_tensor(yt[:, t, :], psum[:, p.ring.bank(m), :], ot[:, t, :], ALU.add), m)

                def normalize_heads(t, c):
                    x = qk[:, t, c * D:(c + 1) * D].rearrange("p (h d) -> p h d", d=DH)
                    r = rsh[:, 0, (2 * t + c) * H:(2 * t + c + 1) * H].unsqueeze(2).broadcast_to([P, H, DH])
                    V.tensor_tensor(x, x, r, ALU.mult).then_inc(p.qn, 1)

                dve.wait_ge(p.y_free, b + 1)
                y(0, b, "out")
                normalize_heads(0, 0)
                normalize_heads(1, 0)
                y(1, b, "out")
                normalize_heads(2, 0)
                normalize_heads(3, 0)
                normalize_heads(3, 1)
                y(2, b, "out")
                y(3, b, "out")
                heads(p, b, link, causal=False)
                assert link.n == STEPS[1]
            once = Chain(prep2)
            dve.wait_ge(ph[2].w_ld[0], 16 * NLOAD[2][0])
            for c in range(NC):
                w = stage(0)[:, c * 512:(c + 1) * 512]
                V.tensor_scalar(w, w, vcol[:, 28 + c:29 + c], None, ALU.mult).then_inc(ph[2].w_ln, 1)
            dve.wait_ge(p.y_free, B + 1)
            y(0, B - 1, "last")
            y(1, B - 1, "last")
            weights(2, [0])
            y(2, B - 1, "last")
            normalize(ph[2], 0, once, EPS_FFN, xt, xt, 0, 2 * NT)
            y(3, B - 1, "last")
            weights(2, [1])
            p = ph[2]
            take_over(dve, ph[1].ring, p.ring)
            take_over(dve, ph[1].sq, p.sq)
            dve.sem_inc(p.ra, 2)
            for c in range(NC):
                lo_of(p, 0, ("x0", c), xh[:, c, :], xl[:, c, :])
            for c in range(NC):
                ins = V.tensor_scalar(rwt[:, c, :], rwt[:, c, :], vcol[:, 32 + c:33 + c], None, ALU.mult)
            ins.then_inc(rw_ok, 1)
            weights(2, [2])
            dve.wait_ge(p.w_hi, len(PIECES[2]) + 1)
            V.tensor_tensor(rwl[:, :, :], rwt[:, :, :], rwh[:, :, :].bitcast(F32), ALU.subtract).then_inc(p.w_lo, 1)

            def add_h(t, b, key):
                m = item(p, (key, t))
                p.ring.wait_full(dve, b, m)
                p.ring.cleared(V.tensor_tensor(ot[:, t, :], psum[:, p.ring.bank(m), :], resid(t), ALU.add), m)

            def scale_expert():
                for c in range(NC):
                    V.tensor_scalar(wstage[:, c, :], wstage[:, c, :], vcol[:, 32 + c:33 + c], None,
                                    ALU.mult).then_inc(ew_ln, 1)

            with dve.Fori(0, B) as b:
                link = Chain(p.step, b, STEPS[2])
                lo_of(p, b, "kv_d", wh[:, 6144:6656], wl[:, 6144:6656])
                lo_of(p, b, "q_d", wh[:, 6656:7168], wl[:, 6656:7168])
                for n in range(2 * NT):
                    t, c = divmod(n, 2)
                    m = item(p, ("qk", t, "qk"[c]))
                    dve.wait_ge(p.head_sq, b * 2 * NT + (n + 1))
                    dve.wait_ge(p.ra, b * 2 * NT + (n + 1))
                    x = psum[:, p.ring.bank(m), 256:512].rearrange("p (h d) -> p h d", d=RD)
                    t1 = probs[:, n % 2, 0:256].rearrange("p (h d) -> p h d", d=RD)
                    t2 = probs[:, n % 2, 256:512].rearrange("p (h d) -> p h d", d=RD)
                    wide = lambda a, w: a.unsqueeze(1).broadcast_to([P, H, w])
                    V.tensor_tensor(t1, x, wide(rope[:, 0, t, :], RD), ALU.mult)
                    V.tensor_tensor(t2[:, :, 0:RD // 2], x[:, :, RD // 2:RD], wide(rope[:, 1, t, 0:RD // 2], RD // 2), ALU.mult)
                    V.tensor_tensor(t2[:, :, RD // 2:RD], x[:, :, 0:RD // 2], wide(rope[:, 1, t, RD // 2:RD], RD // 2),
                                    ALU.mult).then_inc(p.rt, 1)
                    dve.wait_ge(p.rt, b * 2 * NT + (n + 1))
                    dve.sem_inc(p.ring.free[m % 2], 1)
                dve.wait_ge(p.r_ld, b * 48 + 1)
                for t in range(NT):
                    add_h(t, b, "out")
                heads(p, b, link, causal=True)
                assert link.n == STEPS[2]
            dve.wait_ge(p.r_ld, B * 48 + 1)
            add_h(0, B - 1, "last")
            add_h(1, B - 1, "last")
            dve.wait_ge(ew_ld, 48)
            scale_expert()
            add_h(2, B - 1, "last")
            add_h(3, B - 1, "last")
            dve.wait_ge(ew_hi, 1)
            V.tensor_tensor(ew[:, 0, 1, 0:2, :], wstage[:, 0:2, :], ew[:, 0, 0, 0:2, :].bitcast(F32),
                            ALU.subtract).then_inc(ew_lo, 1)
            dve.wait_ge(p.acc_ok, B * NT + NT)
            normalize(p, B - 1, once, EPS_FFN, ot, ot, 3, 2 * NT)
            for c in range(NC):
                lo_of(p, B - 1, ("last_x2", c), xh[:, c, :], xl[:, c, :])
            for n in range(2):
                route(p, B - 1, ("last_router", n), n, logits[:, (B - 1) * NT + 2 * n:(B - 1) * NT + 2 * n + 2, :])

            dve.sem_inc(h_v, 2)
            for n in range(2):
                dve.sem_inc(guring.free[n], 1)
                dve.wait_ge(p.sq.free[n], B * p.sq.per + 1)
                dve.sem_inc(guring.free[2 + n], 1)
            link = Chain(g_step)
            prob, rank, cmp, gg = gtmp[:, 1], gtmp[:, 2], gtmp[:, 3], gtmp[:, 4]
            dve.wait_ge(g_exp, 1)
            link(V.tensor_scalar(gtmp[:, 0], gtmp[:, 0], 1.0, None, ALU.add))
            link(V.reciprocal(prob, gtmp[:, 0]))
            link(V.memset(rank, 0.0))
            for j in range(NR):
                for lo, hi, op in ((0, j, ALU.is_gt), (j + 1, NR, ALU.is_ge)):
                    if lo < hi:
                        pj = prob[:, :, j:j + 1].broadcast_to([P, B * NT, hi - lo])
                        link(V.tensor_tensor(cmp[:, :, lo:hi], pj, prob[:, :, lo:hi], op))
                        link(V.tensor_tensor(rank[:, :, lo:hi], rank[:, :, lo:hi], cmp[:, :, lo:hi], ALU.add))
            link(V.tensor_scalar(cmp[:, :, 0:NR], rank[:, :, 0:NR], 2.0, None, ALU.is_lt))
            link(V.tensor_tensor(gg[:, :, 0:NR], prob[:, :, 0:NR], cmp[:, :, 0:NR], ALU.mult))
            link(V.tensor_reduce(gden[:, 0, :], gg[:, :, 0:NR], AX.X, ALU.add))
            link(V.reciprocal(gden[:, 1, :], gden[:, 0, :]))
            link(V.memset(w8[:, 0, :], 1.0 / SCALING))
            for e in range(NR):
                link(V.scalar_tensor_tensor(out=w8[:, 1 + e, :], in0=gg[:, :, e], scalar=1.0 / SCALING,
                                            in1=gden[:, 1, :], op0=ALU.mult, op1=ALU.mult))
            with dve.Fori(0, NE // 2) as i:
                def combine(k):
                    j, blk = divmod(k, B)
                    if blk < B - 1 and j == 0:
                        dve.wait_ge(acc_ld[blk], 16)
                    for t in range(NT):
                        m = 4 * k + t
                        a = acc_of(blk)[:, t, :]
                        dring.wait_full(dve, i, m)
                        dring.cleared(V.scalar_tensor_tensor(out=a, in0=psum[:, dring.bank(m), :],
                                                             scalar=wcur[:, j, blk * NT + t:blk * NT + t + 1], in1=a,
                                                             op0=ALU.mult, op1=ALU.add), m)

                for k in range(2 * B):
                    j, blk = divmod(k, B)
                    if blk == 0:
                        V.tensor_copy(wcur[:, j, :], w8[:, bass.ds(i * 2 + j, 1), :].rearrange("p a t -> p (a t)"))\
                            .then_inc(w_cur, 1)
                        dve.wait_ge(w_cur, i * 2 + (j + 1))
                        dve.wait_ge(ew_ld, i * 96 + 48 * (j + 2))
                        scale_expert()
                    for n in range(NI):
                        m = 4 * k + 2 * n + 1
                        guring.wait_full(dve, i, m)
                        guring.wait_read(dve, i, m - 1)
                        dve.wait_ge(h_lo, i * 16 + (2 * k + n + 1))
                        V.tensor_tensor(hv[:, n, :], psum[:, guring.bank(m), :], sg[:, n, :], ALU.mult).then_inc(h_v, 1)
                        dve.wait_ge(h_v, i * 16 + (2 + 2 * k + n + 1))
                        dve.sem_inc(guring.free[m % 4], 1)
                    if k:
                        combine(k - 1)
                combine(2 * B - 1)


_INS = ['x', 'cond_2048', 'L0_cond_W_emb', 'L0_cond_b_emb', 'L0_cond_g_norm', 'L0_cond_W_qkv', 'L0_cond_g_q',
        'L0_cond_g_k', 'L0_cond_W_out', 'L0_ffn_ln1_w', 'L0_ffn_ln2_w', 'L0_ffn_kv_d_w', 'L0_ffn_q_d_w',
        'L0_ffn_k_u_w', 'L0_ffn_v_u_w', 'L0_ffn_q_u_w', 'L0_ffn_rope_k_w', 'L0_ffn_rope_q_w', 'L0_ffn_o_w',
        'gate', 'up', 'down', 'L0_ffn_router_w', 'L0_ffn_router_b', 'rope_cos', 'rope_sin']


def rope_tables():
    half = RD // 2
    freq = (1.0 / np.float32(10000.0) ** (np.arange(0, RD, 2, dtype=np.float32) / np.float32(RD))).astype(np.float32)
    ang = np.outer(np.arange(S, dtype=np.float32), freq).astype(np.float32)
    cos, sin = np.cos(ang), np.sin(ang)
    return (np.concatenate([cos, cos], 1).astype(np.float32), np.concatenate([-sin, sin], 1).astype(np.float32))


def kernel(**inputs):
    import concourse.bacc as bacc
    from concourse.bass_utils import run_bass_kernel_spmd as run

    data = dict(inputs)
    for name in ("gate", "up", "down"):
        shared = np.asarray(inputs[f"L0_ffn_sh_{name}"])[None]
        data[name] = np.concatenate([shared, np.asarray(inputs[f"L0_ffn_r_{name}"])], axis=0)
    data["rope_cos"], data["rope_sin"] = rope_tables()

    nc = bacc.Bacc("TRN2", target_bir_lowering=False, num_devices=1,
                   dynamic_dma_scratch_size=1024)
    arrays, args = {}, []
    for name in _INS:
        a = np.ascontiguousarray(data[name])
        arrays[f"in_{name}_dram"] = a
        args.append(nc.dram_tensor(f"in_{name}_dram", a.shape, mybir.dt.from_np(a.dtype), kind="ExternalInput").ap())
    args.append(nc.dram_tensor("out_dram", (B, S, D), F32, kind="ExternalOutput").ap())
    build(nc, *args)
    r = run(nc, [arrays], core_ids=[0])
    return r.results[0]["out_dram"]
```

```python
from contextlib import ExitStack

import numpy as np

import concourse.bass as bass
from concourse import mybir

F32 = mybir.dt.float32
F32R = mybir.dt.float32r
I32 = mybir.dt.int32
ALU = mybir.AluOpType
ACT = mybir.ActivationFunctionType
AX = mybir.AxisListType

P = 128
B, S, D = 4, 512, 512
NT, NC = S // P, D // P
H, DH = 16, 32
RD = DH // 2
LAT = 128
INNER = 256
NE, NR = 8, 7
NI = INNER // P
HPG, NG = P // DH, H * DH // P
SCALE = float(DH) ** -0.5
SCALING = 8.0
EPS_COND, EPS_FFN = 1e-6, 1e-5
EPS = {1: EPS_COND, 2: EPS_FFN}
NEG = -1e30
MAGIC = 0x5F3759DF
RSQRT_STEPS = 12
XSTACK = 3 * DH
NSTK = 8

STEPS_H = H * NT
LEAD = 2 * NT
LAG = 4
NP = LAG + 1
NX = 4
VH = 2 * DH + 1
VW = H * VH + P - VH


def hi_by_dve(n, m):
    return m % NT == NT - 1 or n == 1 and m % (2 * NT) == 2 * NT - 2


def head_max(m):
    return m // NT + 1 if m % NT == 1 and m // NT + 1 < H else None


def head_out(m):
    h = (m - NT + 1 - LAG - 3) // NT
    return h if (m - NT + 1 - LAG - 3) % NT == 0 and 0 <= h < H else None


def group_turn(m):
    g = m // (4 * NT) + 2
    return g if m % (4 * NT) == 3 * NT - 1 and g < NG else None


LAST = NT - 1 + LAG + 3 + NT * (H - 1)

SQUARE_STEP, NORM_STEP = 30, 33
BESIDE = {
    1: {43 + 4 * c: ("x", c) for c in range(NC)},
    2: {43 + 4 * c: ("x", c) for c in range(NC)} | {m: ("x2", c) for c, m in enumerate((3, 4, 7, 8))}
    | {m: ("router", n) for n, m in enumerate((12, 15))},
}
_OUT = [("out", t) for t in range(NT)]
_V = [("v", t) for t in range(NT)]
_TURN = [[("turn", g, "k"), ("turn", g, "q")] for g in range(2)]
FIRST = {1: _OUT[:3] + _TURN[0] + _OUT[3:] + _V + _TURN[1], 2: _OUT[:1] + _TURN[0] + _OUT[1:] + _V + _TURN[1]}

_HEADS = {n: [("max", 0)] + [
    x for m in range(LAST + 1) for x in
    ([("max", head_max(m))] if head_max(m) is not None else [])
    + ([("o", head_out(m))] if head_out(m) is not None else [])
    + ([("turn", group_turn(m), "k"), ("turn", group_turn(m), "q")] if group_turn(m) else [])
    + ([BESIDE[n][m]] if m in BESIDE[n] else [])] for n in (1, 2)}
_TURN_O = [("turn_o", c) for c in range(NC)]
_X0 = [("x0", c) for c in range(NC)]
_QK = [("qk", t, c) for t in range(NT) for c in "qk"]
BEFORE = {1: _X0, 2: _X0}
BODY = {
    1: _QK + FIRST[1] + _HEADS[1] + _TURN_O,
    2: ["kv_d", "q_d"] + _QK + FIRST[2] + _HEADS[2] + _TURN_O,
}
AFTER = {
    1: [("last", t) for t in range(NT)],
    2: [("last", t) for t in range(NT)] + [("last_x2", c) for c in range(NC)] + [("last_router", n) for n in range(2)],
}
ITEMS = {n: BEFORE[n] + BODY[n] + AFTER[n] for n in (1, 2)}
assert all(len(x[n]) % 2 == 0 for x in (BEFORE, BODY, AFTER) for n in (1, 2))


class Ring:

    def __init__(self, name, sem, banks, per_loop, outside=0):
        self.banks, self.n = banks, len(banks)
        self.per = per_loop // self.n
        self.extra = outside // self.n
        self.full = [sem(f"{name}_full{i}") for i in range(self.n)]
        self.free = [sem(f"{name}_free{i}") for i in range(self.n)]

    def bank(self, m):
        return self.banks[m % self.n]

    def wait_free(self, eng, i, m):
        eng.wait_ge(self.free[m % self.n], i * self.per + (m // self.n + 1))

    def wait_full(self, eng, i, m):
        eng.wait_ge(self.full[m % self.n], i * self.per + (m // self.n + 1))

    def wait_read(self, eng, i, m):
        eng.wait_ge(self.free[m % self.n], i * self.per + (m // self.n + 2))

    def filled(self, ins, m):
        ins.then_inc(self.full[m % self.n], 1)

    def cleared(self, ins, m):
        ins.then_inc(self.free[m % self.n], 1)


def build(nc, x_d, cond_d, wemb_d, bemb_d, gnorm_d, wqkv_d, gq_d, gk_d, wout_d, ln1_d, ln2_d, kvd_d,
          qd_d, ku_d, vu_d, qu_d, rk_d, rq_d, ow_d, gate_d, up_d, down_d, rw_d, rb_d, cos_d, sin_d,
          out_d):
    dram = lambda name, shape: nc.dram_tensor(name, shape, F32, kind="Internal").ap()
    x1_s = dram("x1_s", (B, P, NT, D))
    acc_s = dram("acc_s", (B, P, NT, D))
    xt_s = dram("xt_s", (B, P, 2, NC, S))
    split_s = dram("split_s", (2, P, 4, S))

    with ExitStack() as ctx:
        sem = lambda name: ctx.enter_context(nc.semaphore(name))
        keep = lambda name, shape, dt=F32: ctx.enter_context(nc.sbuf_tensor(name, shape, dt))
        psum = ctx.enter_context(nc.psum_tensor("psum", [P, 8, 512], F32))

        ident = keep("ident", [P, P])
        identr = keep("identr", [P, P], F32R)
        fold = keep("fold", [P, DH + 1])
        vcol = keep("vcol", [P, 38])
        logits = keep("logits", [P, B * NT, NE])
        xh = keep("xh", [P, NC, S], F32R)
        xl = keep("xl", [P, NC, S], F32R)
        yt = keep("yt", [P, NT, D])

        room = ExitStack()
        sb = lambda name, shape, dt=F32: room.enter_context(nc.sbuf_tensor(name, shape, dt))
        wh = sb("wh", [P, 8192], F32R)
        wl = sb("wl", [P, 8192], F32R)
        split = sb("split", [P, 4, S], F32R)
        stack = sb("stack", [P, NSTK, 2, S], F32R)
        vs = sb("vs", [P, 2, S])
        qk = sb("qk", [P, NT, 2 * D])
        vals = sb("vals", [P, NT, VW], F32R)
        probs = sb("probs", [P, NX, S])
        ph_ = sb("probs_hi", [P, NP, S], F32R)
        pl_ = sb("probs_lo", [P, NP, S], F32R)
        ov = sb("ov", [P, 2, S])
        vrow = ov[:, 0, 0:P]
        xt = sb("xt", [P, NT, D])
        ot = sb("ot", [P, NT, D])
        mask = sb("mask", [P, P], F32R)
        rope = sb("rope", [P, 2, NT, RD])
        modall = sb("modall", [P, B + 1, 2 * NC])
        mod = sb("mod", [P, 2 * NC])
        gqk = sb("gqk", [P, 1])
        junk = sb("junk", [P, S])
        sst = sb("sst", [P, NT])
        rst = sb("rst", [P, 2, NT])
        ssh = sb("ssh", [P, NT, 2 * H])
        rsh = sb("rsh", [P, 2, NT * 2 * H])
        nmax = sb("nmax", [P, 4, NT])
        rden = sb("rden", [P, 2, NT])
        rwt = sb("rwt", [P, NC, NE])
        rwh = sb("rwh", [P, NC, NE], F32R)
        rwl = sb("rwl", [P, NC, NE], F32R)
        rb = sb("rb", [P, NE])
        lg = sb("lg", [P, NT, NE])
        room.close()

        room3 = ctx.enter_context(ExitStack())
        sb = lambda name, shape, dt=F32: room3.enter_context(nc.sbuf_tensor(name, shape, dt))
        x3 = sb("x3", [P, B - 1, 2, NC, S], F32R)
        acc = sb("acc", [P, B - 1, NT, D])
        wstage = sb("wstage", [P, NC + NI, 512])
        sg = sb("sg", [P, NI, S])
        hs = sb("hs", [P, 2, 2, NI, S], F32R)
        ew = sb("ew", [P, 2, 2, NC + NI, 512], F32R)
        hv = sb("hv", [P, NI, S])
        w8 = sb("w8", [P, NE, B * NT])
        wcur = sb("wcur", [P, 2, B * NT])
        gtmp = sb("gtmp", [P, 6, B * NT, NE])
        gden = sb("gden", [P, 2, B * NT])

        v_ld, v2_ld = sem("vectors_loaded"), sem("small_tables_loaded")
        c_ok = sem("constants_ready")
        prep, prep2 = sem("vector_prep_steps"), sem("dve_steps_between_loops")
        vT = sem("vectors_turned")
        wemb_ld = sem("w_emb_loaded")
        mod_mm = sem("modulation_product")
        spn, pln, pen = sem("sp_waits_passed"), sem("pool_waits_passed"), sem("pe_waits_passed")
        r_ok = sem("rounded_constants_ready")
        rw_ok = sem("router_weights_scaled")
        x3_ld = [sem(f"x3_loaded{blk}") for blk in range(B - 1)]
        acc_ld = [sem(f"acc_loaded{blk}") for blk in range(B - 1)]
        ew_ld, ew_ln, ew_hi, ew_lo = (sem(f"expert_{x}") for x in ("loaded", "scaled", "hi", "lo"))
        h_v, h_hi, h_lo = (sem(f"hidden_{x}") for x in ("ready", "hi", "lo"))
        w_cur = sem("expert_token_weights")
        g_exp, g_step = sem("router_exp"), sem("router_steps")
        out_st = sem("out_stored")
        guring = Ring("gate_up", sem, (0, 1, 2, 3), 2 * B * 4)
        dring = Ring("down", sem, (4, 5, 6, 7), 2 * B * 4)

        class Phase:
            pass

        ph = {}
        for n in (1, 2):
            p = ph[n] = Phase()
            s = lambda name, n=n: sem(f"{name}_{n}")
            p.n = n
            p.items = {k: i for i, k in enumerate(ITEMS[n])}
            p.ring = Ring(f"ring{n}", sem, (0, 1), len(BODY[n]), len(BEFORE[n]) + len(AFTER[n]))
            p.sq = Ring(f"scores{n}", sem, (2, 3), H * NT)
            p.sk = Ring(f"scoresT{n}", sem, (4, 5), H * NT)
            p.o = Ring(f"pv{n}", sem, (6, 7), H)
            p.w_ld = [s("weights_loaded_even"), s("weights_loaded_odd"), s("weights_loaded_apart")]
            p.w_lo_pool = s("weights_lo_by_pool")
            p.w_hi, p.w_lo, p.w_ln = s("weights_hi"), s("weights_lo"), s("weights_scaled")
            p.x_ld, p.xn, p.ss = s("x_loaded"), s("x_normalized"), s("token_squares")
            p.step = s("dve_steps")
            p.hi = s("hi_of_psum")
            p.v, p.vhi, p.vlo = s("value_ready"), s("value_hi"), s("value_lo")
            p.head_sq, p.head_ss = s("head_squares"), s("head_square_sums")
            p.qn, p.kn = s("q_normalized"), s("k_normalized")
            p.p_x = [s(f"probs_ready{t}") for t in range(NT - 1)]
            p.p_hi = s("probs_hi_by_dve")
            p.p_lo = [s(f"probs_lo{t}") for t in range(NT)]
            p.rt, p.ra = s("rotary_terms"), s("rotary_added")
            p.split_st, p.split_free = s("split_stored"), s("split_free")
            p.stack_ld = [s("stack_loaded_even"), s("stack_loaded_odd")]
            p.y_st, p.y_free = s("y_stored"), s("y_free")
            p.ones = s("ones_rows_set")
            p.acc_ok = s("acc_ready")
            p.r_ld = s("residual_inputs_loaded")
            p.lg_ok = s("logits_ready")
        V1 = NC + NG

        def item(p, key):
            return p.items[key]

        HI_ORDER = {
            1: [k for k in ITEMS[1] if k[0] in ("turn", "v", "turn_o") and k[-1] != "q"],
            2: [k for k in ITEMS[2] if k in ("kv_d", "q_d") or k[0] in ("x0", "x", "turn", "v", "turn_o", "x2", "last_x2")],
        }
        HI = {n: sum(k in BODY[n] for k in x) for n, x in HI_ORDER.items()}
        hi_no = {n: {k: i for i, k in enumerate(x)} for n, x in HI_ORDER.items()}
        STEPS = {1: 1 + 2 * RSQRT_STEPS + H, 2: 2 * RSQRT_STEPS + H}
        X_BY_ACT = {n: [[m for m in range(t, STEPS_H, NT) if not hi_by_dve(n, m)] for t in range(NT)] for n in (1, 2)}
        X_BY_DVE = {n: [m for m in range(STEPS_H) if hi_by_dve(n, m)] for n in (1, 2)}
        PER = {1: NT, 2: 2 * NT}

        W2_D, W2_KU, W2_Q, W2_VU, W2_O = 0, 2048, 2304, 2816, 3328
        fc = lambda w: w.rearrange("(c p) n -> p c n", p=P)
        PIECES = {
            1: [(c * 1536, 1536, [(slice(0, 1536), wqkv_d[c * P:(c + 1) * P, :])]) for c in range(NC)]
            + [(6144, 2048, [("c", 0, 512, fc(wout_d))])],
            2: [(W2_D, 2048, [("c", 0, 128, fc(kvd_d)), ("c", 128, 128, fc(qd_d)), ("c", 256, 256, fc(rk_d))]),
                (W2_KU, 1280, [(slice(0, 256), ku_d), (slice(256, 512), qu_d), (slice(512, 768), rq_d),
                               (slice(768, 1280), vu_d)]),
                (W2_O, 2048, [("c", 0, 512, fc(ow_d))])],
        }
        BY_POOL = {1: (1, 3), 2: ()}

        def place(n, i):
            return 2 if n == 1 and i == 4 else i % 2

        NLOAD = {n: [sum(len(pc[k][2]) for k in range(i + 1) if place(n, k) == place(n, i)) for i in range(len(pc))]
                 for n, pc in PIECES.items()}

        def stage(n, i):
            if place(n, i) == 2:
                return ot[:, :, :].rearrange("p t n -> p (t n)")
            return qk[:, :, :].rearrange("p t n -> p (t n)")[:, 2048 * (i % 2):2048 * (i % 2) + 2048]

        def take_over(eng, old, new):
            for m in range(2):
                eng.wait_ge(old.free[m], B * old.per + old.extra + 1)
                eng.sem_inc(new.free[m], 1)

        def v_part(t, at):
            return vals[:, t, 0:H * VH].rearrange("p (h d) -> p h d", d=VH)[:, :, at:at + DH]

        def acc_of(blk):
            return acc[:, blk] if blk < B - 1 else yt

        def x3_of(blk, c):
            return (x3[:, blk, 0, c, :], x3[:, blk, 1, c, :]) if blk < B - 1 else (xh[:, c, :], xl[:, c, :])

        def resid(t):
            return (wh, wl)[t // 2][:, 7168 + t % 2 * D:7168 + (t % 2 + 1) * D].bitcast(F32)

        def o_t(c):
            return stack[:, HPG + c, 0, :], stack[:, HPG + c, 1, :]

        block = ctx.enter_context(nc.Block())

        @block.sync
        def _(sp):
            def passed():
                sp.sem_inc(spn, 1)

            def load_weights(n, pieces):
                p = ph[n]
                for i in pieces:
                    parts = PIECES[n][i][2]
                    if place(n, i) == 2:
                        sp.wait_ge(mod_mm, 1)
                    elif i >= 2 and i - 2 in BY_POOL[n]:
                        sp.wait_ge(p.w_lo_pool, 1)
                    elif i >= 2:
                        sp.wait_ge(p.w_lo, i - 1 if n == 2 else 1)
                    for part in parts:
                        if part[0] == "c":
                            _, at, width, src = part
                            dst = stage(n, i).rearrange("p (c n) -> p c n", c=NC)[:, :, at:at + width]
                        else:
                            dst, src = stage(n, i)[:, part[0]], part[1]
                        sp.dma_start(dst, src).then_inc(p.w_ld[place(n, i)], 16)

            def stacks(p, b, g):
                if p.n == 1:
                    sp.wait_ge(p.vlo, b * V1 + (2 + NC + g + 1))
                    passed()
                else:
                    p.ring.wait_read(sp, b, item(p, ("turn", g, "q")))
                    passed()
                p.ring.wait_read(sp, b, item(p, ("turn", g, "k")))
                passed()
                sp.dma_start(split_s[g % 2], split[:, :, :].bitcast(F32)).then_inc(p.split_st, 16)
                sp.wait_ge(p.split_st, b * 16 * NG + 16 * (g + 1))
                passed()
                sp.sem_inc(p.split_free, 1)
                last = 4 * (HPG * (g - 2) + HPG - 1) + 3
                sp.wait_ge(p.sk.full[1], b * p.sk.per + (H + last // 2 + 1))
                passed()
                if g == 1:
                    for t in (NT - 2, NT - 1):
                        p.ring.wait_full(sp, b, item(p, ("out", t)))
                        passed()
                src = split_s[g % 2].rearrange("(h p) c t -> p h c t", p=DH)
                at = HPG * (g % 2)
                for role, (cq, ck) in enumerate(((0, 2), (1, 2), (0, 3))):
                    for n, c in enumerate((cq, ck)):
                        sp.dma_start(stack[DH * role:DH * role + DH, at:at + HPG, n].bitcast(F32),
                                     src[:, :, c]).then_inc(p.stack_ld[g % 2], 16)

            def load_x(b):
                sp.dma_start(xt[:, :, :], x_d[bass.ds(b, 1)].rearrange("a (t p) n -> p (a t) n", p=P))\
                    .then_inc(ph[1].x_ld, 16)

            def load_x1(b):
                sp.dma_start(xt[:, :, :], x1_s[bass.ds(b, 1)].rearrange("a p t n -> p (a t) n")).then_inc(ph[2].x_ld, 16)

            for n, t_ in enumerate((ot, yt)):
                sp.dma_start(t_[:, :, :].rearrange("p a n -> p (a n)").rearrange("p (k n) -> p k n", k=2),
                             wemb_d.rearrange("(k p) n -> p k n", p=P)[:, 2 * n:2 * n + 2]).then_inc(wemb_ld, 16)
            sp.dma_start(vrow[0:16, :], cond_d.rearrange("b (c p) -> (b c) p", p=P)).then_inc(v_ld, 16)
            for at, rows, src in ((16, 8, bemb_d), (24, 4, gnorm_d), (28, 4, ln1_d), (32, 4, ln2_d)):
                sp.dma_start(vrow[at:at + rows, :], src.rearrange("(c p) -> c p", p=P)).then_inc(v_ld, 16)
            for row, src in ((36, gq_d), (37, gk_d)):
                sp.dma_start(vrow[row:row + 1, :].rearrange("a (h d) -> a h d", d=DH),
                             src.rearrange("(a d) -> a d", a=1).unsqueeze(1).broadcast_to([1, HPG, DH])).then_inc(v_ld, 16)
            load_x(0)
            load_weights(1, range(len(PIECES[1])))
            sp.dma_start(rope[:, 0], cos_d.rearrange("(t p) r -> p t r", p=P)).then_inc(v2_ld, 16)
            sp.dma_start(rope[:, 1], sin_d.rearrange("(t p) r -> p t r", p=P)).then_inc(v2_ld, 16)
            sp.dma_start(rwt[:, :, 0:NR], rw_d.rearrange("(c p) e -> p c e", p=P)).then_inc(v2_ld, 16)
            sp.dma_start(rb[:, 0:NR], rb_d.rearrange("(a e) -> a e", a=1).broadcast_to([P, NR])).then_inc(v2_ld, 16)
            p = ph[1]
            sp.sem_inc(p.split_free, 1)
            sp.sem_inc(p.y_free, 1)
            with sp.Fori(0, B) as b:
                sp.wait_ge(p.v, b * V1 + NC)
                passed()
                load_x((b + 1) % B)
                stacks(p, b, 0)
                for t in (NT - 2, NT - 1):
                    p.ring.wait_read(sp, b, item(p, ("out", t)))
                    passed()
                sp.dma_start(x1_s[bass.ds((b + (B - 1)) % B, 1)].rearrange("a p t n -> p (a t) n"), yt[:, :, :])\
                    .then_inc(p.y_st, 16)
                for g in range(1, NG):
                    stacks(p, b, g)
                sp.wait_ge(p.y_st, b * 16 + 16)
                passed()
                sp.sem_inc(p.y_free, 1)
            load_weights(2, range(2))
            sp.wait_ge(p.v, B * V1 + NC)
            load_x1(0)
            load_weights(2, range(2, 3))
            for t in (NT - 2, NT - 1):
                p.ring.wait_read(sp, B - 1, item(p, ("last", t)))
            sp.dma_start(x1_s[B - 1], yt[:, :, :]).then_inc(p.y_st, 16)
            sp.wait_ge(p.y_st, 16 * (B + 1))

            p = ph[2]
            sp.sem_inc(p.split_free, 1)
            sp.sem_inc(p.r_ld, 1)
            with sp.Fori(0, B) as b:
                sp.wait_ge(p.hi, b * HI[2] + NC)
                passed()
                load_x1((b + 1) % B)
                for g in range(2):
                    stacks(p, b, g)
                sp.wait_ge(p.acc_ok, b * NT + NT)
                passed()
                before = bass.ds((b + (B - 1)) % B, 1)
                sp.dma_start(acc_s[before].rearrange("a p t n -> p (a t) n"), yt[:, :, :]).then_inc(p.y_st, 16)
                for c in (NC - 2, NC - 1):
                    p.ring.wait_read(sp, b, item(p, ("x2", c)))
                    passed()
                for n, t_ in enumerate((xh, xl)):
                    sp.dma_start(xt_s[bass.ds((b + (B - 1)) % B, 1), :, n].rearrange("a p c t -> p (a c) t"),
                                 t_[:, :, :].bitcast(F32)).then_inc(p.y_st, 16)
                stacks(p, b, 2)
                sp.wait_ge(p.lg_ok, b + 1)
                passed()
                sp.dma_start(logits[:, bass.ds((b + (B - 1)) % B * NT, NT), :], lg[:, :, :]).then_inc(p.y_st, 16)
                sp.wait_ge(p.y_st, b * 64 + 64)
                passed()
                sp.sem_inc(p.y_free, 1)
                sp.dma_start(yt[:, :, :], x_d[bass.ds(b, 1)].rearrange("a (t p) n -> p (a t) n", p=P)).then_inc(p.r_ld, 16)
                for n, w in enumerate((wh, wl)):
                    sp.dma_start(w[:, 7168:8192].bitcast(F32).rearrange("p (t n) -> p t n", n=D),
                                 x1_s[bass.ds(b, 1), :, 2 * n:2 * n + 2].rearrange("a p t n -> p (a t) n"))\
                        .then_inc(p.r_ld, 16)
                stacks(p, b, 3)

            def load_expert(e):
                for at, src in ((0, gate_d), (INNER, up_d)):
                    sp.dma_start(wstage[:, 0:NC, at:at + INNER],
                                 src[bass.ds(e, 1)].rearrange("a (c p) i -> p (a c) i", p=P)).then_inc(ew_ld, 16)
                sp.dma_start(wstage[:, NC:, :],
                             down_d[bass.ds(e, 1)].rearrange("a (c p) i -> p (a c) i", p=P)).then_inc(ew_ld, 16)

            sp.wait_ge(p.sk.full[1], B * p.sk.per + H)
            load_expert(0)
            p.ring.wait_full(sp, B - 1, item(p, ("last", NT - 1)))
            for blk in range(B - 1):
                sp.dma_start(x3[:, blk].rearrange("p n c t -> p (n c t)").bitcast(F32),
                             xt_s[blk].rearrange("p n c t -> p (n c t)")).then_inc(x3_ld[blk], 16)
                if blk == 0:
                    for t in (NT - 2, NT - 1):
                        p.ring.wait_read(sp, B - 1, item(p, ("last", t)))
                sp.dma_start(acc[:, blk], acc_s[blk]).then_inc(acc_ld[blk], 16)
            with sp.Fori(0, NE // 2) as i:
                for j in range(2):
                    sp.wait_ge(ew_lo, i * 6 + 3 * (j + 1))
                    passed()
                    load_expert((i * 2 + (j + 1)) % NE)
            sp.wait_ge(ew_ld, 48 * (NE + 1))
            sp.wait_ge(ph[2].y_st, 64 * B)
            sp.wait_ge(ph[2].x_ld, 16 * (B + 1))
            for blk in range(B):
                for t in range(NT):
                    sp.wait_ge(dring.free[t], 1 + B * (NE - 1) + blk + 1)
                sp.dma_start(out_d[blk].rearrange("(t p) n -> p t n", p=P), acc_of(blk)[:, :, :]).then_inc(out_st, 16)
            sp.wait_ge(out_st, 16 * B)

        @block.tensor
        def _(pe):
            def three(out, lhs, rhs, last_of=None):
                n = len(lhs)
                for i, ((ah, al), (bh, bl)) in enumerate(zip(lhs, rhs)):
                    nc.tensor.matmul(out, ah, bh, start=(i == 0), stop=False)
                    nc.tensor.matmul(out, al, bh, start=False, stop=False)
                    last = nc.tensor.matmul(out, ah, bl, start=False, stop=(i == n - 1))
                return last

            def turn(p, b, key, src):
                m = item(p, key)
                p.ring.wait_free(pe, b, m)
                for t in range(NT):
                    last = nc.tensor.transpose(psum[:, p.ring.bank(m), t * P:(t + 1) * P], src(t), ident[:, :])
                p.ring.filled(last, m)

            def beside(p, b, key, c):
                if key == "x":
                    if c == 0:
                        pe.wait_ge(p.xn, b * PER[p.n] + (PER[p.n] + NT))
                    turn(p, b, (key, c), lambda t: xt[:, t, c * P:(c + 1) * P])
                elif key in ("x2", "last_x2"):
                    if c == 0:
                        pe.wait_ge(p.xn, b * 2 * NT + (4 * NT if key == "last_x2" else 2 * NT))
                    turn(p, b, (key, c), lambda t: ot[:, t, c * P:(c + 1) * P])
                else:
                    if c == 0:
                        for k in (NC - 2, NC - 1):
                            p.ring.wait_read(pe, b, item(p, (key.replace("router", "x2"), k)))
                    else:
                        p.ring.wait_read(pe, b, item(p, (key, 0)))
                    m = item(p, (key, c))
                    p.ring.wait_free(pe, b, m)
                    if c == 0:
                        last = three(psum[0:NE, p.ring.bank(m), :], [(rwh[:, k, :], rwl[:, k, :]) for k in range(NC)],
                                     chans())
                    else:
                        pe.sem_inc(pen, 1)
                        for t in range(NT):
                            last = nc.tensor.transpose(psum[:, p.ring.bank(m), t * NE:(t + 1) * NE],
                                                       junk[0:NE, t * P:(t + 1) * P], ident[0:NE, 0:NE])
                    p.ring.filled(last, m)

            def heads(p, b, causal, values, out):
                def scores(h, t):
                    m = 4 * h + t
                    g = h // HPG
                    if t == 0:
                        pe.wait_ge(p.stack_ld[g % 2], b * 192 + 96 * (g // 2 + 1))
                    p.sq.wait_free(pe, b, m)
                    n = (t + 1) * P if causal else S
                    bank = p.sq.bank(m)
                    st = stack[0:XSTACK, h % NSTK]
                    last = nc.tensor.matmul(psum[:, bank, 0:n], st[:, 0, t * P:(t + 1) * P], st[:, 1, 0:n],
                                            start=True, stop=not causal)
                    if causal:
                        last = nc.tensor.matmul(psum[:, bank, t * P:n], mask[:, :], identr[:, :],
                                                start=False, stop=True)
                    p.sq.filled(last, m)

                def turn_max(h):
                    m = item(p, ("max", h))
                    p.ring.wait_free(pe, b, m)
                    for t in (2, 3):
                        p.sq.wait_read(pe, b, 4 * h + t)
                    for t in range(NT):
                        last = nc.tensor.transpose(psum[0:1, p.ring.bank(m), t * P:(t + 1) * P],
                                                   nmax[:, h % 4, t:t + 1], ident[:, :])
                    p.ring.filled(last, m)

                def scores_t(h, t):
                    m = 4 * h + t
                    if t == 0:
                        p.ring.wait_read(pe, b, item(p, ("max", h)))
                    if m == HPG * NT:
                        pe.wait_ge(p.ones, b + 1)
                    p.sk.wait_free(pe, b, m)
                    lo = t * P if causal else 0
                    bank = p.sk.bank(m)
                    st = stack[0:XSTACK + 1, h % NSTK]
                    last = nc.tensor.matmul(psum[:, bank, lo:S], st[:, 1, t * P:(t + 1) * P], st[:, 0, lo:S],
                                            start=True, stop=not causal)
                    if causal:
                        last = nc.tensor.matmul(psum[:, bank, lo:lo + P], identr[:, :], mask[:, :],
                                                start=False, stop=True)
                    last.then_inc(p.sk.full[m % 2], 1)

                def pv(h, t):
                    m = 4 * h + t
                    if t == 0:
                        p.o.wait_free(pe, b, h)
                    pe.wait_ge(p.p_lo[t], b * H + (h + 1))
                    lo = t * P if causal else 0
                    out = psum[:, p.o.bank(h), lo:S]
                    for n, pr in enumerate((ph_, pl_)):
                        last = nc.tensor.matmul(out, vals[:, t, h * VH:h * VH + P], pr[:, m % NP, lo:S],
                                                start=(t == 0 and n == 0), stop=(t == NT - 1 and n == 1))
                    if t == NT - 1:
                        p.o.filled(last, h)

                def turn_out(h):
                    m = item(p, ("o", h))
                    p.ring.wait_free(pe, b, m)
                    p.o.wait_read(pe, b, h)
                    for t in range(NT):
                        last = nc.tensor.matmul(psum[:, p.ring.bank(m), t * P:t * P + DH + 1],
                                                ov[:, h % 2, t * P:(t + 1) * P], fold[:, :], start=True, stop=True)
                    p.ring.filled(last, m)

                def turn_qk(g, c):
                    at = (D if c == "k" else 0) + g * P
                    turn(p, b, ("turn", g, c), lambda t: qk[:, t, at:at + P])

                for key, *at in FIRST[p.n]:
                    if key == "out":
                        out(*at)
                    elif key == "v":
                        values(*at)
                    else:
                        if at == [0, "k"]:
                            if p.n == 1:
                                pe.wait_ge(p.kn, b * 3 + 3)
                                pe.wait_ge(p.qn, b * (NT + 1) + NT + 1)
                            else:
                                pe.wait_ge(p.ra, b * 8 + 10)
                        turn_qk(*at)
                for m in range(LEAD):
                    scores(*divmod(m, NT))
                turn_max(0)
                for t in (2, 3):
                    p.ring.wait_read(pe, b, item(p, ("v", t)))
                for m in range(LAST + 1):
                    if m + LEAD < STEPS_H:
                        scores(*divmod(m + LEAD, NT))
                    if head_max(m) is not None:
                        turn_max(head_max(m))
                    if m < STEPS_H:
                        scores_t(*divmod(m, NT))
                    if 0 <= m - LAG < STEPS_H:
                        pv(*divmod(m - LAG, NT))
                    if head_out(m) is not None:
                        turn_out(head_out(m))
                    if group_turn(m):
                        for c in "kq":
                            turn_qk(group_turn(m), c)
                    if m in BESIDE[p.n]:
                        beside(p, b, *BESIDE[p.n][m])
                for h in (H - 2, H - 1):
                    p.ring.wait_read(pe, b, item(p, ("o", h)))
                for c in range(NC):
                    turn(p, b, ("turn_o", c), lambda t: ot[:, t, c * P:(c + 1) * P])

            def x_by(wat, width, stride):
                return [(wh[:, wat + c * stride:wat + c * stride + width], wl[:, wat + c * stride:wat + c * stride + width])
                        for c in range(NC)]

            def tokens(t):
                return [(xh[:, c, t * P:(t + 1) * P], xl[:, c, t * P:(t + 1) * P]) for c in range(NC)]

            def o_tokens(t):
                return [tuple(o_t(c)[n][:, t * P:(t + 1) * P] for n in range(2)) for c in range(NC)]

            def chans():
                return [(xh[:, c, :], xl[:, c, :]) for c in range(NC)]

            def project(p, b, key, lhs, rhs):
                m = item(p, key)
                p.ring.wait_free(pe, b, m)
                n = rhs[0][0].shape[-1]
                p.ring.filled(three(psum[:, p.ring.bank(m), 0:n], lhs, rhs), m)

            pe.wait_ge(c_ok, 10)
            pe.wait_ge(r_ok, 2)
            pe.wait_ge(v_ld, 7 * 16)
            nc.tensor.transpose(psum[:, 2, 0:38], vrow[0:38, :], ident[0:38, 0:38]).then_inc(vT, 1)
            pe.wait_ge(prep, 1)
            pe.wait_ge(wemb_ld, 32)
            wemb = [t_[:, :, :].rearrange("p a n -> p (a n)")[:, k * 2 * D:(k + 1) * 2 * D]
                    for t_ in (ot, yt) for k in range(2)]
            for m in range(2 * NC):
                for k in range(NC):
                    last = nc.tensor.matmul(psum[:, 3, m * B:(m + 1) * B], wemb[k][:, m * P:(m + 1) * P],
                                            vcol[:, k:16:4], start=(k == 0), stop=(k == NC - 1))
            last.then_inc(mod_mm, 1)

            p = ph[1]
            pe.sem_inc(p.sk.full[1], H)
            pe.wait_ge(p.xn, NT)
            for c in range(NC):
                turn(p, 0, ("x0", c), lambda t: xt[:, t, c * P:(c + 1) * P])
            pe.wait_ge(p.w_lo, 2)
            pe.wait_ge(p.w_lo_pool, 2)
            with pe.Fori(0, B) as b:
                pe.wait_ge(p.vlo, b * V1 + (2 + NC))
                for t in range(NT):
                    for n, c in enumerate("qk"):
                        project(p, b, ("qk", t, c), tokens(t), x_by(n * D, D, 3 * D))
                pe.wait_ge(p.w_lo, 3)
                heads(p, b, False, lambda t: project(p, b, ("v", t), tokens(t), x_by(2 * D, D, 3 * D)),
                      lambda t: project(p, b, ("out", t), o_tokens(t), x_by(3 * D * NC, D, D)))
            for c in (NC - 2, NC - 1):
                p.ring.wait_read(pe, B - 1, item(p, ("turn_o", c)))
            for t in range(NT):
                project(p, B - 1, ("last", t), o_tokens(t), x_by(3 * D * NC, D, D))

            p = ph[2]
            pe.sem_inc(p.sk.full[1], H)
            pe.wait_ge(p.xn, NT)
            for c in range(NC):
                turn(p, 0, ("x0", c), lambda t: xt[:, t, c * P:(c + 1) * P])
            pe.wait_ge(p.w_lo, 2)
            kvh, qdh = (wh[:, 6144:6656], wl[:, 6144:6656]), (wh[:, 6656:7168], wl[:, 6656:7168])
            pair = lambda at, n: (wh[:, at:at + n], wl[:, at:at + n])
            cut = lambda xx, t: (xx[0][:, t * P:(t + 1) * P], xx[1][:, t * P:(t + 1) * P])
            for c in (NC - 2, NC - 1):
                p.ring.wait_read(pe, 0, item(p, ("x0", c)))
            with pe.Fori(0, B) as b:
                project(p, b, "kv_d", x_by(W2_D, P, 512), chans())
                project(p, b, "q_d", x_by(W2_D + P, P, 512), chans())
                for key in ("kv_d", "q_d"):
                    p.ring.wait_read(pe, b, item(p, key))
                for t in range(NT):
                    project(p, b, ("qk", t, "q"), [cut(qdh, t)], [pair(W2_Q, 512)])
                    m = item(p, ("qk", t, "k"))
                    p.ring.wait_free(pe, b, m)
                    three(psum[:, p.ring.bank(m), 0:256], [cut(kvh, t)], [pair(W2_KU, 256)])
                    p.ring.filled(three(psum[:, p.ring.bank(m), 256:512], tokens(t), x_by(W2_D + 256, 256, 512)), m)
                pe.wait_ge(p.w_lo, len(PIECES[2]) + 1)
                heads(p, b, True, lambda t: project(p, b, ("v", t), [cut(kvh, t)], [pair(W2_VU, 512)]),
                      lambda t: project(p, b, ("out", t), o_tokens(t), x_by(W2_O, D, D)))
            for c in (NC - 2, NC - 1):
                p.ring.wait_read(pe, B - 1, item(p, ("turn_o", c)))
            for t in range(NT):
                project(p, B - 1, ("last", t), o_tokens(t), x_by(W2_O, D, D))
            for c in range(NC):
                beside(p, B - 1, "last_x2", c)
            for c in range(2):
                beside(p, B - 1, "last_router", c)

            with pe.Fori(0, NE // 2) as i:
                def gate_up(k):
                    j, blk = divmod(k, B)
                    if blk == 0:
                        pe.wait_ge(ew_lo, i * 6 + 3 * (j + 1))
                    if blk < B - 1 and j == 0:
                        pe.wait_ge(x3_ld[blk], 16)
                    for n in range(NI):
                        for u in range(2):
                            m = 4 * k + 2 * n + u
                            guring.wait_free(pe, i, m)
                            at = u * INNER + n * P
                            last = three(psum[:, guring.bank(m), :],
                                         [(ew[:, j, 0, c, at:at + P], ew[:, j, 1, c, at:at + P]) for c in range(NC)],
                                         [x3_of(blk, c) for c in range(NC)])
                            guring.filled(last, m)

                def down(k):
                    j = k // B
                    pe.wait_ge(h_lo, i * 16 + (2 + 2 * k + 2))
                    for t in range(NT):
                        m = 4 * k + t
                        dring.wait_free(pe, i, m)
                        last = three(psum[:, dring.bank(m), :],
                                     [(hs[:, k % 2, 0, n, t * P:(t + 1) * P], hs[:, k % 2, 1, n, t * P:(t + 1) * P])
                                      for n in range(NI)],
                                     [(ew[:, j, 0, NC + n, :], ew[:, j, 1, NC + n, :]) for n in range(NI)])
                        dring.filled(last, m)

                for k in range(2 * B):
                    gate_up(k)
                    if k:
                        down(k - 1)
                down(2 * B - 1)

        @block.scalar
        def _(act):
            def weights(n, pieces):
                p = ph[n]
                for i in pieces:
                    at, cols, _ = PIECES[n][i]
                    if n == 2 and i == 0:
                        act.wait_ge(p.w_ln, NC)
                    act.wait_ge(p.w_ld[place(n, i)], 16 * NLOAD[n][i])
                    nc.scalar.activation(wh[:, at:at + cols], stage(n, i)[:, 0:cols], ACT.Copy).then_inc(p.w_hi, 1)

            def square(p, b, src, first, per, t):
                if first + t:
                    act.wait_ge(p.ss, b * per + (first + t))
                nc.scalar.activation(junk[:, :], src[:, t, :], ACT.Square,
                                     accum_out=sst[:, t:t + 1]).then_inc(p.ss, 1)

            def squares(p, b, src, first, per):
                for t in range(NT):
                    square(p, b, src, first, per, t)

            def hi_of(p, b, key, out):
                m = item(p, key)
                p.ring.wait_full(act, b, m)
                nc.scalar.activation(out, psum[:, p.ring.bank(m), :], ACT.Copy).then_inc(p.hi, 1)

            def hi_of_value(p, b, k, out):
                act.wait_ge(p.v, b * V1 + (k + 1))
                nc.scalar.activation(out, vs[:, k % 2, :], ACT.Copy).then_inc(p.vhi, 1)

            def turn_qk(p, b, g, c):
                at = {"q": 0, "k": 2}[c]
                act.wait_ge(p.split_free, b * NG + (g + 1))
                if p.n == 1 and c == "q":
                    hi_of_value(p, b, NC + g, split[:, at, :])
                else:
                    hi_of(p, b, ("turn", g, c), split[:, at, :])

            def values(p, b, t):
                m = item(p, ("v", t))
                p.ring.wait_full(act, b, m)
                nc.scalar.activation(v_part(t, 0),
                                     psum[:, p.ring.bank(m), :].rearrange("p (h d) -> p h d", d=DH),
                                     ACT.Copy).then_inc(p.hi, 1)

            def max_row(p, b, h):
                m = item(p, ("max", h))
                p.ring.wait_full(act, b, m)
                p.ring.cleared(nc.scalar.activation(stack[XSTACK:XSTACK + 1, h % NSTK, 0, :],
                                                    psum[0:1, p.ring.bank(m), :], ACT.Copy), m)

            def heads(p, b, causal):
                for key, *at in FIRST[p.n]:
                    if key == "turn":
                        turn_qk(p, b, *at)
                    elif key == "v":
                        values(p, b, *at)
                    elif p.n == 2:
                        p.ring.wait_read(act, b, item(p, (key, *at)))
                        square(p, b, ot, NT, 2 * NT, *at)
                max_row(p, b, 0)
                for m in range(LAST + 1):
                    h, t = divmod(m, NT)
                    if m < STEPS_H:
                        act.wait_ge(p.sk.full[m % 2], b * p.sk.per + (H * (m % 2) + m // 2 + 1))
                        if m >= NX:
                            hx, tx = divmod(m - NX, NT)
                            act.wait_ge(p.p_lo[tx], b * H + (hx + 1))
                        lo = t * P if causal else 0
                        scoresT = psum[:, p.sk.bank(m), lo:S]
                        ins = nc.scalar.activation(probs[:, m % NX, lo:S], scoresT, ACT.Exp, scale=SCALE)
                        if not hi_by_dve(p.n, m):
                            ins.then_inc(p.p_x[t], 1)
                            p.sk.cleared(nc.scalar.activation(ph_[:, m % NP, lo:S], scoresT, ACT.Exp, scale=SCALE), m)
                        else:
                            p.sk.cleared(ins, m)
                    if t == 2 and h + 1 < H:
                        max_row(p, b, h + 1)
                    ho = h - (LAG + NT) // NT
                    if t == (NT - 1 + LAG + 1) % NT and 0 <= ho < H:
                        p.o.wait_full(act, b, ho)
                        p.o.cleared(nc.scalar.activation(ov[:, ho % 2, :], psum[:, p.o.bank(ho), :],
                                                         ACT.Copy), ho)
                    if group_turn(m):
                        for c in "kq":
                            turn_qk(p, b, group_turn(m), c)
                    if m == SQUARE_STEP:
                        act.wait_ge(p.x_ld, b * 16 + 32)
                        squares(p, b, xt, PER[p.n], PER[p.n])
                    if m in BESIDE[p.n]:
                        key, c = BESIDE[p.n][m]
                        if p.n == 1:
                            hi_of_value(p, b, NC + NG + c, xh[:, c, :])
                        elif key != "router":
                            if key == "x" and c == 0:
                                act.wait_ge(p.y_free, b + 1)
                            hi_of(p, b, (key, c), xh[:, c, :])
                for c in range(NC):
                    hi_of(p, b, ("turn_o", c), o_t(c)[0])

            act.wait_ge(c_ok, 2)
            nc.scalar.activation(identr[:, :], ident[:, :], ACT.Copy).then_inc(r_ok, 1)
            act.wait_ge(c_ok, 6)
            nc.scalar.activation(mask[:, :], vs[:, 0, 0:P], ACT.Copy).then_inc(r_ok, 1)
            act.wait_ge(ph[1].x_ld, 16)
            squares(ph[1], 0, xt, 0, NT)
            weights(1, range(4))
            p = ph[1]
            act.sem_inc(p.sk.free[0], 1)
            act.sem_inc(p.sk.free[1], 1)
            act.sem_inc(p.o.free[0], 1)
            act.sem_inc(p.o.free[1], 1)
            for k in range(NC):
                hi_of_value(p, 0, k, xh[:, k, :])
            weights(1, [4])
            with act.Fori(0, B) as b:
                for t in range(NT):
                    for n, c in enumerate("qk"):
                        m = item(p, ("qk", t, c))
                        p.ring.wait_full(act, b, m)
                        p.ring.cleared(nc.scalar.activation(qk[:, t, n * D:(n + 1) * D],
                                                            psum[:, p.ring.bank(m), :], ACT.Copy), m)
                heads(p, b, causal=False)

            p = ph[2]
            take_over(act, ph[1].sk, p.sk)
            take_over(act, ph[1].o, p.o)
            act.wait_ge(p.x_ld, 16)
            squares(p, 0, xt, 0, 2 * NT)
            weights(2, range(len(PIECES[2])))
            for c in range(NC):
                hi_of(p, 0, ("x0", c), xh[:, c, :])
            act.wait_ge(rw_ok, 1)
            nc.scalar.activation(rwh[:, :, :], rwt[:, :, :], ACT.Copy).then_inc(p.w_hi, 1)
            with act.Fori(0, B) as b:
                hi_of(p, b, "kv_d", wh[:, 6144:6656])
                hi_of(p, b, "q_d", wh[:, 6656:7168])
                for t in range(NT):
                    for n, c in enumerate("qk"):
                        m = item(p, ("qk", t, c))
                        p.ring.wait_full(act, b, m)
                        nc.scalar.activation(
                            qk[:, t, n * D:(n + 1) * D].rearrange("p (h d) -> p h d", d=DH)[:, :, 0:RD],
                            psum[:, p.ring.bank(m), 0:H * RD].rearrange("p (h d) -> p h d", d=RD),
                            ACT.Copy).then_inc(p.head_sq, 1)
                        if t:
                            act.wait_ge(p.rt, b * 2 * NT + (2 * t + n - 1))
                        p.ring.cleared(nc.scalar.activation(ov[:, n, 0:H * RD], psum[:, p.ring.bank(m), H * RD:],
                                                            ACT.Copy), m)
                heads(p, b, causal=True)

            def split_expert(e, j, c):
                nc.scalar.activation(ew[:, j, 0, 2 * c:2 * c + 2, :], wstage[:, 2 * c:2 * c + 2, :],
                                     ACT.Copy).then_inc(ew_hi, 1)

            for t in range(NT):
                if t >= 2:
                    act.wait_ge(ew_ln, NC)
                    split_expert(0, 0, t - 2)
                p.ring.wait_read(act, B - 1, item(p, ("last", t)))
                square(p, B - 1, ot, 3 * NT, 2 * NT, t)
            split_expert(0, 0, 2)
            for c in range(NC):
                hi_of(p, B - 1, ("last_x2", c), xh[:, c, :])

            for old, n in ((p.sk, 0), (p.o, 2)):
                for m in range(2):
                    act.wait_ge(old.free[m], B * old.per + 1)
                    act.sem_inc(dring.free[n + m], 1)
            act.wait_ge(p.lg_ok, B + 1)
            nc.scalar.activation(gtmp[:, 0], logits[:, :, :], ACT.Exp, scale=-1.0).then_inc(g_exp, 1)
            with act.Fori(0, NE // 2) as i:
                for k in range(2 * B):
                    j, blk = divmod(k, B)
                    for n in range(NI):
                        m = 4 * k + 2 * n
                        guring.wait_full(act, i, m)
                        act.wait_ge(h_v, i * 16 + (2 + 2 * k + n - 1))
                        guring.cleared(nc.scalar.activation(sg[:, n, :], psum[:, guring.bank(m), :], ACT.Silu), m)
                    for n in range(NI):
                        act.wait_ge(h_v, i * 16 + (2 + 2 * k + n + 1))
                        nc.scalar.activation(hs[:, k % 2, 0, n, :], hv[:, n, :], ACT.Copy).then_inc(h_hi, 1)
                    if blk:
                        act.wait_ge(ew_ln, i * 2 * NC + NC * (j + 2))
                        split_expert(0, 1 - j, blk - 1)

        @block.gpsimd
        def _(pool):
            nc.gpsimd.memset(ident[:, :], 0.0).then_inc(c_ok, 1)
            pool.wait_ge(c_ok, 1)
            nc.gpsimd.affine_select(out=ident[:, :], in_=ident[:, :], compare_op=ALU.not_equal, fill=1.0, base=0,
                                    pattern=[[-1, P]], channel_multiplier=1).then_inc(c_ok, 1)
            nc.gpsimd.memset(vals[:, :, :].bitcast(F32), 1.0).then_inc(c_ok, 1)
            nc.gpsimd.memset(fold[:, :], 0.0).then_inc(c_ok, 1)
            nc.gpsimd.memset(vs[:, :, 0:P], 0.0).then_inc(c_ok, 1)
            pool.wait_ge(c_ok, 5)
            nc.gpsimd.affine_select(out=vs[:, 0, 0:P], in_=vs[:, 0, 0:P], compare_op=ALU.is_ge, fill=NEG, base=0,
                                    pattern=[[1, P]], channel_multiplier=-1).then_inc(c_ok, 1)
            nc.gpsimd.affine_select(out=fold[:, :], in_=fold[:, :], compare_op=ALU.not_equal, fill=1.0, base=0,
                                    pattern=[[-1, DH + 1]], channel_multiplier=1).then_inc(c_ok, 1)
            pool.wait_ge(c_ok, 7)
            nc.gpsimd.affine_select(out=fold[:, 0:DH], in_=fold[:, 0:DH], compare_op=ALU.not_equal, fill=1.0,
                                    base=-(DH + 1), pattern=[[-1, DH]], channel_multiplier=1).then_inc(c_ok, 1)
            pool.wait_ge(c_ok, 8)
            nc.gpsimd.memset(stack[:, HPG:HPG + NC].bitcast(F32), 0.0).then_inc(c_ok, 1)
            pool.wait_ge(c_ok, 9)
            nc.gpsimd.memset(stack[XSTACK:XSTACK + 1, 0:HPG, 1, :].bitcast(F32), 1.0).then_inc(c_ok, 1)

            def lo_of_value(p, b, k, hi, out):
                pool.wait_ge(p.vhi, b * V1 + (k + 1))
                nc.gpsimd.tensor_tensor(out, vs[:, k % 2, :], hi.bitcast(F32), ALU.subtract).then_inc(p.vlo, 1)

            def turn_q(p, b, g):
                lo_of_value(p, b, NC + g, split[:, 0, :], split[:, 1, :])

            pool.wait_ge(c_ok, 10)

            def heads(p, b, causal):
                if p.n == 1:
                    turn_q(p, b, 0)
                for t in (NT - 2, NT - 1):
                    p.ring.wait_full(pool, b, item(p, ("out", t)))
                    pool.sem_inc(pln, 1)
                if p.n == 1:
                    pool.wait_ge(p.kn, b * 3 + 3)
                    pool.sem_inc(pln, 1)
                    pool.wait_ge(p.vlo, b * V1 + (2 + NC + 1))
                else:
                    pool.wait_ge(p.acc_ok, b * NT + NT)
                pool.sem_inc(pln, 1)
                nc.gpsimd.memset(stack[XSTACK:XSTACK + 1, HPG:, 1, :].bitcast(F32), 1.0).then_inc(p.ones, 1)
                pool.wait_ge(p.ones, b + 1)
                if p.n == 1:
                    turn_q(p, b, 1)
                for m in range(STEPS_H):
                    h, t = divmod(m, NT)
                    if t < NT - 1:
                        lo = t * P if causal else 0
                        if hi_by_dve(p.n, m):
                            by_dve = X_BY_DVE[p.n]
                            pool.wait_ge(p.p_hi, b * len(by_dve) + (by_dve.index(m) + 1))
                        else:
                            by_act = X_BY_ACT[p.n][t]
                            pool.wait_ge(p.p_x[t], b * len(by_act) + (by_act.index(m) + 1))
                        p.sk.wait_read(pool, b, m)
                        nc.gpsimd.tensor_tensor(pl_[:, m % NP, lo:S], probs[:, m % NX, lo:S], ph_[:, m % NP, lo:S].bitcast(F32),
                                                ALU.subtract).then_inc(p.p_lo[t], 1)
                    if p.n == 1 and group_turn(m):
                        turn_q(p, b, group_turn(m))
                    if p.n == 1 and m in BESIDE[1]:
                        c = BESIDE[1][m][1]
                        lo_of_value(p, b, NC + NG + c, xh[:, c, :], xl[:, c, :])

            p = ph[1]
            pool.sem_inc(p.vlo, 2)
            for i in BY_POOL[1]:
                at, cols, _ = PIECES[1][i]
                pool.wait_ge(p.w_hi, i + 1)
                nc.gpsimd.tensor_tensor(wl[:, at:at + cols], stage(1, i)[:, 0:cols], wh[:, at:at + cols].bitcast(F32),
                                        ALU.subtract).then_inc(p.w_lo_pool, 1)
            for c in range(NC):
                lo_of_value(p, 0, c, xh[:, c, :], xl[:, c, :])
            with pool.Fori(0, B) as b:
                for n in range(2 * NT):
                    t, c = divmod(n, 2)
                    p.ring.wait_read(pool, b, item(p, ("qk", t, "qk"[c])))
                    pool.wait_ge(p.head_ss, b * 2 * NT + (n + 1))
                    src = qk[:, t, c * D:(c + 1) * D]
                    nc.gpsimd.tensor_tensor(probs[:, n % 2, :], src, src, ALU.mult).then_inc(p.head_sq, 1)
                pool.wait_ge(p.step, b * STEPS[1] + RSQRT_STEPS)
                for t in range(3):
                    kk = qk[:, t, D:2 * D].rearrange("p (h d) -> p h d", d=DH)
                    r = rsh[:, 0, t * 2 * H + H:(t + 1) * 2 * H].unsqueeze(2).broadcast_to([P, H, DH])
                    nc.gpsimd.tensor_tensor(kk, kk, r, ALU.mult).then_inc(p.kn, 1)
                heads(p, b, False)

            p = ph[2]

            def add_acc(b, key):
                for t in range(NT):
                    p.ring.wait_read(pool, b, item(p, (key, t)))
                    nc.gpsimd.tensor_tensor(yt[:, t, :], yt[:, t, :], ot[:, t, :], ALU.add).then_inc(p.acc_ok, 1)

            pool.wait_ge(ph[1].y_st, 16 * (B + 1))
            with pool.Fori(0, B) as b:
                for n in range(2 * NT):
                    t, c = divmod(n, 2)
                    pool.wait_ge(p.rt, b * 2 * NT + (n + 1))
                    r = lambda a: probs[:, n % 2, a * 256:(a + 1) * 256].rearrange("p (h d) -> p h d", d=RD)
                    nc.gpsimd.tensor_tensor(
                        qk[:, t, c * D:(c + 1) * D].rearrange("p (h d) -> p h d", d=DH)[:, :, RD:DH],
                        r(0), r(1), ALU.add).then_inc(p.ra, 1)
                pool.wait_ge(p.r_ld, b * 48 + 1)
                add_acc(b, "out")
                heads(p, b, True)
            pool.wait_ge(p.r_ld, B * 48 + 1)
            add_acc(B - 1, "last")

            pool.sem_inc(h_lo, 2)

            def split_expert(e, j, c):
                nc.gpsimd.tensor_tensor(ew[:, j, 1, 2 * c:2 * c + 2, :], wstage[:, 2 * c:2 * c + 2, :],
                                        ew[:, j, 0, 2 * c:2 * c + 2, :].bitcast(F32), ALU.subtract).then_inc(ew_lo, 1)

            for c in (1, 2):
                pool.wait_ge(ew_hi, c + 1)
                split_expert(0, 0, c)
            with pool.Fori(0, NE // 2) as i:
                for k in range(2 * B):
                    j, blk = divmod(k, B)
                    for n in range(NI):
                        pool.wait_ge(h_hi, i * 16 + (2 * k + n + 1))
                        nc.gpsimd.tensor_tensor(hs[:, k % 2, 1, n, :], hv[:, n, :], hs[:, k % 2, 0, n, :].bitcast(F32),
                                                ALU.subtract).then_inc(h_lo, 1)
                    if blk:
                        pool.wait_ge(ew_hi, i * 6 + (3 * (j + 1) + blk))
                        split_expert(0, 1 - j, blk - 1)

        @block.vector
        def _(dve):
            class Chain:

                def __init__(self, s, base=None, per=0):
                    self.s, self.base, self.per, self.n = s, base, per, 0

                def __call__(self, ins):
                    self.n += 1
                    ins.then_inc(self.s, 1)
                    v = self.n if self.base is None else self.base * self.per + self.n
                    dve.wait_ge(self.s, v)

            V = nc.vector

            def rsqrt(link, x, y, t, mean, eps):
                for k in range(4):
                    rsqrt_part(link, k, x, y, t, mean, eps)

            def rsqrt_part(link, k, x, y, t, mean, eps):
                if k == 0:
                    link(V.tensor_scalar(x, x, mean, eps, ALU.mult, ALU.add))
                    link(V.tensor_scalar(y.bitcast(I32), x.bitcast(I32), 1, None, ALU.logical_shift_right))
                    link(V.tensor_scalar(y.bitcast(I32), y.bitcast(I32), -1, MAGIC, ALU.mult, ALU.add))
                else:
                    link(V.scalar_tensor_tensor(out=t, in0=y, scalar=-0.5, in1=y, op0=ALU.mult, op1=ALU.mult))
                    link(V.tensor_tensor(t, t, x, ALU.mult))
                    link(V.scalar_tensor_tensor(out=y, in0=t, scalar=1.5, in1=y, op0=ALU.add, op1=ALU.mult))

            def normalize_part(p, b, link, k, eps, x, nth, per):
                if k == 0:
                    dve.wait_ge(p.ss, b * per + NT * (nth + 1))
                if k < 4:
                    rsqrt_part(link, k, sst[:, :], rst[:, 0, :], rst[:, 1, :], 1.0 / D, eps)
                else:
                    t = k - 4
                    V.tensor_scalar(x[:, t, :], x[:, t, :], rst[:, 0, t:t + 1], None, ALU.mult).then_inc(p.xn, 1)

            def normalize(p, b, link, eps, x, nth, per):
                for k in range(8):
                    normalize_part(p, b, link, k, eps, x, nth, per)

            def lo_of(p, b, key, hi, out):
                m = item(p, key)
                dve.wait_ge(p.hi, b * HI[p.n] + (hi_no[p.n][key] + 1))
                p.ring.cleared(V.tensor_tensor(out, psum[:, p.ring.bank(m), :], hi.bitcast(F32), ALU.subtract), m)

            def value(p, b, k, key, s1, s2):
                m = item(p, key)
                p.ring.wait_full(dve, b, m)
                dve.wait_ge(p.vlo, b * V1 + (k + 1))
                if s2 is None:
                    V.tensor_scalar(vs[:, k % 2, :], psum[:, p.ring.bank(m), :], s1, None, ALU.mult).then_inc(p.v, 1)
                else:
                    V.tensor_scalar(vs[:, k % 2, :], psum[:, p.ring.bank(m), :], s1, s2, ALU.mult, ALU.add)\
                        .then_inc(p.v, 1)
                dve.wait_ge(p.v, b * V1 + (k + 1))
                dve.sem_inc(p.ring.free[m % 2], 1)

            def turn_qk(p, b, g, c):
                if p.n == 1 and c == "q":
                    value(p, b, NC + g, ("turn", g, c), gqk[:, 0:1], None)
                else:
                    at = {"q": 0, "k": 2}[c]
                    lo_of(p, b, ("turn", g, c), split[:, at, :], split[:, at + 1, :])

            def route(p, b, key, n, out):
                m = item(p, key)
                p.ring.wait_full(dve, b, m)
                if n == 0:
                    p.ring.cleared(V.tensor_copy(junk[0:NE, :], psum[0:NE, p.ring.bank(m), :]), m)
                else:
                    V.tensor_tensor(out, psum[:, p.ring.bank(m), 0:NT * NE].rearrange("p (t e) -> p t e", e=NE),
                                    rb[:, :].unsqueeze(1).broadcast_to([P, NT, NE]), ALU.add).then_inc(p.lg_ok, 1)
                    dve.wait_ge(p.lg_ok, b + (2 if key[0] == "last_router" else 1))
                    dve.sem_inc(p.ring.free[m % 2], 1)

            def heads(p, b, link, causal, out):
                def maximum(h, t):
                    m = 4 * h + t
                    p.sq.wait_full(dve, b, m)
                    n = (t + 1) * P if causal else S
                    p.sq.cleared(V.tensor_reduce(nmax[:, h % 4, t:t + 1], psum[:, p.sq.bank(m), 0:n], AX.X,
                                                 ALU.max, negate=True), m)

                def output(h):
                    m = item(p, ("o", h))
                    p.ring.wait_full(dve, b, m)
                    o = psum[:, p.ring.bank(m), :].rearrange("p (t d) -> p t d", d=P)
                    r = rden[:, h % 2, :]
                    link(V.reciprocal(r, o[:, :, DH]))
                    p.ring.cleared(V.tensor_tensor(ot[:, :, h * DH:(h + 1) * DH], o[:, :, 0:DH],
                                                   r.unsqueeze(2).broadcast_to([P, NT, DH]), ALU.mult), m)

                def split_probs(m):
                    h, t = divmod(m, NT)
                    lo = t * P if causal else 0
                    p.sk.wait_read(dve, b, m)
                    V.tensor_copy(ph_[:, m % NP, lo:S], probs[:, m % NX, lo:S]).then_inc(p.p_hi, 1)
                    if t == NT - 1:
                        by_dve = X_BY_DVE[p.n]
                        dve.wait_ge(p.p_hi, b * len(by_dve) + (by_dve.index(m) + 1))
                        V.tensor_tensor(pl_[:, m % NP, lo:S], probs[:, m % NX, lo:S], ph_[:, m % NP, lo:S].bitcast(F32),
                                        ALU.subtract).then_inc(p.p_lo[t], 1)

                for key, *at in FIRST[p.n]:
                    if key == "turn":
                        turn_qk(p, b, *at)
                    elif key == "out":
                        out(*at)
                    else:
                        t, = at
                        m = item(p, ("v", t))
                        dve.wait_ge(p.hi, b * HI[p.n] + (hi_no[p.n][("v", t)] + 1))
                        p.ring.cleared(V.tensor_tensor(
                            v_part(t, DH + 1), psum[:, p.ring.bank(m), :].rearrange("p (h d) -> p h d", d=DH),
                            v_part(t, 0).bitcast(F32), ALU.subtract), m)
                for m in range(LEAD):
                    maximum(*divmod(m, NT))
                    if p.n == 2:
                        if m == 0:
                            dve.wait_ge(p.acc_ok, b * NT + NT)
                        normalize_part(p, b, link, m, EPS_FFN, ot, 1, 2 * NT)
                for m in range(LAST + 2):
                    if m + LEAD < STEPS_H:
                        maximum(*divmod(m + LEAD, NT))
                    if 0 < m <= STEPS_H and hi_by_dve(p.n, m - 1):
                        split_probs(m - 1)
                    if m and head_out(m - 1) is not None:
                        output(head_out(m - 1))
                    if group_turn(m):
                        for c in "kq":
                            turn_qk(p, b, group_turn(m), c)
                    if p.n == 1 and m == NORM_STEP:
                        link(V.tensor_copy(mod[:, :], modall[:, bass.ds(b + 1, 1), :].rearrange("p a m -> p (a m)")))
                    if NORM_STEP <= m < NORM_STEP + 8:
                        normalize_part(p, b, link, m - NORM_STEP, EPS[p.n], xt, p.n, PER[p.n])
                    if m in BESIDE[p.n]:
                        key, c = BESIDE[p.n][m]
                        if p.n == 1:
                            value(p, b, NC + NG + c, ("x", c), mod[:, c:c + 1], mod[:, NC + c:NC + c + 1])
                        elif key != "router":
                            lo_of(p, b, (key, c), xh[:, c, :], xl[:, c, :])
                        else:
                            route(p, b, (key, c), c, lg[:, :, :])
                for c in range(NC):
                    lo_of(p, b, ("turn_o", c), *o_t(c))

            def weights(n, pieces):
                p = ph[n]
                for i in pieces:
                    at, cols, _ = PIECES[n][i]
                    dve.wait_ge(p.w_hi, i + 1)
                    V.tensor_tensor(wl[:, at:at + cols], stage(n, i)[:, 0:cols], wh[:, at:at + cols].bitcast(F32),
                                    ALU.subtract).then_inc(p.w_lo, 1)

            p = ph[1]
            for n in range(2):
                dve.sem_inc(p.ring.free[n], 1)
            dve.sem_inc(p.head_ss, 2)
            link = Chain(prep)
            dve.wait_ge(vT, 1)
            link(V.tensor_copy(vcol[:, :], psum[:, 2, 0:38]))
            link(V.tensor_tensor(gqk[:, :], vcol[:, 36:37], vcol[:, 37:38], ALU.mult))
            link(V.memset(rwt[:, :, NR:NE], 0.0))
            link(V.memset(rb[:, NR:NE], 0.0))
            normalize(p, 0, link, EPS_COND, xt, 0, NT)
            weights(1, [0, 2])
            dve.wait_ge(mod_mm, 1)
            for m in range(2 * NC):
                link(V.tensor_scalar(modall[:, 0:B, m], psum[:, 3, m * B:(m + 1) * B], vcol[:, 16 + m:17 + m], None, ALU.add))
            for m in range(NC):
                link(V.tensor_scalar(modall[:, 0:B, m], modall[:, 0:B, m], 1.0, vcol[:, 24 + m:25 + m], ALU.add, ALU.mult))
            link(V.tensor_copy(modall[:, B, :], modall[:, 0, :]))
            for n in range(2):
                dve.sem_inc(p.sq.free[n], 1)
            dve.wait_ge(r_ok, 2)
            for c in range(NC):
                value(p, 0, c, ("x0", c), modall[:, 0, c:c + 1], modall[:, 0, NC + c:NC + c + 1])
            weights(1, [4])
            with dve.Fori(0, B) as b:
                link = Chain(p.step, b, STEPS[1])
                for n in range(2 * NT):
                    t, c = divmod(n, 2)
                    dve.wait_ge(p.head_sq, b * 2 * NT + (n + 1))
                    V.tensor_reduce(ssh[:, t, c * H:(c + 1) * H], probs[:, n % 2, :].rearrange("p (h d) -> p h d", d=DH),
                                    AX.X, ALU.add).then_inc(p.head_ss, 1)
                dve.wait_ge(p.head_ss, b * 2 * NT + (2 * NT + 2))
                rsqrt(link, ssh[:, :, :].rearrange("p t h -> p (t h)"), rsh[:, 0, :], rsh[:, 1, :], 1.0 / DH, EPS_COND)

                def y(t, i, key):
                    m = item(p, (key, t))
                    p.ring.wait_full(dve, i, m)
                    p.ring.cleared(V.tensor_tensor(yt[:, t, :], psum[:, p.ring.bank(m), :], ot[:, t, :], ALU.add), m)

                def normalize_heads(t, c):
                    x = qk[:, t, c * D:(c + 1) * D].rearrange("p (h d) -> p h d", d=DH)
                    r = rsh[:, 0, (2 * t + c) * H:(2 * t + c + 1) * H].unsqueeze(2).broadcast_to([P, H, DH])
                    V.tensor_tensor(x, x, r, ALU.mult).then_inc(p.qn, 1)

                def out(t):
                    y(t, b, "out")
                    for tc in {0: ((0, 0), (1, 0)), 1: ((2, 0), (3, 0), (3, 1))}.get(t, ()):
                        normalize_heads(*tc)

                dve.wait_ge(p.y_free, b + 1)
                heads(p, b, link, False, out)
                assert link.n == STEPS[1]
            once = Chain(prep2)
            dve.wait_ge(ph[2].w_ld[0], 16 * NLOAD[2][0])
            for c in range(NC):
                w = stage(2, 0)[:, c * 512:(c + 1) * 512]
                V.tensor_scalar(w, w, vcol[:, 28 + c:29 + c], None, ALU.mult).then_inc(ph[2].w_ln, 1)
            dve.wait_ge(p.y_free, B + 1)
            y(0, B - 1, "last")
            y(1, B - 1, "last")
            weights(2, [0])
            y(2, B - 1, "last")
            normalize(ph[2], 0, once, EPS_FFN, xt, 0, 2 * NT)
            y(3, B - 1, "last")
            weights(2, [1])
            p = ph[2]
            dve.wait_ge(v2_ld, 64)
            take_over(dve, ph[1].ring, p.ring)
            take_over(dve, ph[1].sq, p.sq)
            dve.sem_inc(p.ra, 2)
            for c in range(NC):
                lo_of(p, 0, ("x0", c), xh[:, c, :], xl[:, c, :])
            for c in range(NC):
                ins = V.tensor_scalar(rwt[:, c, :], rwt[:, c, :], vcol[:, 32 + c:33 + c], None, ALU.mult)
            ins.then_inc(rw_ok, 1)
            weights(2, [2])
            dve.wait_ge(p.w_hi, len(PIECES[2]) + 1)
            V.tensor_tensor(rwl[:, :, :], rwt[:, :, :], rwh[:, :, :].bitcast(F32), ALU.subtract).then_inc(p.w_lo, 1)

            def add_h(t, b, key):
                m = item(p, (key, t))
                p.ring.wait_full(dve, b, m)
                p.ring.cleared(V.tensor_tensor(ot[:, t, :], psum[:, p.ring.bank(m), :], resid(t), ALU.add), m)

            def scale_expert():
                for c in range(NC):
                    V.tensor_scalar(wstage[:, c, :], wstage[:, c, :], vcol[:, 32 + c:33 + c], None,
                                    ALU.mult).then_inc(ew_ln, 1)

            with dve.Fori(0, B) as b:
                link = Chain(p.step, b, STEPS[2])
                lo_of(p, b, "kv_d", wh[:, 6144:6656], wl[:, 6144:6656])
                lo_of(p, b, "q_d", wh[:, 6656:7168], wl[:, 6656:7168])
                for n in range(2 * NT):
                    t, c = divmod(n, 2)
                    m = item(p, ("qk", t, "qk"[c]))
                    p.ring.wait_read(dve, b, m)
                    dve.wait_ge(p.ra, b * 2 * NT + (n + 1))
                    x = ov[:, c, 0:H * RD].rearrange("p (h d) -> p h d", d=RD)
                    t1 = probs[:, n % 2, 0:256].rearrange("p (h d) -> p h d", d=RD)
                    t2 = probs[:, n % 2, 256:512].rearrange("p (h d) -> p h d", d=RD)
                    wide = lambda a, w: a.unsqueeze(1).broadcast_to([P, H, w])
                    V.tensor_tensor(t1, x, wide(rope[:, 0, t, :], RD), ALU.mult)
                    V.tensor_tensor(t2[:, :, 0:RD // 2], x[:, :, RD // 2:RD], wide(rope[:, 1, t, 0:RD // 2], RD // 2), ALU.mult)
                    V.tensor_tensor(t2[:, :, RD // 2:RD], x[:, :, 0:RD // 2], wide(rope[:, 1, t, RD // 2:RD], RD // 2),
                                    ALU.mult).then_inc(p.rt, 1)
                dve.wait_ge(p.r_ld, b * 48 + 1)
                heads(p, b, link, True, lambda t: add_h(t, b, "out"))
                assert link.n == STEPS[2]
            dve.wait_ge(p.r_ld, B * 48 + 1)
            add_h(0, B - 1, "last")
            add_h(1, B - 1, "last")
            dve.wait_ge(ew_ld, 48)
            scale_expert()
            add_h(2, B - 1, "last")
            add_h(3, B - 1, "last")
            dve.wait_ge(ew_hi, 1)
            V.tensor_tensor(ew[:, 0, 1, 0:2, :], wstage[:, 0:2, :], ew[:, 0, 0, 0:2, :].bitcast(F32),
                            ALU.subtract).then_inc(ew_lo, 1)
            dve.wait_ge(p.acc_ok, B * NT + NT)
            normalize(p, B - 1, once, EPS_FFN, ot, 3, 2 * NT)
            for c in range(NC):
                lo_of(p, B - 1, ("last_x2", c), xh[:, c, :], xl[:, c, :])
            for n in range(2):
                route(p, B - 1, ("last_router", n), n, logits[:, (B - 1) * NT:, :])

            dve.sem_inc(h_v, 2)
            for n in range(2):
                dve.sem_inc(guring.free[n], 1)
                dve.wait_ge(p.sq.free[n], B * p.sq.per + 1)
                dve.sem_inc(guring.free[2 + n], 1)
            link = Chain(g_step)
            prob, rank, cmp, gg = gtmp[:, 1], gtmp[:, 2], gtmp[:, 3], gtmp[:, 4]
            dve.wait_ge(g_exp, 1)
            link(V.tensor_scalar(gtmp[:, 0], gtmp[:, 0], 1.0, None, ALU.add))
            link(V.reciprocal(prob, gtmp[:, 0]))
            link(V.memset(rank, 0.0))
            for j in range(NR):
                for lo, hi, op in ((0, j, ALU.is_gt), (j + 1, NR, ALU.is_ge)):
                    if lo < hi:
                        pj = prob[:, :, j:j + 1].broadcast_to([P, B * NT, hi - lo])
                        link(V.tensor_tensor(cmp[:, :, lo:hi], pj, prob[:, :, lo:hi], op))
                        link(V.tensor_tensor(rank[:, :, lo:hi], rank[:, :, lo:hi], cmp[:, :, lo:hi], ALU.add))
            link(V.tensor_scalar(cmp[:, :, 0:NR], rank[:, :, 0:NR], 2.0, None, ALU.is_lt))
            link(V.tensor_tensor(gg[:, :, 0:NR], prob[:, :, 0:NR], cmp[:, :, 0:NR], ALU.mult))
            link(V.tensor_reduce(gden[:, 0, :], gg[:, :, 0:NR], AX.X, ALU.add))
            link(V.reciprocal(gden[:, 1, :], gden[:, 0, :]))
            link(V.memset(w8[:, 0, :], 1.0 / SCALING))
            for e in range(NR):
                link(V.scalar_tensor_tensor(out=w8[:, 1 + e, :], in0=gg[:, :, e], scalar=1.0 / SCALING,
                                            in1=gden[:, 1, :], op0=ALU.mult, op1=ALU.mult))
            with dve.Fori(0, NE // 2) as i:
                def combine(k):
                    j, blk = divmod(k, B)
                    if blk < B - 1 and j == 0:
                        dve.wait_ge(acc_ld[blk], 16)
                    for t in range(NT):
                        m = 4 * k + t
                        a = acc_of(blk)[:, t, :]
                        dring.wait_full(dve, i, m)
                        dring.cleared(V.scalar_tensor_tensor(out=a, in0=psum[:, dring.bank(m), :],
                                                             scalar=wcur[:, j, blk * NT + t:blk * NT + t + 1], in1=a,
                                                             op0=ALU.mult, op1=ALU.add), m)

                for k in range(2 * B):
                    j, blk = divmod(k, B)
                    if blk == 0:
                        V.tensor_copy(wcur[:, j, :], w8[:, bass.ds(i * 2 + j, 1), :].rearrange("p a t -> p (a t)"))\
                            .then_inc(w_cur, 1)
                        dve.wait_ge(w_cur, i * 2 + (j + 1))
                        dve.wait_ge(ew_ld, i * 96 + 48 * (j + 2))
                        scale_expert()
                    for n in range(NI):
                        m = 4 * k + 2 * n + 1
                        guring.wait_full(dve, i, m)
                        guring.wait_read(dve, i, m - 1)
                        dve.wait_ge(h_lo, i * 16 + (2 * k + n + 1))
                        V.tensor_tensor(hv[:, n, :], psum[:, guring.bank(m), :], sg[:, n, :], ALU.mult).then_inc(h_v, 1)
                        dve.wait_ge(h_v, i * 16 + (2 + 2 * k + n + 1))
                        dve.sem_inc(guring.free[m % 4], 1)
                    if k:
                        combine(k - 1)
                combine(2 * B - 1)


_INS = ['x', 'cond_2048', 'L0_cond_W_emb', 'L0_cond_b_emb', 'L0_cond_g_norm', 'L0_cond_W_qkv', 'L0_cond_g_q',
        'L0_cond_g_k', 'L0_cond_W_out', 'L0_ffn_ln1_w', 'L0_ffn_ln2_w', 'L0_ffn_kv_d_w', 'L0_ffn_q_d_w',
        'L0_ffn_k_u_w', 'L0_ffn_v_u_w', 'L0_ffn_q_u_w', 'L0_ffn_rope_k_w', 'L0_ffn_rope_q_w', 'L0_ffn_o_w',
        'gate', 'up', 'down', 'L0_ffn_router_w', 'L0_ffn_router_b', 'rope_cos', 'rope_sin']


def rope_tables():
    half = RD // 2
    freq = (1.0 / np.float32(10000.0) ** (np.arange(0, RD, 2, dtype=np.float32) / np.float32(RD))).astype(np.float32)
    ang = np.outer(np.arange(S, dtype=np.float32), freq).astype(np.float32)
    cos, sin = np.cos(ang), np.sin(ang)
    return (np.concatenate([cos, cos], 1).astype(np.float32), np.concatenate([-sin, sin], 1).astype(np.float32))


def kernel(**inputs):
    import concourse.bacc as bacc
    from concourse.bass_utils import run_bass_kernel_spmd as run

    data = dict(inputs)
    for name in ("gate", "up", "down"):
        shared = np.asarray(inputs[f"L0_ffn_sh_{name}"])[None]
        data[name] = np.concatenate([shared, np.asarray(inputs[f"L0_ffn_r_{name}"])], axis=0)
    data["rope_cos"], data["rope_sin"] = rope_tables()

    nc = bacc.Bacc("TRN2", target_bir_lowering=False, num_devices=1,
                   dynamic_dma_scratch_size=1024)
    arrays, args = {}, []
    for name in _INS:
        a = np.ascontiguousarray(data[name])
        arrays[f"in_{name}_dram"] = a
        args.append(nc.dram_tensor(f"in_{name}_dram", a.shape, mybir.dt.from_np(a.dtype), kind="ExternalInput").ap())
    args.append(nc.dram_tensor("out_dram", (B, S, D), F32, kind="ExternalOutput").ap())
    build(nc, *args)
    r = run(nc, [arrays], core_ids=[0])
    return r.results[0]["out_dram"]
```
